# Optimizing a Trainium2 kernel written in Bass

```python
import numpy as np
import jax
import jax.numpy as jnp

def _softmax(x, axis=-1):
    return jax.nn.softmax(x, axis=axis)

def _gelu(x):
    return jax.nn.gelu(x, approximate=True)

def _silu(x):
    return jax.nn.silu(x)

def _sigmoid(x):
    return jax.nn.sigmoid(x)

def _layernorm(x, axis=-1, eps=1e-05):
    m = jnp.mean(x, axis=axis, keepdims=True)
    v = jnp.var(x, axis=axis, keepdims=True)
    return (x - m) / jnp.sqrt(v + eps)

def _scatter_add(tgt, idx, src, axis=0):
    return tgt.at[idx].add(src)

def _segment_sum(src, seg, n):
    return jax.ops.segment_sum(src, seg, n)
kernel_name = 'mk_perceiver_d1_seqx_r4_de3200'

def setup_inputs(seed: int=0):
    np.random.seed(seed)
    _w = jnp.asarray

    def _rec_inputs():
        import jax
        import jax.numpy as jnp
        _rk = jax.random.key(seed)
        x = -0.0002928 + 1 * jax.random.normal(jax.random.fold_in(_rk, 1), (128, 32, 256), jnp.float32)
        _lenS = 32 - jax.random.randint(jax.random.fold_in(_rk, 7), (128,), 0, max(1, 32 // 4) + 1, jnp.int32)
        _lenS2 = 257 - jax.random.randint(jax.random.fold_in(_rk, 8), (128,), 0, max(1, 257 // 4) + 1, jnp.int32)
        _ctx_1024P = jax.random.normal(jax.random.fold_in(_rk, 11), (128, 16, 256), jnp.float32)
        _ctx_1024c = jax.random.dirichlet(jax.random.fold_in(_rk, 511), 0.3 * jnp.ones((16,), jnp.float32), (128, 257))
        _ctx_1024t = jnp.einsum('bsk,bkd->bsd', _ctx_1024c, _ctx_1024P)
        _ctx_1024t = _ctx_1024t * jax.lax.rsqrt(jnp.mean(jnp.square(_ctx_1024t)) + 1e-12) * 0.953939
        ctx_1024 = -1.39393e-06 + 0.999914 * (_ctx_1024t + 0.3 * jax.random.normal(jax.random.fold_in(_rk, 611), (128, 257, 256), jnp.float32))
        return (x, ctx_1024)
    x, ctx_1024 = _rec_inputs()

    def _L0_xattn_setup():
        import jax, jax.numpy as jnp
        import numpy as np
        D_MODEL = 256
        NUM_HEADS = 16
        HEAD_DIM = D_MODEL // NUM_HEADS

        def _split_heads(x):
            B, N, _ = x.shape
            return x.reshape(B, N, NUM_HEADS, HEAD_DIM).transpose(0, 2, 1, 3)
        key = jax.random.key(seed)
        ks = jax.random.split(key, 11)
        B, N = (2, 512)
        s = 1.0 / np.sqrt(D_MODEL)
        return {'query': jax.random.normal(ks[0], (B, N, D_MODEL), jnp.float32), 'key': jax.random.normal(ks[1], (B, N, D_MODEL), jnp.float32), 'value': jax.random.normal(ks[2], (B, N, D_MODEL), jnp.float32), 'Wq': jax.random.normal(ks[3], (D_MODEL, D_MODEL), jnp.float32) * s, 'bq': jax.random.normal(ks[4], (D_MODEL,), jnp.float32) * 0.01, 'Wk': jax.random.normal(ks[5], (D_MODEL, D_MODEL), jnp.float32) * s, 'bk': jax.random.normal(ks[6], (D_MODEL,), jnp.float32) * 0.01, 'Wv': jax.random.normal(ks[7], (D_MODEL, D_MODEL), jnp.float32) * s, 'bv': jax.random.normal(ks[8], (D_MODEL,), jnp.float32) * 0.01, 'Wo': jax.random.normal(ks[9], (D_MODEL, D_MODEL), jnp.float32) * s, 'bo': jax.random.normal(ks[10], (D_MODEL,), jnp.float32) * 0.01}
    _L0_xattn_all = _L0_xattn_setup()
    _L0_xattn_in = {k: v for k, v in _L0_xattn_all.items() if k in ('Wq', 'bq', 'Wk', 'bk', 'Wv', 'bv', 'Wo', 'bo')}
    del _L0_xattn_all

    def _L0_attn_setup():
        import jax, jax.numpy as jnp
        import numpy as np
        D = 256
        H = 16
        HD = D // H
        ROPE_BASE = 10000.0
        EPS_RMS = 1e-08
        EPS_RENORM = 1e-08

        def rms_norm(x, scale):
            norm = jnp.mean(x * x, axis=-1, keepdims=True)
            return scale * (x * jax.lax.rsqrt(norm + EPS_RMS))

        def rope_tables(seq_len):
            inv_freq = 1.0 / ROPE_BASE ** (jnp.arange(0, HD, 2, dtype=jnp.float32) / HD)
            t = jnp.arange(seq_len, dtype=jnp.float32)
            freqs = t[:, None] * inv_freq[None, :]
            emb = jnp.concatenate([freqs, freqs], axis=-1)
            return (jnp.cos(emb), jnp.sin(emb))

        def apply_rotary(x, cos, sin):
            x1 = x[..., ::2]
            x2 = x[..., 1::2]
            x_rot = jnp.stack([-x2, x1], axis=-1).reshape(x.shape)
            return x * cos + x_rot * sin
        key = jax.random.key(seed)
        ks = jax.random.split(key, 11)
        B, L = (2, 512)
        s = 1.0 / np.sqrt(D)
        inp = {'x': jax.random.normal(ks[0], (B, L, D), dtype=jnp.float32), 'q_w': jax.random.uniform(ks[1], (D, D), jnp.float32, -s, s), 'q_b': jax.random.uniform(ks[2], (D,), jnp.float32, -s, s), 'k_w': jax.random.uniform(ks[3], (D, D), jnp.float32, -s, s), 'k_b': jax.random.uniform(ks[4], (D,), jnp.float32, -s, s), 'v_w': jax.random.uniform(ks[5], (D, D), jnp.float32, -s, s), 'v_b': jax.random.uniform(ks[6], (D,), jnp.float32, -s, s), 'o_w': jax.random.uniform(ks[7], (D, D), jnp.float32, -s, s), 'o_b': jax.random.uniform(ks[8], (D,), jnp.float32, -s, s), 'qn_scale': jnp.ones((D,), dtype=jnp.float32), 'kn_scale': jnp.ones((D,), dtype=jnp.float32)}
        return inp
    _L0_attn_all = _L0_attn_setup()
    _L0_attn_in = {k: v for k, v in _L0_attn_all.items() if k in ('q_w', 'q_b', 'k_w', 'k_b', 'v_w', 'v_b', 'o_w', 'o_b', 'qn_scale', 'kn_scale')}
    del _L0_attn_all

    def _L0_ffn_setup():
        import jax, jax.numpy as jnp
        import numpy as np
        NUM_EXPERTS = 8
        CAPACITY = 160
        key = jax.random.key(seed)
        ks = jax.random.split(key, 5)
        D, E, F = (256, NUM_EXPERTS, 1024)
        inputs = jax.random.normal(ks[0], (2, 512, D), dtype=jnp.float32)
        gate_w = jax.random.normal(ks[1], (D, E), dtype=jnp.float32) * 0.02
        gate_b = jnp.zeros((E,), dtype=jnp.float32)
        w1 = jax.random.normal(ks[2], (E, D, F), dtype=jnp.float32) * 0.02
        b1 = jnp.zeros((E, F), dtype=jnp.float32)
        w2 = jax.random.normal(ks[3], (E, F, D), dtype=jnp.float32) * 0.02
        b2 = jnp.zeros((E, D), dtype=jnp.float32)
        return {'inputs': inputs, 'gate_w': gate_w, 'gate_b': gate_b, 'w1': w1, 'b1': b1, 'w2': w2, 'b2': b2}
    _L0_ffn_all = _L0_ffn_setup()
    _L0_ffn_in = {k: v for k, v in _L0_ffn_all.items() if k in ('gate_w', 'gate_b', 'w1', 'b1', 'w2', 'b2')}
    del _L0_ffn_all
    return {'x': x, 'ctx_1024': ctx_1024, 'L0_xattn_Wq': _L0_xattn_in['Wq'], 'L0_xattn_bq': _L0_xattn_in['bq'], 'L0_xattn_Wk': _L0_xattn_in['Wk'], 'L0_xattn_bk': _L0_xattn_in['bk'], 'L0_xattn_Wv': _L0_xattn_in['Wv'], 'L0_xattn_bv': _L0_xattn_in['bv'], 'L0_xattn_Wo': _L0_xattn_in['Wo'], 'L0_xattn_bo': _L0_xattn_in['bo'], 'L0_attn_q_w': _L0_attn_in['q_w'], 'L0_attn_q_b': _L0_attn_in['q_b'], 'L0_attn_k_w': _L0_attn_in['k_w'], 'L0_attn_k_b': _L0_attn_in['k_b'], 'L0_attn_v_w': _L0_attn_in['v_w'], 'L0_attn_v_b': _L0_attn_in['v_b'], 'L0_attn_o_w': _L0_attn_in['o_w'], 'L0_attn_o_b': _L0_attn_in['o_b'], 'L0_attn_qn_scale': _L0_attn_in['qn_scale'], 'L0_attn_kn_scale': _L0_attn_in['kn_scale'], 'L0_ffn_gate_w': _L0_ffn_in['gate_w'], 'L0_ffn_gate_b': _L0_ffn_in['gate_b'], 'L0_ffn_w1': _L0_ffn_in['w1'], 'L0_ffn_b1': _L0_ffn_in['b1'], 'L0_ffn_w2': _L0_ffn_in['w2'], 'L0_ffn_b2': _L0_ffn_in['b2']}

def reference(x, ctx_1024, L0_xattn_Wq, L0_xattn_bq, L0_xattn_Wk, L0_xattn_bk, L0_xattn_Wv, L0_xattn_bv, L0_xattn_Wo, L0_xattn_bo, L0_attn_q_w, L0_attn_q_b, L0_attn_k_w, L0_attn_k_b, L0_attn_v_w, L0_attn_v_b, L0_attn_o_w, L0_attn_o_b, L0_attn_qn_scale, L0_attn_kn_scale, L0_ffn_gate_w, L0_ffn_gate_b, L0_ffn_w1, L0_ffn_b1, L0_ffn_w2, L0_ffn_b2):
    import jax
    import jax.numpy as jnp

    def _L0_xattn_ref(query, key, value, Wq, bq, Wk, bk, Wv, bv, Wo, bo):
        import jax, jax.numpy as jnp
        import numpy as np
        D_MODEL = 256
        NUM_HEADS = 16
        HEAD_DIM = D_MODEL // NUM_HEADS

        def _split_heads(x):
            B, N, _ = x.shape
            return x.reshape(B, N, NUM_HEADS, HEAD_DIM).transpose(0, 2, 1, 3)
        B, N, _ = query.shape
        q = _split_heads(query @ Wq.T + bq)
        k = _split_heads(key @ Wk.T + bk)
        v = _split_heads(value @ Wv.T + bv)
        scores = jnp.einsum('bhnd,bhmd->bhnm', q, k)
        attn = jax.nn.softmax(scores, axis=-1)
        out = jnp.einsum('bhnm,bhmd->bhnd', attn, v)
        out = out.transpose(0, 2, 1, 3).reshape(B, N, D_MODEL)
        return out @ Wo.T + bo

    def _L0_attn_ref(x, q_w, q_b, k_w, k_b, v_w, v_b, o_w, o_b, qn_scale, kn_scale):
        import jax, jax.numpy as jnp
        import numpy as np
        D = 256
        H = 16
        HD = D // H
        ROPE_BASE = 10000.0
        EPS_RMS = 1e-08
        EPS_RENORM = 1e-08

        def rms_norm(x, scale):
            norm = jnp.mean(x * x, axis=-1, keepdims=True)
            return scale * (x * jax.lax.rsqrt(norm + EPS_RMS))

        def rope_tables(seq_len):
            inv_freq = 1.0 / ROPE_BASE ** (jnp.arange(0, HD, 2, dtype=jnp.float32) / HD)
            t = jnp.arange(seq_len, dtype=jnp.float32)
            freqs = t[:, None] * inv_freq[None, :]
            emb = jnp.concatenate([freqs, freqs], axis=-1)
            return (jnp.cos(emb), jnp.sin(emb))

        def apply_rotary(x, cos, sin):
            x1 = x[..., ::2]
            x2 = x[..., 1::2]
            x_rot = jnp.stack([-x2, x1], axis=-1).reshape(x.shape)
            return x * cos + x_rot * sin
        B, L, _ = x.shape
        q = rms_norm(x, qn_scale) @ q_w.T + q_b
        k = rms_norm(x, kn_scale) @ k_w.T + k_b
        v = x @ v_w.T + v_b
        q = q.reshape(B, L, H, HD).transpose(0, 2, 1, 3)
        k = k.reshape(B, L, H, HD).transpose(0, 2, 1, 3)
        v = v.reshape(B, L, H, HD).transpose(0, 2, 1, 3)
        cos, sin = rope_tables(L)
        q = apply_rotary(q, cos, sin)
        k = apply_rotary(k, cos, sin)
        scale = 1.0 / np.sqrt(HD)
        scores = jnp.einsum('bhqd,bhkd->bhqk', q, k) * scale
        weights = jax.nn.sigmoid(scores)
        weights = weights / (jnp.sum(weights, axis=-1, keepdims=True) + EPS_RENORM)
        attn = jnp.einsum('bhqk,bhkd->bhqd', weights, v)
        attn = attn.transpose(0, 2, 1, 3).reshape(B, L, D)
        return attn @ o_w.T + o_b

    def _L0_ffn_ref(inputs, gate_w, gate_b, w1, b1, w2, b2):
        import jax, jax.numpy as jnp
        import numpy as np
        NUM_EXPERTS = 8
        CAPACITY = 160
        D = inputs.shape[-1]
        tokens = inputs.reshape(-1, D)
        logits = tokens @ gate_w + gate_b
        probs = jax.nn.softmax(logits, axis=-1)
        expert_idx = jnp.argmax(probs, axis=-1)
        mask1 = jax.nn.one_hot(expert_idx, NUM_EXPERTS, dtype=jnp.float32)
        pos = jnp.sum(jnp.cumsum(mask1, axis=0) * mask1, axis=-1) - 1.0
        pos = pos.astype(jnp.int32)
        keep = (pos < CAPACITY).astype(jnp.float32)
        gate_prob = jnp.sum(probs * mask1, axis=-1)
        pos_oh = jax.nn.one_hot(pos, CAPACITY, dtype=jnp.float32)
        sec_mask = mask1[:, :, None] * pos_oh[:, None, :] * keep[:, None, None]
        combine_weights = sec_mask * gate_prob[:, None, None]
        dispatch = jnp.einsum('nec,nd->ecd', sec_mask, tokens)
        h = jax.nn.gelu(jnp.einsum('ecd,edf->ecf', dispatch, w1) + b1[:, None, :])
        expert_out = jnp.einsum('ecf,efd->ecd', h, w2) + b2[:, None, :]
        out = jnp.einsum('nec,ecd->nd', combine_weights, expert_out)
        return out.reshape(inputs.shape)
    x = x + _L0_xattn_ref(_layernorm(x, axis=-1), ctx_1024, ctx_1024, L0_xattn_Wq, L0_xattn_bq, L0_xattn_Wk, L0_xattn_bk, L0_xattn_Wv, L0_xattn_bv, L0_xattn_Wo, L0_xattn_bo)
    x = x + _L0_attn_ref(_layernorm(x, axis=-1), L0_attn_q_w, L0_attn_q_b, L0_attn_k_w, L0_attn_k_b, L0_attn_v_w, L0_attn_v_b, L0_attn_o_w, L0_attn_o_b, L0_attn_qn_scale, L0_attn_kn_scale)
    x = x + _L0_ffn_ref(_layernorm(x, axis=-1), L0_ffn_gate_w, L0_ffn_gate_b, L0_ffn_w1, L0_ffn_b1, L0_ffn_w2, L0_ffn_b2)
    return x

_drawn_inputs = setup_inputs


def setup_inputs(seed=0):
    import zlib

    import numpy as np

    out = dict(_drawn_inputs(seed))
    spreads = {'L0_attn_qn_scale': (1.0, 0.6),
     'L0_attn_kn_scale': (1.0, 0.6),
     'L0_ffn_gate_b': (0.0, 0.782),
     'L0_ffn_b1': (0.0, 0.8),
     'L0_ffn_b2': (0.0, 0.8)}
    factors = {'L0_xattn_bq': 6.244,
     'L0_xattn_bk': 8.0,
     'L0_xattn_bv': 7.873,
     'L0_xattn_bo': 7.455,
     'L0_attn_q_w': 7.587,
     'L0_attn_q_b': 8.0,
     'L0_attn_k_w': 7.55,
     'L0_attn_k_b': 8.0,
     'L0_attn_v_b': 3.85,
     'L0_ffn_gate_w': 4.815,
     'L0_ffn_w1': 6.536,
     'L0_ffn_w2': 6.101}
    for name, (base, spread) in spreads.items():
        noise = np.random.default_rng([zlib.crc32(name.encode()), seed]).standard_normal(out[name].shape)
        drawn = base * np.exp(spread * noise) if base else spread * noise
        out[name] = jnp.asarray(drawn.astype(out[name].dtype))
    for name, factor in factors.items():
        out[name] = (out[name] * factor).astype(out[name].dtype)
    return out
```

```python
from contextlib import ExitStack

import numpy as np
import concourse.bass as bass
from concourse import mybir

F32 = mybir.dt.float32
BF16 = mybir.dt.bfloat16
I32 = mybir.dt.int32
ALU = mybir.AluOpType
ACT = mybir.ActivationFunctionType
AX = mybir.AxisListType

P = 128
B, L, D = 128, 32, 256
S = 257
SM = 256
H, HD = 16, 16
C = D // P
TB = P // L
T = B * L // P
HH = H // C
MT = H * L // P
E, CAP, F = 8, 160, 1024
FT = F // P
CR = CAP - P
ROW = 2 * D + 2
SCALE = 1.0 / np.sqrt(HD)

CONST = {}
_at = 0
for _name, _n in (("ident", P), ("tri", P), ("ones", P), ("spread", 2 * P), ("diag", L), ("cos", HD), ("sin", HD),
                  ("even", 1), ("odd", 1), ("rank", E), ("token", 1), ("mhalf", 1), ("sentinel", 1)):
    CONST[_name] = (_at, _at + _n)
    _at += _n
NCONST = _at


def constants():
    t = np.zeros((P, NCONST), np.float32)
    p = np.arange(P)

    def put(name, v):
        t[:, CONST[name][0]:CONST[name][1]] = v

    put("ident", np.eye(P))
    put("tri", p[:, None] <= p[None, :])
    put("ones", 1.0)
    put("spread", np.concatenate([(4 * m + p[:, None] // L) == p[None, :] // HD for m in range(2)], 1))
    put("diag", p[:, None] % L == np.arange(L)[None, :])
    inv_freq = 1.0 / np.float32(10000.0) ** (np.arange(0, HD, 2, dtype=np.float32) / HD)
    angle = (p % L).astype(np.float32)[:, None] * inv_freq[None, :].astype(np.float32)
    angle = np.concatenate([angle, angle], 1)
    put("cos", np.cos(angle))
    put("sin", np.sin(angle) * np.where(np.arange(HD) % 2, 1.0, -1.0))
    put("even", ((p // HD) % 2 == 0)[:, None])
    put("odd", ((p // HD) % 2 == 1)[:, None])
    put("rank", E - np.arange(E)[None, :])
    put("token", (E * CAP + p)[:, None])
    put("mhalf", -0.5)
    put("sentinel", 0.0)
    t[:, CONST["sentinel"][0]] = np.full(P, 1 << 20, np.int32).view(np.float32)
    return t


def floor0(count):
    return max(count, 0) if isinstance(count, int) else count


def build(nc, a, out):
    ctx = ExitStack()
    with ctx:
        def sb(name, shape, dt=F32):
            return ctx.enter_context(nc.sbuf_tensor(name, shape, dt))

        def ps(name, shape, dt=F32):
            return ctx.enter_context(nc.psum_tensor(name, shape, dt))

        def sem(name):
            return ctx.enter_context(nc.semaphore(name))

        slots = nc.dram_tensor("slots", (E * CAP, ROW), F32, kind="Internal").ap()

        wq, wk, wv, wo, av, ao = (sb(n, [P, C, D]) for n in ("wq", "wk", "wv", "wo", "av", "ao"))
        aqk = sb("aqk", [P, C, 2 * D])
        gw = sb("gw", [P, C, E])
        const = sb("const", [P, NCONST])
        k = {n: const[:, lo:hi] for n, (lo, hi) in CONST.items()}
        tri_bf, ones_bf = sb("tri_bf", [P, P], BF16), sb("ones_bf", [P, P], BF16)
        b_q, b_k, b_v = (sb(n, [P, C]) for n in ("b_q", "b_k", "b_v"))
        qn, kn = sb("qn", [P, C]), sb("kn", [P, C])
        r_o, r_v2, r_o2 = (sb(n, [P, D]) for n in ("r_o", "r_v2", "r_o2"))
        r_qk = sb("r_qk", [P, 2 * D])
        r_g = sb("r_g", [P, E])
        ctxT = sb("ctxT", [P, 2, C, 2, S])
        lastT = sb("lastT", [P, C, B])
        klast = sb("klast", [P, C, B])
        vlast = sb("vlast", [P, T, C, TB])
        kT = sb("kT", [P, 2, C, S])
        vv = sb("vv", [P, 2, C, D])
        xq, xn, xnT, qT = sb("xq", [P, D]), sb("xn", [P, D]), sb("xnT", [P, C, P]), sb("qT", [P, C, P])
        qbd = sb("qbd", [P, C, TB, HH, L])
        nmx, esum, rsum = sb("nmx", [P, MT]), sb("esum", [P, MT]), sb("rsum", [P, MT])
        prob = sb("prob", [P, MT, S])
        probT = sb("probT", [P, C, 2, HH * L])
        plast = sb("plast", [P, MT, TB, L])
        att, alast = sb("att", [P, C, P]), sb("alast", [P, C, P])
        xr, x1, x1b, y1, sq = (sb(n, [P, D]) for n in ("xr", "x1", "x1b", "y1", "sq"))
        y1T = sb("y1T", [P, C, P])
        qk, qkc, qks = sb("qk", [P, 2 * D]), sb("qkc", [P, 2 * D]), sb("qks", [P, 2 * D])
        qkT = sb("qkT", [P, 2 * C, P])
        qbd2 = sb("qbd2", [P, C, HH, P])
        v2 = sb("v2", [P, D])
        th, tabs, sneg = (sb(n, [P, 2 * D]) for n in ("th", "tabs", "sneg"))
        wbd = sb("wbd", [P, H, P])
        ssum, att2 = sb("ssum", [P, C, P]), sb("att2", [P, C, P])
        row = sb("row", [P, ROW])
        y2T = sb("y2T", [P, C, P])
        stat = {n: sb("stat_" + n, [P, 6]) for n in "q12"}
        mv = {n: sb("mv_" + n, [P, 2]) for n in "q12"}
        ve = {n: sb("ve_" + n, [P, 1]) for n in "q12"}
        rstd = {n: sb("rstd_" + n, [P, 1]) for n in "q12"}
        msq, mse, rrms = sb("msq", [P, 1]), sb("mse", [P, 1]), sb("rrms", [P, 1])
        logit, nlm, ex, se, rse, pr = (sb(n, [P, w]) for n, w in (("logit", E), ("nlm", 1), ("ex", E), ("se", 1), ("rse", 1), ("pr", E)))
        eqr, top, oh = sb("eqr", [P, E]), sb("top", [P, 1]), sb("oh", [P, E], BF16)
        seen = sb("seen", [P, E], BF16)
        cumoh, pos = sb("cumoh", [P, E]), sb("pos", [P, 1])
        first, slot, off, kept, slotf = (sb(n, [P, 1]) for n in ("first", "slot", "off", "kept", "slotf"))
        away, token = sb("away", [P, 1]), sb("token", [P, 1])
        sloti = sb("sloti", [P, 1], I32)
        w1 = sb("w1", [P, 2, C, F])
        w2 = sb("w2", [P, 2, FT, D])
        b1, b2 = sb("b1", [P, E, FT]), sb("b2", [P, E, C])
        ra, rb = sb("ra", [P, 2, ROW]), sb("rb", [CR, 2, ROW])
        disp = sb("disp", [P, C, CAP])
        hid = sb("hid", [P, FT, CAP])
        eo = sb("eo", [P, C, CAP])
        fa, fb = sb("fa", [P, 2, D]), sb("fb", [CR, 2, D])

        score = ps("score", [P, MT, 512])
        kps, vps = ps("kps", [P, C, SM]), ps("vps", [P, C, D])
        shared = ps("shared", [P, 512])
        gather = ps("gather", [P, C, 2, P])
        sh_c = shared[:, 0:C * P].rearrange("p (c n) -> p c n", c=C)
        sh_pair = shared[:, :].rearrange("p (c g n) -> p c g n", c=C, g=2)

        names = """const_in weights_in w_done bf_consts scaled zeroed klast_done vlast_done last_ps_free last_ps
            xq_in xr_in xn_stat xn_pow xn_done qt_ps xnT_done q_ps qT_done qbd_in
            k_done k_evac klast_cp v_done v_evac s_done max_done exp_done rsum_done norm_done plast_done
            pt_done pta_evac ptb_evac pv_done ll_ps ext_step att_done
            xrb_done o1_ps x1_step x1_done x1_pow y1_done sq_done rms_step rrms_done x1b_done y1t_ps y1T_done
            qk_ps qk_done qkc_done qks_done rope_done v2_ps v2_done qkt_ps qkT_done qbd2_in s2_ps sig_done
            sm_ps sm_step ssum_done pv2_ps ext2_step att2_done o2_ps x2_step x2_done x2_pow y2_done x2_out
            y2t_ps y2T_done g_ps route_step logit_done ex_done oh_done cum_ps pos_step cum_read seen_done pos_done
            slot_step slot_done sent slots_init slots_zero away_done top_done att_tmp
            th_done smin_done tabs_done sneg_exp
            ra_in0 ra_in1 w1_in0 w1_in1 ffb_in dt_ps dt_evac h_ps hid_done eo_ps eo_done et_ps fin_done fin_out0 fin_out1
            settled""".split()
        s = {n: sem(n) for n in names}
        ctx_in = [sem("ctx_in0"), sem("ctx_in1")]
        block = ctx.enter_context(nc.Block())

        def settle(eng):
            eng.sem_inc(s["settled"], 1)

        def tiles(*, loop, body):
            for i in range(3):
                body(i)
            with loop(3, T - 1) as i:
                body(i)
            body(T - 1)
            body(T)
            body(T + 1)

        def stages(i):
            if not isinstance(i, int):
                return True, True, True, True
            return i <= T - 2, i <= T - 1, 1 <= i <= T, 2 <= i

        @block.sync
        def _(sp):
            sp.dma_start(const[:, :], a["const"]).then_inc(s["const_in"], 16)
            for dst, src in ((wk, "Wk"), (wq, "Wq"), (wv, "Wv"), (wo, "Wo"), (av, "v_w"), (ao, "o_w")):
                sp.dma_start(dst[:], a[src].rearrange("(c p) n -> p c n", c=C)).then_inc(s["weights_in"], 16)
            sp.dma_start(aqk[:, :, 0:D], a["q_w"].rearrange("(c p) n -> p c n", c=C)).then_inc(s["weights_in"], 16)
            sp.dma_start(aqk[:, :, D:2 * D], a["k_w"].rearrange("(c p) n -> p c n", c=C)).then_inc(s["weights_in"], 16)
            sp.dma_start(gw[:], a["gate_w"].rearrange("(c p) n -> p c n", c=C)).then_inc(s["weights_in"], 16)
            for dst, src in ((b_q, "bq"), (b_k, "bk"), (b_v, "bv"), (qn, "qn"), (kn, "kn")):
                sp.dma_start(dst[:, :], a[src].rearrange("(c p) -> p c", c=C),
                             allow_slow_non_contiguous=True).then_inc(s["weights_in"], 16)
            for dst, src in ((r_o[:, :], "bo"), (r_v2[:, :], "v_b"), (r_o2[:, :], "o_b"),
                             (r_qk[:, 0:D], "q_b"), (r_qk[:, D:2 * D], "k_b"), (r_g[:, :], "gate_b")):
                sp.dma_start(dst, a[src].partition_broadcast(P)).then_inc(s["weights_in"], 16)
            sp.dma_start(lastT[:], a["lastT"].rearrange("(c p) b -> p c b", c=C)).then_inc(s["weights_in"], 16)

            def load_ctx(t, r):
                sp.wait_ge(s["v_done"], floor0(TB * t + 2 * r - 2))
                b = TB * t + 2 * r
                for c in range(C):
                    sp.dma_start(ctxT[:, r, c], a["ctxT"][c * P:(c + 1) * P, bass.ds(b, 2), :]).then_inc(ctx_in[r], 16)

            def load_x(dst, t, done):
                sp.dma_start(dst[:, :], a["x"][bass.ds(P * t, P), :]).then_inc(s[done], 16)

            def send_diag(src, dst, done):
                for h in range(HH):
                    sp.dma_start(dst(h), src(h)).then_inc(s[done], 16)

            def send_queries(t):
                sp.wait_ge(s["qT_done"], t + 1)
                settle(sp)
                sp.wait_ge(s["s_done"], floor0(2 * TB * t))
                settle(sp)
                send_diag(lambda h: qT[HD * h:HD * (h + 1), :, :].rearrange("p c (j q) -> p c j q", j=TB),
                          lambda h: qbd[HD * h:HD * (h + 1), :, :, h, :], "qbd_in")

            load_x(xq, 0, "xq_in")
            load_ctx(0, 0)
            load_ctx(0, 1)
            load_x(xr, 0, "xr_in")
            sp.wait_ge(s["zeroed"], 3)
            send_queries(0)

            def body(i):
                q, xa, s1, s2 = stages(i)
                if q:
                    sp.wait_ge(s["xn_done"], i + 1)
                    load_x(xq, i + 1, "xq_in")
                if s2:
                    sp.wait_ge(s["qkT_done"], i - 1)
                    send_diag(lambda h: qkT[HD * h:HD * (h + 1), 0:C, :],
                              lambda h: qbd2[HD * h:HD * (h + 1), :, h, :], "qbd2_in")
                if q:
                    load_ctx(i + 1, 0)
                if s1 and xa:
                    sp.wait_ge(s["x1_done"], i)
                    load_x(xr, i, "xr_in")
                if q:
                    load_ctx(i + 1, 1)
                if s2:
                    sp.wait_ge(s["x2_done"], i - 1)
                    sp.dma_start(out[bass.ds(P * (i - 2), P), :], row[:, D:2 * D]).then_inc(s["x2_out"], 16)
                if q:
                    send_queries(i + 1)

            tiles(loop=sp.Fori, body=body)

            sp.wait_ge(s["sent"], 16 * T)

            def load_rows(e, r):
                sp.dma_start(ra[:, r, :], slots[bass.ds(CAP * e, P), :]).then_inc(s[f"ra_in{r}"], 16)
                sp.dma_start(rb[:, r, :], slots[bass.ds(CAP * e + P, CR), :]).then_inc(s[f"ra_in{r}"], 16)

            def load_expert(e, r):
                sp.dma_start(w1[:, r], a["w1"][bass.ds(e, 1), :, :].rearrange("a (c p) f -> p (a c) f", c=C)
                             ).then_inc(s[f"w1_in{r}"], 16)
                sp.dma_start(w2[:, r], a["w2"][bass.ds(e, 1), :, :].rearrange("a (t p) d -> p (a t) d", t=FT)
                             ).then_inc(s[f"w1_in{r}"], 16)

            for r in range(2):
                load_rows(r, r)
            with sp.Fori(0, E // 2 - 1) as i:
                for r in range(2):
                    sp.wait_ge(s["et_ps"], 2 * i + r + 1)
                    settle(sp)
                    load_expert(2 * i + r + 2, r)
                    sp.wait_ge(s[f"fin_out{r}"], 32 * i + 32)
                    load_rows(2 * i + r + 2, r)
            for r in range(2):
                sp.wait_ge(s[f"fin_out{r}"], 32 * (E // 2))
            sp.wait_ge(s["x2_out"], 16 * T)

        @block.tensor
        def _(pe):
            mm = nc.tensor.matmul
            pe.wait_ge(s["weights_in"], 16 * 21)
            pe.wait_ge(s["const_in"], 16)
            for w, o in ((wk, 0), (wv, C * P)):
                for c in range(C):
                    for n in range(C):
                        last = mm(shared[:, o + c * P:o + (c + 1) * P], w[:, n, c * P:(c + 1) * P], lastT[:, n, :],
                                  start=n == 0, stop=n == C - 1)
            last.then_inc(s["last_ps"], 1)

            def transpose_queries(t):
                pe.wait_ge(s["xn_done"], t + 1)
                for c in range(C):
                    last = nc.tensor.transpose(sh_c[:, c], xn[:, c * P:(c + 1) * P], k["ident"])
                last.then_inc(s["qt_ps"], 1)

            def project_queries(t):
                pe.wait_ge(s["xnT_done"], t + 1)
                for c in range(C):
                    for n in range(C):
                        last = mm(sh_c[:, c], wq[:, n, c * P:(c + 1) * P], xnT[:, n, :], start=n == 0, stop=n == C - 1)
                last.then_inc(s["q_ps"], 1)

            def keys(t, j):
                b, r, g = TB * t + j, j // 2, j % 2
                pe.wait_ge(ctx_in[r], 16 * C * (t + 1))
                pe.wait_ge(s["k_evac"], b)
                for c in range(C):
                    for n in range(C):
                        last = mm(kps[:, c, :], wk[:, n, c * P:(c + 1) * P], ctxT[:, r, n, g, 0:SM],
                                  start=n == 0, stop=n == C - 1)
                last.then_inc(s["k_done"], 1)

            def values(t, j):
                b, r, g = TB * t + j, j // 2, j % 2
                pe.wait_ge(s["v_evac"], b)
                for c in range(C):
                    for n in range(C):
                        last = mm(vps[:, c, :], ctxT[:, r, n, g, c * P:(c + 1) * P], wv[:, n, :],
                                  start=n == 0, stop=n == C - 1)
                last.then_inc(s["v_done"], 1)

            def scores(t, j):
                b = TB * t + j
                pe.wait_ge(s["k_evac"], b + 1)
                pe.wait_ge(s["klast_cp"], b + 1)
                if j == 0:
                    pe.wait_ge(s["qbd_in"], 16 * HH * (t + 1))
                for m in range(MT):
                    c, g = m // 2, m % 2
                    last = mm(score[:, m, 0:S], qbd[:, c, j, 4 * g:4 * g + 4, :].rearrange("p h q -> p (h q)"),
                              kT[:, b_slot(j), c, :], start=True, stop=True)
                    if g:
                        last.then_inc(s["s_done"], 1)

            def b_slot(j):
                return j % 2

            def transpose_probs(t, j):
                b = TB * t + j
                for c in range(C):
                    pe.wait_ge(s["norm_done"], 2 * b + c + 1)
                    for g in range(2):
                        for n in range(2):
                            at = n * HH * L + g * P
                            last = nc.tensor.transpose(score[:, 2 * c, at:at + P], prob[:, 2 * c + g, n * P:(n + 1) * P],
                                                       k["ident"])
                    last.then_inc(s["pt_done"], 1)

            def weighted_values(t, j):
                b = TB * t + j
                pe.wait_ge(s["v_evac"], b + 1)
                if j == 0:
                    pe.wait_ge(s["ext_step"], floor0(2 * t))
                for c in range(C):
                    pe.wait_ge(s["ptb_evac" if c else "pta_evac"], b + 1)
                    for g in range(4):
                        for n in range(2):
                            last = mm(gather[32 * g:32 * g + 32, c, :, j * L:(j + 1) * L],
                                      vv[:, b_slot(j), n, c * P + 32 * g:c * P + 32 * g + 32],
                                      probT[:, c, n, 2 * L * g:2 * L * (g + 1)].rearrange("p (h q) -> p h q", h=2),
                                      start=n == 0, stop=n == 1)
                last.then_inc(s["pv_done"], 1)

            def last_probs(t):
                pe.wait_ge(s["plast_done"], TB * (t + 1))
                for c in range(C):
                    for g in range(2):
                        last = mm(sh_c[:, c], k["spread"][:, g * P:(g + 1) * P],
                                  plast[:, 2 * c + g, :, :].rearrange("p j q -> p (j q)"), start=g == 0, stop=g == 1)
                last.then_inc(s["ll_ps"], 1)

            def project_out(x, w, ready, t, done):
                pe.wait_ge(s[ready], t + 1)
                for c in range(C):
                    last = mm(shared[:, 0:D], x[:, c, :], w[:, c, :], start=c == 0, stop=c == C - 1)
                last.then_inc(s[done], 1)

            def transpose_rows(x, ready, t, done):
                pe.wait_ge(s[ready], t + 1)
                for c in range(C):
                    last = nc.tensor.transpose(sh_c[:, c], x[:, c * P:(c + 1) * P], k["ident"])
                last.then_inc(s[done], 1)

            def project_qk(t):
                pe.wait_ge(s["y1T_done"], t + 1)
                pe.wait_ge(s["scaled"], 2 * C)
                for c in range(C):
                    last = mm(shared[:, :], y1T[:, c, :], aqk[:, c, :], start=c == 0, stop=c == C - 1)
                last.then_inc(s["qk_ps"], 1)

            def transpose_qk(t):
                pe.wait_ge(s["rope_done"], t + 1)
                for c in range(2 * C):
                    last = nc.tensor.transpose(shared[:, c * P:(c + 1) * P], qk[:, c * P:(c + 1) * P], k["ident"])
                last.then_inc(s["qkt_ps"], 1)

            def scores2(t):
                pe.wait_ge(s["qbd2_in"], 16 * HH * (t + 1))
                for c in range(C):
                    for j in range(TB):
                        last = mm(shared[32 * j:32 * j + 32, c * D:(c + 1) * D], qkT[:, C + c, 32 * j:32 * j + 32],
                                  qbd2[:, c, :, 32 * j:32 * j + 32], start=True, stop=True)
                last.then_inc(s["s2_ps"], 1)

            def weight_sums(t):
                pe.wait_ge(s["sig_done"], TB * (t + 1))
                for c in range(C):
                    for g in range(4):
                        last = mm(shared[32 * g:32 * g + 32, c * D:(c + 1) * D], k["ones"][:, 0:32],
                                  wbd[:, 8 * c + 2 * g:8 * c + 2 * g + 2, :].rearrange("p h n -> p (h n)"),
                                  start=True, stop=True)
                last.then_inc(s["sm_ps"], 1)

            def weighted_values2(t):
                pe.wait_ge(s["v2_done"], t + 1)
                for c in range(C):
                    for g in range(4):
                        last = mm(shared[32 * g:32 * g + 32, c * D:(c + 1) * D], v2[:, c * P + 32 * g:c * P + 32 * g + 32],
                                  wbd[:, 8 * c + 2 * g:8 * c + 2 * g + 2, :].rearrange("p h n -> p (h n)"),
                                  start=True, stop=True)
                last.then_inc(s["pv2_ps"], 1)

            def gate(t):
                pe.wait_ge(s["y2T_done"], t + 1)
                for c in range(C):
                    last = mm(shared[:, 0:E], y2T[:, c, :], gw[:, c, :], start=c == 0, stop=c == C - 1)
                last.then_inc(s["g_ps"], 1)

            def positions(t):
                pe.wait_ge(s["oh_done"], t + 1)
                pe.wait_ge(s["seen_done"], t + 1)
                pe.wait_ge(s["bf_consts"], 2)
                mm(shared[:, 0:E], tri_bf[:, :], oh[:, :], start=True, stop=False)
                mm(shared[:, 0:E], ones_bf[:, :], seen[:, :], start=False, stop=True).then_inc(s["cum_ps"], 1)

            reader = ["vlast_done", 1]

            def turn(sem_name, count):
                pe.wait_ge(s[reader[0]], reader[1])
                reader[:] = sem_name, count

            turn("xnT_done", 1)
            transpose_queries(0)
            turn("qT_done", 1)
            project_queries(0)
            keys(0, 0)
            values(0, 0)

            def body(i):
                q, xa, s1, s2 = stages(i)
                t1, t2 = i - 1, i - 2
                if not isinstance(i, int):
                    reader[:] = "cum_read", i - 2
                between = {
                    (0, 0): s1 and (lambda: (turn("att_tmp", t1 + 1), last_probs(t1))),
                    (0, 1): s2 and (lambda: (turn("smin_done", t2 + 1), scores2(t2))),
                    (0, 2): s1 and (lambda: (turn("x1_step", 3 * t1 + 1), project_out(att, wo, "att_done", t1, "o1_ps"))),
                    (0, 3): q and (lambda: (turn("xnT_done", i + 2), transpose_queries(i + 1))),
                    (1, 0): q and (lambda: (turn("qT_done", i + 2), project_queries(i + 1))),
                    (1, 1): s1 and (lambda: (turn("y1T_done", t1 + 1), transpose_rows(y1, "y1_done", t1, "y1t_ps"))),
                    (1, 2): s2 and (lambda: (turn("sm_step", 2 * (t2 + 1)), weight_sums(t2))),
                    (1, 3): s2 and (lambda: (turn("ext2_step", 2 * (t2 + 1)), weighted_values2(t2))),
                    (2, 0): s1 and (lambda: (turn("qk_done", t1 + 1), project_qk(t1))),
                    (2, 1): s1 and (lambda: (turn("v2_done", t1 + 1), project_out(y1T, av, "y1T_done", t1, "v2_ps"))),
                    (2, 2): s2 and (lambda: (turn("x2_step", 3 * t2 + 1), project_out(att2, ao, "att2_done", t2, "o2_ps"))),
                    (3, 0): s2 and (lambda: (turn("y2T_done", t2 + 1), transpose_rows(row, "y2_done", t2, "y2t_ps"))),
                    (3, 1): s2 and (lambda: (turn("logit_done", t2 + 1), gate(t2))),
                    (3, 2): s1 and (lambda: (turn("qkT_done", t1 + 1), transpose_qk(t1))),
                    (3, 3): s2 and (lambda: (turn("cum_read", t2 + 1), positions(t2))),
                }

                def short(j, place):
                    if between.get((j, place)):
                        between[j, place]()

                for j in range(TB):
                    ahead = xa and (j < TB - 1 or q)
                    ta, ja = (i, j + 1) if j < TB - 1 else (i + 1, 0)
                    if xa:
                        scores(i, j)
                    short(j, 0)
                    if ahead:
                        keys(ta, ja)
                    short(j, 1)
                    if ahead:
                        values(ta, ja)
                    short(j, 2)
                    if xa:
                        transpose_probs(i, j)
                    short(j, 3)
                    if xa:
                        weighted_values(i, j)

            tiles(loop=pe.Fori, body=body)

            hps = [score[:, m, 0:3 * CAP].rearrange("p (f n) -> p f n", f=3) for m in range(3)]
            dps = shared[:, 0:C * CAP].rearrange("p (c n) -> p c n", c=C)
            ops_ = score[:, 3, 0:C * CAP].rearrange("p (c n) -> p c n", c=C)
            turn("dt_evac", 0)

            def expert(i, r):
                e = 2 * i + r
                pe.wait_ge(s[f"ra_in{r}"], 32 * (i + 1))
                pe.wait_ge(s["dt_evac"], e)
                for c in range(C):
                    nc.tensor.transpose(dps[:, c, 0:P], ra[:, r, c * P:(c + 1) * P], k["ident"])
                    last = nc.tensor.transpose(dps[:, c, P:CAP], rb[:, r, c * P:(c + 1) * P],
                                               k["ident"][0:CR, 0:CR])
                last.then_inc(s["dt_ps"], 1)
                pe.wait_ge(s["dt_evac"], e + 1)
                pe.wait_ge(s[f"w1_in{r}"], 32 * (i + 1))
                for f in range(FT):
                    if f % 3 == 0:
                        pe.wait_ge(s["hid_done"], floor0(FT * (e - 1) + min(f + 3, FT)))
                    for c in range(C):
                        last = mm(hps[f // 3][:, f % 3, :], w1[:, r, c, f * P:(f + 1) * P], disp[:, c, :],
                                  start=c == 0, stop=c == C - 1)
                    if f % 3 == 2 or f == FT - 1:
                        last.then_inc(s["h_ps"], 1)
                pe.wait_ge(s["eo_done"], e)
                for c in range(C):
                    for f in range(FT):
                        if c == 0:
                            pe.wait_ge(s["hid_done"], FT * e + f + 1)
                        last = mm(ops_[:, c, :], w2[:, r, f, c * P:(c + 1) * P], hid[:, f, :],
                                  start=f == 0, stop=f == FT - 1)
                last.then_inc(s["eo_ps"], 1)
                last = None
                pe.wait_ge(s["eo_done"], e + 1)
                pe.wait_ge(s["fin_done"], e)
                for c in range(C):
                    nc.tensor.transpose(kps[:, 0, c * P:(c + 1) * P], eo[:, c, 0:P], k["ident"])
                    last = nc.tensor.transpose(vps[0:CR, 0, c * P:(c + 1) * P], eo[:, c, P:CAP], k["ident"])
                last.then_inc(s["et_ps"], 1)

            expert(0, 0)
            expert(0, 1)
            with pe.Fori(1, E // 2) as i:
                expert(i, 0)
                expert(i, 1)

        @block.scalar
        def _(act):
            af = nc.scalar.activation

            for r in range(2):
                act.dma_start(w1[:, r], a["w1"][r, :, :].rearrange("(c p) f -> p c f", c=C)).then_inc(s[f"w1_in{r}"], 16)
                act.dma_start(w2[:, r], a["w2"][r, :, :].rearrange("(t p) d -> p t d", t=FT)).then_inc(s[f"w1_in{r}"], 16)
            act.dma_start(b1[:], a["b1"].rearrange("e (t p) -> p e t", t=FT),
                          allow_slow_non_contiguous=True).then_inc(s["ffb_in"], 16)
            act.dma_start(b2[:], a["b2"].rearrange("e (c p) -> p e c", c=C),
                          allow_slow_non_contiguous=True).then_inc(s["ffb_in"], 16)
            act.wait_ge(s["weights_in"], 16 * 21)
            act.wait_ge(s["last_ps"], 1)
            for c in range(C):
                last = af(klast[:, c, :], shared[:, c * P:(c + 1) * P], ACT.Identity, bias=b_k[:, c:c + 1], scale=1.0)
            last.then_inc(s["klast_done"], 1)

            def copy_rows(dst, src, ready, t, done):
                act.wait_ge(s[ready], t + 1)
                af(dst, src, ACT.Copy).then_inc(s[done], 1)

            def queries(t):
                act.wait_ge(s["q_ps"], t + 1)
                act.wait_ge(s["qbd_in"], 16 * HH * t)
                for c in range(C):
                    last = af(qT[:, c, :], sh_c[:, c], ACT.Identity, bias=b_q[:, c:c + 1], scale=1.0)
                last.then_inc(s["qT_done"], 1)

            def exps(t, j):
                b = TB * t + j
                act.wait_ge(s["plast_done"], b)
                for c in range(C):
                    act.wait_ge(s["max_done"], 2 * b + c + 1)
                    for g in range(2):
                        m = 2 * c + g
                        last = af(prob[:, m, :], score[:, m, 0:S], ACT.Exp, bias=nmx[:, m:m + 1], scale=1.0,
                                  accum_out=esum[:, m:m + 1])
                    last.then_inc(s["exp_done"], 1)

            def keys(t, j):
                b = TB * t + j
                act.wait_ge(s["k_done"], b + 1)
                act.wait_ge(s["s_done"], floor0(2 * (b - 1)))
                for c in range(C):
                    last = af(kT[:, j % 2, c, 0:SM], kps[:, c, :], ACT.Identity, bias=b_k[:, c:c + 1], scale=1.0)
                last.then_inc(s["k_evac"], 1)

            def values(t, j):
                b = TB * t + j
                act.wait_ge(s["v_done"], b + 1)
                act.wait_ge(s["pv_done"], floor0(b - 1))
                af(vv[:, j % 2], vps[:, :, :], ACT.Copy).then_inc(s["v_evac"], 1)

            def probsT(t, j):
                b = TB * t + j
                act.wait_ge(s["pt_done"], 2 * b + 2)
                af(probT[:, 1, :, :].rearrange("p n x -> p (n x)"), score[:, 2, :], ACT.Copy).then_inc(s["ptb_evac"], 1)

            def squares(t):
                act.wait_ge(s["y1_done"], t + 1)
                act.wait_ge(s["rms_step"], t)
                af(sq[:, :], y1[:, :], ACT.Square, scale=float(1 / np.sqrt(D)), accum_out=msq[:, 0:1]).then_inc(s["sq_done"], 1)

            def sigmoid_tanh(t):
                act.wait_ge(s["s2_ps"], t + 1)
                act.wait_ge(s["sig_done"], TB * t)
                af(th[:, :], shared[:, :], ACT.Tanh, scale=float(SCALE / 2)).then_inc(s["th_done"], 1)

            def sigmoid_exp(t):
                act.wait_ge(s["smin_done"], t + 1)
                af(sneg[:, :], sneg[:, :], ACT.Exp, scale=float(SCALE)).then_inc(s["sneg_exp"], 1)

            def gate_exp(t):
                act.wait_ge(s["logit_done"], t + 1)
                act.wait_ge(s["route_step"], floor0(5 * t))
                af(ex[:, :], logit[:, :], ACT.Exp, bias=nlm[:, 0:1], scale=1.0, accum_out=se[:, 0:1]).then_inc(s["ex_done"], 1)

            copy_rows(xnT[:, :, :], sh_c, "qt_ps", 0, "xnT_done")
            queries(0)
            keys(0, 0)
            values(0, 0)

            def body(i):
                q, xa, s1, s2 = stages(i)
                t1, t2 = i - 1, i - 2
                for j in range(TB):
                    ahead = xa and (j < TB - 1 or q)
                    ta, ja = (i, j + 1) if j < TB - 1 else (i + 1, 0)
                    if xa:
                        exps(i, j)
                    if j == 1 and q:
                        queries(i + 1)
                    if j == 3 and s2:
                        copy_rows(y2T[:, :, :], sh_c, "y2t_ps", t2, "y2T_done")
                    if ahead:
                        keys(ta, ja)
                    if j == 0 and s2:
                        sigmoid_tanh(t2)
                    if j == 1 and s1:
                        squares(t1)
                        copy_rows(y1T[:, :, :], sh_c, "y1t_ps", t1, "y1T_done")
                    if j == 3 and s2:
                        gate_exp(t2)
                    if ahead:
                        values(ta, ja)
                    if j == 0 and s2:
                        sigmoid_exp(t2)
                    if j == 3 and s1:
                        act.wait_ge(s["qbd2_in"], 16 * HH * t1)
                        copy_rows(qkT[:, :, :].rearrange("p c n -> p (c n)"), shared[:, :], "qkt_ps", t1, "qkT_done")
                    if xa:
                        probsT(i, j)
                    if j == 0 and q:
                        copy_rows(xnT[:, :, :], sh_c, "qt_ps", i + 1, "xnT_done")

            tiles(loop=act.Fori, body=body)

            hps = [score[:, m, 0:3 * CAP].rearrange("p (f n) -> p f n", f=3) for m in range(3)]
            act.wait_ge(s["ffb_in"], 32)

            def hidden(e):
                act.wait_ge(s["eo_ps"], e)
                for f in range(FT):
                    if f % 3 == 0:
                        act.wait_ge(s["h_ps"], 3 * e + f // 3 + 1)
                    af(hid[:, f, :], hps[f // 3][:, f % 3, :], ACT.Gelu_apprx_tanh,
                       bias=b1[:, bass.ds(e, 1), f:f + 1].rearrange("p a b -> p (a b)"), scale=1.0).then_inc(s["hid_done"], 1)

            hidden(0)
            with act.Fori(1, E) as e:
                hidden(e)

        @block.vector
        def _(dve):
            v = nc.vector
            v.memset(qbd[:], 0.0).then_inc(s["zeroed"], 1)
            v.memset(qbd2[:], 0.0).then_inc(s["zeroed"], 1)
            v.memset(wbd[:], 0.0).then_inc(s["zeroed"], 1)
            v.memset(seen[:, :], 0.0).then_inc(s["seen_done"], 1)
            v.memset(row[:, :], 0.0).then_inc(s["slots_init"], 1)
            dve.wait_ge(s["const_in"], 16)
            v.tensor_copy(tri_bf[:, :], k["tri"]).then_inc(s["bf_consts"], 1)
            v.tensor_copy(ones_bf[:, :], k["ones"]).then_inc(s["bf_consts"], 1)
            dve.wait_ge(s["slots_init"], 1)
            v.tensor_copy(row[:, 2 * D + 1:ROW], k["sentinel"]).then_inc(s["slots_init"], 1)
            dve.wait_ge(s["weights_in"], 16 * 21)
            for c in range(C):
                v.tensor_scalar(aqk[:, c, 0:D], aqk[:, c, 0:D], qn[:, c:c + 1], None, ALU.mult).then_inc(s["scaled"], 1)
                v.tensor_scalar(aqk[:, c, D:2 * D], aqk[:, c, D:2 * D], kn[:, c:c + 1], None, ALU.mult).then_inc(s["scaled"], 1)
            dve.wait_ge(s["klast_done"], 1)
            v.tensor_copy(vlast[:, :, :, :].rearrange("p t c j -> p c t j"),
                          shared[:, C * P:2 * C * P].rearrange("p (c t j) -> p c t j", c=C, j=TB)).then_inc(s["vlast_done"], 1)

            def norm_stats(x, n, step, base):
                v.bn_stats(stat[n][:, :], x).then_inc(s[step], 1)
                dve.wait_ge(s[step], base + 1)
                settle(dve)
                v.bn_aggr(mv[n][:, :], stat[n][:, :]).then_inc(s[step], 1)
                dve.wait_ge(s[step], base + 2)

            def norm_x(t):
                dve.wait_ge(s["xq_in"], 16 * (t + 1))
                norm_stats(xq[:, :], "q", "xn_stat", 3 * t)
                dve.wait_ge(s["xn_pow"], t)
                v.tensor_scalar(ve["q"][:, :], mv["q"][:, 1:2], 1e-5, None, ALU.add).then_inc(s["xn_stat"], 1)

            def norm_x_apply(t):
                dve.wait_ge(s["xn_pow"], t + 1)
                dve.wait_ge(s["qt_ps"], t)
                v.tensor_scalar(xn[:, :], xq[:, :], mv["q"][:, 0:1], rstd["q"][:, 0:1], ALU.subtract, ALU.mult
                                ).then_inc(s["xn_done"], 1)

            def maxima(t, j):
                b = TB * t + j
                for c in range(C):
                    dve.wait_ge(s["s_done"], 2 * b + c + 1)
                    v.tensor_reduce(nmx[:, 2 * c:2 * c + 2], score[:, 2 * c:2 * c + 2, 0:S], AX.X, ALU.max, negate=True
                                    ).then_inc(s["max_done"], 1)

            def normalise(t, j):
                b = TB * t + j
                for c in range(C):
                    dve.wait_ge(s["exp_done"], 2 * b + c + 1)
                    v.reciprocal(rsum[:, 2 * c:2 * c + 2], esum[:, 2 * c:2 * c + 2]).then_inc(s["rsum_done"], 1)
                    dve.wait_ge(s["rsum_done"], 2 * b + c + 1)
                    for g in range(2):
                        m = 2 * c + g
                        last = v.tensor_scalar(prob[:, m, :], prob[:, m, :], rsum[:, m:m + 1], None, ALU.mult)
                    last.then_inc(s["norm_done"], 1)

            def probsT(t, j):
                b = TB * t + j
                dve.wait_ge(s["pt_done"], 2 * b + 1)
                v.tensor_copy(probT[:, 0, :, :].rearrange("p n x -> p (n x)"), score[:, 0, :]).then_inc(s["pta_evac"], 1)

            def extract(t):
                dve.wait_ge(s["pv_done"], TB * (t + 1))
                v.tensor_scalar(att[:, :, :], gather[:, :, 0, :], k["even"], None, ALU.mult).then_inc(s["ext_step"], 1)
                dve.wait_ge(s["ext_step"], 2 * t + 1)
                v.scalar_tensor_tensor(att[:, :, :], gather[:, :, 1, :], k["odd"], att[:, :, :], ALU.mult, ALU.add
                                       ).then_inc(s["ext_step"], 1)
                dve.wait_ge(s["ll_ps"], t + 1)
                v.tensor_tensor(alast[:, :, :].rearrange("p c (j q) -> p (c j) q", j=TB),
                                shared[:, 0:C * P].rearrange("p (x q) -> p x q", q=L),
                                vlast[:, bass.ds(t, 1), :, :].rearrange("p a c j -> p (a c j)").unsqueeze(2)
                                .to_broadcast([P, C * TB, L]), ALU.mult).then_inc(s["att_tmp"], 1)
                dve.wait_ge(s["att_tmp"], t + 1)
                dve.wait_ge(s["ext_step"], 2 * t + 2)
                for c in range(C):
                    last = v.scalar_tensor_tensor(att[:, c, :], alast[:, c, :], b_v[:, c:c + 1], att[:, c, :],
                                                  ALU.add, ALU.add)
                last.then_inc(s["att_done"], 1)

            def residual1(t):
                dve.wait_ge(s["o1_ps"], t + 1)
                dve.wait_ge(s["xrb_done"], t + 1)
                dve.wait_ge(s["x1b_done"], t)
                v.tensor_tensor(x1[:, :], shared[:, 0:D], xr[:, :], ALU.add).then_inc(s["x1_step"], 1)

            def residual1_stats(t):
                dve.wait_ge(s["x1_step"], 3 * t + 1)
                v.bn_stats(stat["1"][:, :], x1[:, :]).then_inc(s["x1_step"], 1)
                dve.wait_ge(s["x1_step"], 3 * t + 2)
                settle(dve)
                v.bn_aggr(mv["1"][:, :], stat["1"][:, :]).then_inc(s["x1_step"], 1)
                dve.wait_ge(s["x1_step"], 3 * t + 3)
                v.tensor_scalar(ve["1"][:, :], mv["1"][:, 1:2], 1e-5, None, ALU.add).then_inc(s["x1_done"], 1)

            def norm1(t):
                dve.wait_ge(s["x1_pow"], t + 1)
                v.tensor_scalar(y1[:, :], x1[:, :], mv["1"][:, 0:1], rstd["1"][:, 0:1], ALU.subtract, ALU.mult
                                ).then_inc(s["y1_done"], 1)

            def evac_qk(t):
                dve.wait_ge(s["qk_ps"], t + 1)
                dve.wait_ge(s["rrms_done"], t + 1)
                v.scalar_tensor_tensor(qk[:, :], shared[:, :], rrms[:, 0:1], r_qk[:, :], ALU.mult, ALU.add
                                       ).then_inc(s["qk_done"], 1)
                dve.wait_ge(s["qk_done"], t + 1)
                v.tensor_tensor(qkc[:, :].rearrange("p (h d) -> p h d", d=HD), qk[:, :].rearrange("p (h d) -> p h d", d=HD),
                                k["cos"].unsqueeze(1).to_broadcast([P, 2 * H, HD]), ALU.mult).then_inc(s["qkc_done"], 1)

            def evac_v2(t):
                dve.wait_ge(s["v2_ps"], t + 1)
                v.tensor_tensor(v2[:, :], shared[:, 0:D], r_v2[:, :], ALU.add).then_inc(s["v2_done"], 1)

            def sigmoid_min(t):
                dve.wait_ge(s["th_done"], t + 1)
                v.tensor_scalar(sneg[:, :], shared[:, :], 0.0, None, ALU.min).then_inc(s["smin_done"], 1)
                v.scalar_tensor_tensor(tabs[:, :], th[:, :], -1.0, th[:, :], ALU.mult, ALU.max).then_inc(s["tabs_done"], 1)

            def sigmoid_blocks(t):
                dve.wait_ge(s["tabs_done"], t + 1)
                dve.wait_ge(s["sneg_exp"], t + 1)
                for j in range(TB):
                    b = slice(32 * j, 32 * j + 32)
                    v.scalar_tensor_tensor(wbd[b, :, b], tabs[b, :].rearrange("p (h q) -> p h q", h=H), 1.0,
                                           sneg[b, :].rearrange("p (h q) -> p h q", h=H), ALU.add, ALU.mult
                                           ).then_inc(s["sig_done"], 1)

            def sums2(t):
                dve.wait_ge(s["sm_ps"], t + 1)
                v.tensor_scalar(ssum[:, :, :], sh_pair[:, :, 0, :], k["even"], 2e-8, ALU.mult, ALU.add).then_inc(s["sm_step"], 1)
                dve.wait_ge(s["sm_step"], 2 * t + 1)
                v.scalar_tensor_tensor(ssum[:, :, :], sh_pair[:, :, 1, :], k["odd"], ssum[:, :, :], ALU.mult, ALU.add
                                       ).then_inc(s["sm_step"], 1)

            def inverse2(t):
                dve.wait_ge(s["sm_step"], 2 * t + 2)
                v.reciprocal(ssum[:, :, :], ssum[:, :, :]).then_inc(s["ssum_done"], 1)

            def extract2(t):
                dve.wait_ge(s["pv2_ps"], t + 1)
                v.tensor_scalar(att2[:, :, :], sh_pair[:, :, 0, :], k["even"], None, ALU.mult).then_inc(s["ext2_step"], 1)
                dve.wait_ge(s["ext2_step"], 2 * t + 1)
                v.scalar_tensor_tensor(att2[:, :, :], sh_pair[:, :, 1, :], k["odd"], att2[:, :, :], ALU.mult, ALU.add
                                       ).then_inc(s["ext2_step"], 1)
                dve.wait_ge(s["ext2_step"], 2 * t + 2)
                dve.wait_ge(s["ssum_done"], t + 1)
                v.tensor_tensor(att2[:, :, :], att2[:, :, :], ssum[:, :, :], ALU.mult).then_inc(s["att2_done"], 1)

            def residual2(t):
                dve.wait_ge(s["o2_ps"], t + 1)
                dve.wait_ge(s["sent"], 16 * t)
                dve.wait_ge(s["x2_out"], 16 * t)
                v.tensor_tensor(row[:, D:2 * D], shared[:, 0:D], x1b[:, :], ALU.add).then_inc(s["x2_step"], 1)

            def residual2_stats(t):
                dve.wait_ge(s["x2_step"], 3 * t + 1)
                v.bn_stats(stat["2"][:, :], row[:, D:2 * D]).then_inc(s["x2_step"], 1)
                dve.wait_ge(s["x2_step"], 3 * t + 2)
                settle(dve)
                v.bn_aggr(mv["2"][:, :], stat["2"][:, :]).then_inc(s["x2_step"], 1)
                dve.wait_ge(s["x2_step"], 3 * t + 3)
                v.tensor_scalar(ve["2"][:, :], mv["2"][:, 1:2], 1e-5, None, ALU.add).then_inc(s["x2_done"], 1)

            def norm2(t):
                dve.wait_ge(s["x2_pow"], t + 1)
                v.tensor_scalar(row[:, 0:D], row[:, D:2 * D], mv["2"][:, 0:1], rstd["2"][:, 0:1], ALU.subtract, ALU.mult
                                ).then_inc(s["y2_done"], 1)

            def logits(t):
                dve.wait_ge(s["g_ps"], t + 1)
                v.tensor_tensor(logit[:, :], shared[:, 0:E], r_g[:, :], ALU.add).then_inc(s["route_step"], 1)
                dve.wait_ge(s["route_step"], 5 * t + 1)
                v.tensor_reduce(nlm[:, :], logit[:, :], AX.X, ALU.max, negate=True).then_inc(s["logit_done"], 1)

            def choose(t):
                dve.wait_ge(s["ex_done"], t + 1)
                v.reciprocal(rse[:, :], se[:, :]).then_inc(s["route_step"], 1)
                dve.wait_ge(s["route_step"], 5 * t + 2)
                v.tensor_scalar(pr[:, :], ex[:, :], rse[:, 0:1], None, ALU.mult).then_inc(s["route_step"], 1)
                dve.wait_ge(s["route_step"], 5 * t + 3)
                v.tensor_reduce(row[:, 2 * D:2 * D + 1], pr[:, :], AX.X, ALU.max).then_inc(s["route_step"], 1)
                dve.wait_ge(s["route_step"], 5 * t + 4)
                v.scalar_tensor_tensor(eqr[:, :], pr[:, :], row[:, 2 * D:2 * D + 1], k["rank"], ALU.is_equal, ALU.mult
                                       ).then_inc(s["route_step"], 1)
                dve.wait_ge(s["route_step"], 5 * t + 5)
                dve.wait_ge(s["slot_done"], t)
                v.tensor_reduce(top[:, :], eqr[:, :], AX.X, ALU.max).then_inc(s["top_done"], 1)
                dve.wait_ge(s["top_done"], t + 1)
                v.tensor_scalar(oh[:, :], eqr[:, :], top[:, 0:1], None, ALU.is_equal).then_inc(s["oh_done"], 1)

            def position(t):
                dve.wait_ge(s["cum_ps"], t + 1)
                dve.wait_ge(s["oh_done"], t + 1)
                v.tensor_tensor(cumoh[:, :], shared[:, 0:E], oh[:, :], ALU.mult).then_inc(s["cum_read"], 1)
                v.tensor_tensor(seen[:, :], seen[:, :], oh[:, :], ALU.add).then_inc(s["seen_done"], 1)
                dve.wait_ge(s["cum_read"], t + 1)
                v.tensor_reduce(pos[:, :], cumoh[:, :], AX.X, ALU.add).then_inc(s["pos_done"], 1)

            norm_x(0)
            norm_x_apply(0)

            def body(i):
                q, xa, s1, s2 = stages(i)
                t1, t2 = i - 1, i - 2
                for j in range(TB):
                    if xa:
                        maxima(i, j)
                    if j == 0 and q:
                        norm_x(i + 1)
                    if xa:
                        normalise(i, j)
                    if j == 0:
                        if s1:
                            extract(t1)
                        if q:
                            norm_x_apply(i + 1)
                        if s2:
                            sigmoid_min(t2)
                        if s1:
                            residual1(t1)
                    if j == 1:
                        if s1:
                            norm1(t1)
                        if s2:
                            sigmoid_blocks(t2)
                            sums2(t2)
                    if j == 2:
                        if s1:
                            evac_qk(t1)
                            evac_v2(t1)
                        if s2:
                            residual2(t2)
                    if j == 3 and s2:
                        logits(t2)
                        choose(t2)
                    if xa:
                        probsT(i, j)
                    if j == 0 and s1:
                        residual1_stats(t1)
                    if j == 1 and s2:
                        inverse2(t2)
                        extract2(t2)
                    if j == 2 and s2:
                        residual2_stats(t2)
                        norm2(t2)
                    if j == 3 and s2:
                        position(t2)

            tiles(loop=dve.Fori, body=body)

            dps = shared[:, 0:C * CAP]
            ops_ = score[:, 3, 0:C * CAP].rearrange("p (c n) -> p c n", c=C)

            def expert(i, r):
                e = 2 * i + r
                dve.wait_ge(s["dt_ps"], e + 1)
                v.tensor_copy(disp[:, :, :].rearrange("p c n -> p (c n)"), dps).then_inc(s["dt_evac"], 1)
                dve.wait_ge(s["eo_ps"], e + 1)
                for c in range(C):
                    last = v.tensor_scalar(eo[:, c, :], ops_[:, c, :], b2_of(e, c), None, ALU.add)
                last.then_inc(s["eo_done"], 1)
                dve.wait_ge(s["et_ps"], e + 1)
                dve.wait_ge(s[f"fin_out{r}"], 32 * i)
                v.scalar_tensor_tensor(fa[:, r, :], kps[:, 0, :], ra[:, r, 2 * D:2 * D + 1], ra[:, r, D:2 * D],
                                       ALU.mult, ALU.add)
                v.scalar_tensor_tensor(fb[:, r, :], vps[0:CR, 0, :], rb[:, r, 2 * D:2 * D + 1], rb[:, r, D:2 * D],
                                       ALU.mult, ALU.add).then_inc(s["fin_done"], 1)

            def b2_of(e, c):
                return b2[:, bass.ds(e, 1), c:c + 1].rearrange("p a b -> p (a b)")

            dve.wait_ge(s["ffb_in"], 32)
            for r in range(2):
                expert(0, r)
            with dve.Fori(1, E // 2) as i:
                for r in range(2):
                    expert(i, r)

        @block.gpsimd
        def _(pool):
            g = nc.gpsimd

            def power(n, ready, count, t, done):
                pool.wait_ge(s[ready], count)
                g.tensor_tensor(rstd[n][:, :], ve[n][:, :], k["mhalf"], ALU.pow).then_inc(s[done], 1)

            def last_key(t, j):
                b = TB * t + j
                pool.wait_ge(s["s_done"], floor0(2 * (b - 1)))
                g.tensor_copy(kT[:, j % 2, :, SM:S], klast[:, :, bass.ds(b, 1)]).then_inc(s["klast_cp"], 1)

            def last_prob(t, j):
                b = TB * t + j
                pool.wait_ge(s["norm_done"], 2 * b + 2)
                if j == 0:
                    pool.wait_ge(s["ll_ps"], t)
                g.tensor_tensor(plast[:, :, j, :], k["diag"].unsqueeze(1).to_broadcast([P, MT, L]),
                                prob[:, :, SM:S].to_broadcast([P, MT, L]), ALU.mult).then_inc(s["plast_done"], 1)

            def residual_bias(t):
                pool.wait_ge(s["xr_in"], 16 * (t + 1))
                g.tensor_tensor(xr[:, :], xr[:, :], r_o[:, :], ALU.add).then_inc(s["xrb_done"], 1)

            def rms(t):
                pool.wait_ge(s["sq_done"], t + 1)
                settle(pool)
                g.tensor_scalar(mse[:, :], msq[:, :], 1e-8, None, ALU.add).then_inc(s["rms_step"], 1)
                pool.wait_ge(s["rms_step"], t + 1)
                g.tensor_tensor(rrms[:, :], mse[:, :], k["mhalf"], ALU.pow).then_inc(s["rrms_done"], 1)

            def rope_sin(t):
                pool.wait_ge(s["qk_done"], t + 1)
                for o in range(2):
                    last = g.tensor_tensor(
                        qks[:, :].rearrange("p (h d o) -> p h d o", d=HD // 2, o=2)[:, :, :, o],
                        qk[:, :].rearrange("p (h d o) -> p h d o", d=HD // 2, o=2)[:, :, :, 1 - o],
                        k["sin"].rearrange("p (d o) -> p d o", o=2)[:, :, o].unsqueeze(1).to_broadcast([P, 2 * H, HD // 2]),
                        ALU.mult)
                last.then_inc(s["qks_done"], 1)

            def rope_add(t):
                pool.wait_ge(s["qkc_done"], t + 1)
                pool.wait_ge(s["qks_done"], t + 1)
                g.tensor_tensor(qk[:, :], qkc[:, :], qks[:, :], ALU.add).then_inc(s["rope_done"], 1)

            def residual_bias2(t):
                pool.wait_ge(s["y1_done"], t + 1)
                pool.wait_ge(s["x2_step"], floor0(3 * (t - 1) + 1))
                g.tensor_tensor(x1b[:, :], x1[:, :], r_o2[:, :], ALU.add).then_inc(s["x1b_done"], 1)

            def slot_numbers(t):
                pool.wait_ge(s["top_done"], t + 1)
                settle(pool)
                g.tensor_scalar(first[:, :], top[:, :], -float(CAP), float(E * CAP - 1), ALU.mult, ALU.add
                                ).then_inc(s["slot_step"], 1)
                g.tensor_scalar(token[:, :], away[:, :], -float(E * CAP), None, ALU.add).then_inc(s["slot_step"], 1)
                pool.wait_ge(s["slot_step"], 7 * t + 2)
                pool.wait_ge(s["pos_done"], t + 1)
                settle(pool)
                g.tensor_copy(row[:, 2 * D + 1:ROW].bitcast(I32), token[:, :]).then_inc(s["slot_step"], 1)
                g.tensor_tensor(slot[:, :], first[:, :], pos[:, :], ALU.add).then_inc(s["slot_step"], 1)
                pool.wait_ge(s["slot_step"], 7 * t + 4)
                g.tensor_tensor(off[:, :], slot[:, :], away[:, :], ALU.subtract).then_inc(s["slot_step"], 1)
                pool.wait_ge(s["slot_step"], 7 * t + 5)
                settle(pool)
                g.tensor_scalar(kept[:, :], pos[:, :], float(CAP), off[:, 0:1], ALU.is_le, ALU.mult).then_inc(s["slot_step"], 1)
                pool.wait_ge(s["slot_step"], 7 * t + 6)
                g.tensor_tensor(slotf[:, :], kept[:, :], away[:, :], ALU.add).then_inc(s["slot_step"], 1)
                pool.wait_ge(s["slot_step"], 7 * t + 7)
                pool.wait_ge(s["sent"], 16 * t)
                settle(pool)
                g.tensor_copy(sloti[:, :], slotf[:, :]).then_inc(s["slot_done"], 1)
                g.tensor_scalar(away[:, :], away[:, :], float(P), None, ALU.add).then_inc(s["away_done"], 1)
                pool.wait_ge(s["slot_done"], t + 1)
                pool.wait_ge(s["away_done"], t + 2)

            def send(t):
                pool.wait_ge(s["y2_done"], t + 1)
                settle(pool)
                g.indirect_dma_start(out=slots, out_offset=bass.IndirectOffsetOnAxis(sloti[:, 0:1], 0), in_=row[:, :],
                                     in_offset=None, bounds_check=E * CAP - 1, oob_is_err=False).then_inc(s["sent"], 16)

            pool.wait_ge(s["const_in"], 16)
            g.tensor_copy(away[:, :], k["token"]).then_inc(s["away_done"], 1)
            pool.wait_ge(s["slots_init"], 2)
            for n in range(E * CAP // P):
                pool.dma_start(slots[n * P:(n + 1) * P, :], row[:, :]).then_inc(s["slots_zero"], 16)
            power("q", "xn_stat", 3, 0, "xn_pow")
            pool.wait_ge(s["klast_done"], 1)
            last_key(0, 0)
            pool.wait_ge(s["slots_zero"], 16 * (E * CAP // P))

            def body(i):
                q, xa, s1, s2 = stages(i)
                t1, t2 = i - 1, i - 2
                for j in range(TB):
                    if xa and (j < TB - 1 or q):
                        last_key(*((i, j + 1) if j < TB - 1 else (i + 1, 0)))
                    if j == 0 and s1:
                        residual_bias(t1)
                    if j == 2 and s1:
                        rope_sin(t1)
                        rope_add(t1)
                    if xa:
                        last_prob(i, j)
                    if j == 0:
                        if q:
                            power("q", "xn_stat", 3 * (i + 2), i + 1, "xn_pow")
                        if s1:
                            power("1", "x1_done", t1 + 1, t1, "x1_pow")
                    if j == 1 and s1:
                        rms(t1)
                    if j == 2 and s2:
                        power("2", "x2_done", t2 + 1, t2, "x2_pow")
                    if j == 3 and s1:
                        residual_bias2(t1)
                    if j == 3 and s2:
                        slot_numbers(t2)
                        send(t2)

            tiles(loop=pool.Fori, body=body)

            with pool.Fori(0, E // 2) as i:
                for r in range(2):
                    pool.wait_ge(s["fin_done"], 2 * i + r + 1)
                    settle(pool)
                    for rows, res in ((ra, fa), (rb, fb)):
                        g.indirect_dma_start(out=out, out_offset=bass.IndirectOffsetOnAxis(
                                                 rows[:, r, 2 * D + 1:ROW].bitcast(I32), 0),
                                             in_=res[:, r, :], in_offset=None, bounds_check=B * L - 1, oob_is_err=False
                                             ).then_inc(s[f"fin_out{r}"], 16)


def kernel(x, ctx_1024, L0_xattn_Wq, L0_xattn_bq, L0_xattn_Wk, L0_xattn_bk, L0_xattn_Wv, L0_xattn_bv, L0_xattn_Wo,
           L0_xattn_bo, L0_attn_q_w, L0_attn_q_b, L0_attn_k_w, L0_attn_k_b, L0_attn_v_w, L0_attn_v_b, L0_attn_o_w,
           L0_attn_o_b, L0_attn_qn_scale, L0_attn_kn_scale, L0_ffn_gate_w, L0_ffn_gate_b, L0_ffn_w1, L0_ffn_b1,
           L0_ffn_w2, L0_ffn_b2):
    import concourse.bacc as bacc
    from concourse.bass_utils import run_bass_kernel_spmd

    ctxT = np.asarray(ctx_1024).transpose(2, 0, 1)
    arrays = {
        "x": np.asarray(x).reshape(B * L, D), "ctxT": ctxT, "lastT": ctxT[:, :, S - 1], "const": constants(),
        "Wq": np.asarray(L0_xattn_Wq).T, "Wk": np.asarray(L0_xattn_Wk).T, "Wv": np.asarray(L0_xattn_Wv).T,
        "Wo": np.asarray(L0_xattn_Wo).T, "q_w": np.asarray(L0_attn_q_w).T, "k_w": np.asarray(L0_attn_k_w).T,
        "v_w": np.asarray(L0_attn_v_w).T, "o_w": np.asarray(L0_attn_o_w).T,
        "bq": L0_xattn_bq, "bk": L0_xattn_bk, "bv": L0_xattn_bv, "bo": L0_xattn_bo,
        "q_b": L0_attn_q_b, "k_b": L0_attn_k_b, "v_b": L0_attn_v_b, "o_b": L0_attn_o_b,
        "qn": L0_attn_qn_scale, "kn": L0_attn_kn_scale, "gate_w": L0_ffn_gate_w, "gate_b": L0_ffn_gate_b,
        "w1": L0_ffn_w1, "b1": L0_ffn_b1, "w2": L0_ffn_w2, "b2": L0_ffn_b2,
    }
    arrays = {n: np.ascontiguousarray(v) for n, v in arrays.items()}
    nc = bacc.Bacc("TRN2", target_bir_lowering=False, num_devices=1)
    aps = {n: nc.dram_tensor("in_" + n, v.shape, mybir.dt.from_np(v.dtype), kind="ExternalInput").ap()
           for n, v in arrays.items()}
    out = nc.dram_tensor("out", (B * L, D), F32, kind="ExternalOutput").ap()
    build(nc, aps, out)
    r = run_bass_kernel_spmd(nc, [{"in_" + n: v for n, v in arrays.items()}], core_ids=[0])
    return r.results[0]["out"].reshape(B, L, D)
```

```python
from contextlib import ExitStack

import numpy as np
import concourse.bass as bass
from concourse import mybir

F32 = mybir.dt.float32
F32R = mybir.dt.float32r
BF16 = mybir.dt.bfloat16
I32 = mybir.dt.int32
ALU = mybir.AluOpType
ACT = mybir.ActivationFunctionType
AX = mybir.AxisListType

P = 128
B, L, D = 128, 32, 256
S = 257
SE = S + 1
SM = 256
H, HD = 16, 16
C = D // P
TB = P // L
T = B * L // P
HH = H // C
MT = H * L // P
E, CAP, F = 8, 160, 1024
FT = F // P
CR = CAP - P
ROW = 2 * D + 2
SCALE = 1.0 / np.sqrt(HD)

CONST = {}
_at = 0
for _name, _n in (("ident", P), ("tri", P), ("ones", P), ("spread", 2 * P), ("diag", L), ("cos", HD), ("sin", HD),
                  ("even", 1), ("odd", 1), ("rank", E), ("token", 1), ("mhalf", 1), ("sentinel", 1)):
    CONST[_name] = (_at, _at + _n)
    _at += _n
NCONST = _at


def constants():
    t = np.zeros((P, NCONST), np.float32)
    p = np.arange(P)

    def put(name, v):
        t[:, CONST[name][0]:CONST[name][1]] = v

    put("ident", np.eye(P))
    put("tri", p[:, None] <= p[None, :])
    put("ones", 1.0)
    put("spread", np.concatenate([(4 * m + p[:, None] // L) == p[None, :] // HD for m in range(2)], 1))
    put("diag", p[:, None] % L == np.arange(L)[None, :])
    inv_freq = 1.0 / np.float32(10000.0) ** (np.arange(0, HD, 2, dtype=np.float32) / HD)
    angle = (p % L).astype(np.float32)[:, None] * inv_freq[None, :].astype(np.float32)
    angle = np.concatenate([angle, angle], 1)
    put("cos", np.cos(angle))
    put("sin", np.sin(angle) * np.where(np.arange(HD) % 2, 1.0, -1.0))
    put("even", ((p // HD) % 2 == 0)[:, None])
    put("odd", ((p // HD) % 2 == 1)[:, None])
    put("rank", E - np.arange(E)[None, :])
    put("token", (E * CAP + p)[:, None])
    put("mhalf", -0.5)
    put("sentinel", 0.0)
    t[:, CONST["sentinel"][0]] = np.full(P, 1 << 20, np.int32).view(np.float32)
    return t


PASSES = ((1, 0), (0, 0), (0, 1))
HI, LO = 0, 1


def floor0(count):
    return max(count, 0) if isinstance(count, int) else count


def build(nc, a, out):
    ctx = ExitStack()
    with ctx:
        def sb(name, shape, dt=F32):
            return ctx.enter_context(nc.sbuf_tensor(name, shape, dt))

        def ps(name, shape, dt=F32):
            return ctx.enter_context(nc.psum_tensor(name, shape, dt))

        def sem(name):
            return ctx.enter_context(nc.semaphore(name))

        slots = nc.dram_tensor("slots", (E * CAP, ROW), F32, kind="Internal").ap()

        wq, wk, wv, wo, av, ao = (sb(n, [P, C, D]) for n in ("wq", "wk", "wv", "wo", "av", "ao"))
        aqk = sb("aqk", [P, C, 2 * D])
        gw = sb("gw", [P, C, E])
        const = sb("const", [P, NCONST])
        wk_p, wv_p, av_p = (sb(n, [P, 2, C, D], F32R) for n in ("wk_p", "wv_p", "av_p"))
        aqk_p = sb("aqk_p", [P, 2, C, 2 * D], F32R)
        k = {n: const[:, lo:hi] for n, (lo, hi) in CONST.items()}
        tri_bf, ones_bf = sb("tri_bf", [P, P], BF16), sb("ones_bf", [P, P], BF16)
        b_q, b_k, b_v = (sb(n, [P, C]) for n in ("b_q", "b_k", "b_v"))
        qn, kn = sb("qn", [P, C]), sb("kn", [P, C])
        r_o, r_v2, r_o2 = (sb(n, [P, D]) for n in ("r_o", "r_v2", "r_o2"))
        r_qk = sb("r_qk", [P, 2 * D])
        r_g = sb("r_g", [P, E])
        ctxT = sb("ctxT", [P, 2, C, 2, S])
        lastT = sb("lastT", [P, C, B])
        ctx_p = sb("ctx_p", [P, 2, 2, C, SM], F32R)
        klast = sb("klast", [P, C, B])
        klast_p = sb("klast_p", [P, 2, C, B], F32R)
        vlast = sb("vlast", [P, T, C, TB])
        kT = sb("kT", [P, 2, 2, C, SE], F32R)
        vv = sb("vv", [P, 2, C, D])
        xq, xn, xnT, qT = sb("xq", [P, D]), sb("xn", [P, D]), sb("xnT", [P, C, P]), sb("qT", [P, C, P])
        qbd = sb("qbd", [P, C, TB, HH, L])
        qbd_p = sb("qbd_p", [P, 2, 2, C, HH * L], F32R)
        nmx, esum, rsum = sb("nmx", [P, MT]), sb("esum", [P, MT]), sb("rsum", [P, MT])
        prob = sb("prob", [P, MT, S])
        probT = sb("probT", [P, C, 2, HH * L])
        plast = sb("plast", [P, MT, TB, L])
        att, alast = sb("att", [P, C, P]), sb("alast", [P, C, P])
        xr, x1, x1b, y1, sq = (sb(n, [P, D]) for n in ("xr", "x1", "x1b", "y1", "sq"))
        y1T = sb("y1T", [P, C, P])
        y1T_p = sb("y1T_p", [P, 2, C, P], F32R)
        qk, qkc, qks = sb("qk", [P, 2 * D]), sb("qkc", [P, 2 * D]), sb("qks", [P, 2 * D])
        qkT = sb("qkT", [P, 2 * C, P])
        qbd2 = sb("qbd2", [P, C, HH, P])
        v2 = sb("v2", [P, D])
        th, tabs, sneg = (sb(n, [P, 2 * D]) for n in ("th", "tabs", "sneg"))
        wbd = sb("wbd", [P, H, P])
        ssum, att2 = sb("ssum", [P, C, P]), sb("att2", [P, C, P])
        row = sb("row", [P, ROW])
        y2T = sb("y2T", [P, C, P])
        stat = {n: sb("stat_" + n, [P, 6]) for n in "q12"}
        mv = {n: sb("mv_" + n, [P, 2]) for n in "q12"}
        ve = {n: sb("ve_" + n, [P, 1]) for n in "q12"}
        rstd = {n: sb("rstd_" + n, [P, 1]) for n in "q12"}
        msq, mse, rrms = sb("msq", [P, 1]), sb("mse", [P, 1]), sb("rrms", [P, 1])
        logit, nlm, ex, se, rse, pr = (sb(n, [P, w]) for n, w in (("logit", E), ("nlm", 1), ("ex", E), ("se", 1), ("rse", 1), ("pr", E)))
        eqr, top, oh = sb("eqr", [P, E]), sb("top", [P, 1]), sb("oh", [P, E], BF16)
        seen = sb("seen", [P, E], BF16)
        cumoh, pos = sb("cumoh", [P, E]), sb("pos", [P, 1])
        first, slot, off, kept, slotf = (sb(n, [P, 1]) for n in ("first", "slot", "off", "kept", "slotf"))
        away, token = sb("away", [P, 1]), sb("token", [P, 1])
        sloti = sb("sloti", [P, 1], I32)
        w1 = sb("w1", [P, 2, C, F])
        w2 = sb("w2", [P, 2, FT, D])
        b1, b2 = sb("b1", [P, E, FT]), sb("b2", [P, E, C])
        ra, rb = sb("ra", [P, 2, ROW]), sb("rb", [CR, 2, ROW])
        disp = sb("disp", [P, C, CAP])
        hid = sb("hid", [P, FT, CAP])
        eo = sb("eo", [P, C, CAP])
        fa, fb = sb("fa", [P, 2, D]), sb("fb", [CR, 2, D])

        score = ps("score", [P, MT, 512])
        kps, vps = ps("kps", [P, C, SM]), ps("vps", [P, C, D])
        shared = ps("shared", [P, 512])
        gather = ps("gather", [P, C, 2, P])
        sh_c = shared[:, 0:C * P].rearrange("p (c n) -> p c n", c=C)
        sh_pair = shared[:, :].rearrange("p (c g n) -> p c g n", c=C, g=2)

        names = """const_in weights_in w_done bf_consts scaled zeroed klast_done vlast_done last_ps_free last_ps
            xq_in xr_in xn_stat xn_pow xn_done qt_ps xnT_done q_ps qT_done qbd_in
            k_done k_evac klast_cp v_done v_evac s_done max_done exp_done rsum_done norm_done plast_done
            pt_done pta_evac ptb_evac pv_done ll_ps ext_step att_done
            xrb_done o1_ps x1_step x1_done x1_pow y1_done sq_done rms_step rrms_done x1b_done y1t_ps y1T_done
            qk_ps qk_done qkc_done qks_done rope_done v2_ps v2_done qkt_ps qkT_done qbd2_in s2_ps sig_done
            sm_ps sm_step ssum_done pv2_ps ext2_step att2_done o2_ps x2_step x2_done x2_pow y2_done x2_out
            y2t_ps y2T_done g_ps route_step logit_done ex_done oh_done cum_ps pos_step cum_read seen_done pos_done
            slot_step slot_done sent slots_init slots_zero away_done top_done att_tmp
            th_done relu_done sneg_exp
            ra_in0 ra_in1 w1_in0 w1_in1 ffb_in dt_ps dt_evac h_ps hid_done eo_ps eo_done et_ps fin_done fin_out0 fin_out1
            wparts_hi wparts_done klast_hi klast_parts ctx_hi ctx_parts qbd_hi qbd_parts k_lo y1T_hi y1T_parts
            settled""".split()
        s = {n: sem(n) for n in names}
        ctx_in = [sem("ctx_in0"), sem("ctx_in1")]
        block = ctx.enter_context(nc.Block())

        def settle(eng):
            eng.sem_inc(s["settled"], 1)

        def tiles(*, loop, body):
            for i in range(3):
                body(i)
            with loop(3, T - 1) as i:
                body(i)
            body(T - 1)
            body(T)
            body(T + 1)

        def stages(i):
            if not isinstance(i, int):
                return True, True, True, True
            return i <= T - 2, i <= T - 1, 1 <= i <= T, 2 <= i

        @block.sync
        def _(sp):
            sp.dma_start(const[:, :], a["const"]).then_inc(s["const_in"], 16)
            for dst, src in ((wk, "Wk"), (wq, "Wq"), (wv, "Wv"), (wo, "Wo"), (av, "v_w"), (ao, "o_w")):
                sp.dma_start(dst[:], a[src].rearrange("(c p) n -> p c n", c=C)).then_inc(s["weights_in"], 16)
            sp.dma_start(aqk[:, :, 0:D], a["q_w"].rearrange("(c p) n -> p c n", c=C)).then_inc(s["weights_in"], 16)
            sp.dma_start(aqk[:, :, D:2 * D], a["k_w"].rearrange("(c p) n -> p c n", c=C)).then_inc(s["weights_in"], 16)
            sp.dma_start(gw[:], a["gate_w"].rearrange("(c p) n -> p c n", c=C)).then_inc(s["weights_in"], 16)
            for dst, src in ((b_q, "bq"), (b_k, "bk"), (b_v, "bv"), (qn, "qn"), (kn, "kn")):
                sp.dma_start(dst[:, :], a[src].rearrange("(c p) -> p c", c=C),
                             allow_slow_non_contiguous=True).then_inc(s["weights_in"], 16)
            for dst, src in ((r_o[:, :], "bo"), (r_v2[:, :], "v_b"), (r_o2[:, :], "o_b"),
                             (r_qk[:, 0:D], "q_b"), (r_qk[:, D:2 * D], "k_b"), (r_g[:, :], "gate_b")):
                sp.dma_start(dst, a[src].partition_broadcast(P)).then_inc(s["weights_in"], 16)
            sp.dma_start(lastT[:], a["lastT"].rearrange("(c p) b -> p c b", c=C)).then_inc(s["weights_in"], 16)

            def load_ctx(t, r):
                sp.wait_ge(s["ctx_parts"], floor0(TB * t + 2 * r - 2))
                b = TB * t + 2 * r
                for c in range(C):
                    sp.dma_start(ctxT[:, r, c], a["ctxT"][c * P:(c + 1) * P, bass.ds(b, 2), :]).then_inc(ctx_in[r], 16)

            def load_x(dst, t, done):
                sp.dma_start(dst[:, :], a["x"][bass.ds(P * t, P), :]).then_inc(s[done], 16)

            def send_diag(src, dst, done):
                for h in range(HH):
                    sp.dma_start(dst(h), src(h)).then_inc(s[done], 16)

            def send_queries(t):
                sp.wait_ge(s["qT_done"], t + 1)
                settle(sp)
                sp.wait_ge(s["qbd_parts"], floor0(TB * t))
                settle(sp)
                send_diag(lambda h: qT[HD * h:HD * (h + 1), :, :].rearrange("p c (j q) -> p c j q", j=TB),
                          lambda h: qbd[HD * h:HD * (h + 1), :, :, h, :], "qbd_in")

            load_x(xq, 0, "xq_in")
            load_ctx(0, 0)
            load_ctx(0, 1)
            load_x(xr, 0, "xr_in")
            sp.wait_ge(s["zeroed"], 4)
            send_queries(0)

            def body(i):
                q, xa, s1, s2 = stages(i)
                if q:
                    sp.wait_ge(s["xn_done"], i + 1)
                    load_x(xq, i + 1, "xq_in")
                    load_ctx(i + 1, 0)
                if s1 and xa:
                    sp.wait_ge(s["x1_done"], i)
                    load_x(xr, i, "xr_in")
                if q:
                    load_ctx(i + 1, 1)
                if q:
                    send_queries(i + 1)
                if s1:
                    sp.wait_ge(s["qkT_done"], i)
                    send_diag(lambda h: qkT[HD * h:HD * (h + 1), 0:C, :],
                              lambda h: qbd2[HD * h:HD * (h + 1), :, h, :], "qbd2_in")
                if s2:
                    sp.wait_ge(s["x2_done"], i - 1)
                    sp.dma_start(out[bass.ds(P * (i - 2), P), :], row[:, D:2 * D]).then_inc(s["x2_out"], 16)

            tiles(loop=sp.Fori, body=body)

            sp.wait_ge(s["sent"], 16 * T)

            def load_rows(e, r):
                sp.dma_start(ra[:, r, :], slots[bass.ds(CAP * e, P), :]).then_inc(s[f"ra_in{r}"], 16)
                sp.dma_start(rb[:, r, :], slots[bass.ds(CAP * e + P, CR), :]).then_inc(s[f"ra_in{r}"], 16)

            def load_expert(e, r):
                sp.dma_start(w1[:, r], a["w1"][bass.ds(e, 1), :, :].rearrange("a (c p) f -> p (a c) f", c=C)
                             ).then_inc(s[f"w1_in{r}"], 16)
                sp.dma_start(w2[:, r], a["w2"][bass.ds(e, 1), :, :].rearrange("a (t p) d -> p (a t) d", t=FT)
                             ).then_inc(s[f"w1_in{r}"], 16)

            for r in range(2):
                load_rows(r, r)
            with sp.Fori(0, E // 2 - 1) as i:
                for r in range(2):
                    sp.wait_ge(s["et_ps"], 2 * i + r + 1)
                    settle(sp)
                    load_expert(2 * i + r + 2, r)
                    sp.wait_ge(s[f"fin_out{r}"], 32 * i + 32)
                    load_rows(2 * i + r + 2, r)
            for r in range(2):
                sp.wait_ge(s[f"fin_out{r}"], 32 * (E // 2))
            sp.wait_ge(s["x2_out"], 16 * T)

        @block.tensor
        def _(pe):
            mm = nc.tensor.matmul
            pe.wait_ge(s["weights_in"], 16 * 21)
            pe.wait_ge(s["const_in"], 16)
            for w, o in ((wk, 0), (wv, C * P)):
                for c in range(C):
                    for n in range(C):
                        last = mm(shared[:, o + c * P:o + (c + 1) * P], w[:, n, c * P:(c + 1) * P], lastT[:, n, :],
                                  start=n == 0, stop=n == C - 1)
            last.then_inc(s["last_ps"], 1)

            def transpose_queries(t):
                pe.wait_ge(s["xn_done"], t + 1)
                for c in range(C):
                    last = nc.tensor.transpose(sh_c[:, c], xn[:, c * P:(c + 1) * P], k["ident"])
                last.then_inc(s["qt_ps"], 1)

            def project_queries(t):
                pe.wait_ge(s["xnT_done"], t + 1)
                for c in range(C):
                    for n in range(C):
                        last = mm(sh_c[:, c], wq[:, n, c * P:(c + 1) * P], xnT[:, n, :], start=n == 0, stop=n == C - 1)
                last.then_inc(s["q_ps"], 1)

            def keys(t, j):
                b, g = TB * t + j, j % 2
                pe.wait_ge(s["ctx_parts"], b + 1)
                pe.wait_ge(s["k_lo"], b)
                for c in range(C):
                    for n in range(C):
                        for x, y in PASSES:
                            last = mm(kps[:, c, :], wk_p[:, x, n, c * P:(c + 1) * P], ctx_p[:, g, y, n, :],
                                      start=(n, x) == (0, LO), stop=(n, y) == (C - 1, LO))
                last.then_inc(s["k_done"], 1)

            def values(t, j):
                b, g = TB * t + j, j % 2
                pe.wait_ge(s["v_evac"], b)
                for c in range(C):
                    for n in range(C):
                        for x, y in PASSES:
                            last = mm(vps[:, c, :], ctx_p[:, g, x, n, c * P:(c + 1) * P], wv_p[:, y, n, :],
                                      start=(n, x) == (0, LO), stop=(n, y) == (C - 1, LO))
                last.then_inc(s["v_done"], 1)

            def scores(t, j):
                b = TB * t + j
                pe.wait_ge(s["qbd_parts"], b + 1)
                pe.wait_ge(s["klast_cp"], b + 1)
                pe.wait_ge(s["k_lo"], b + 1)
                for m in range(MT):
                    c, g = m // 2, m % 2
                    for x, y in PASSES:
                        last = mm(score[:, m, 0:SE], qbd_p[:, b_slot(j), x, c, g * P:(g + 1) * P],
                                  kT[:, b_slot(j), y, c, :], start=x == LO, stop=y == LO)
                    if g:
                        last.then_inc(s["s_done"], 1)

            def b_slot(j):
                return j % 2

            def transpose_probs(t, j):
                b = TB * t + j
                for c in range(C):
                    pe.wait_ge(s["norm_done"], 2 * b + c + 1)
                    for g in range(2):
                        for n in range(2):
                            at = n * HH * L + g * P
                            last = nc.tensor.transpose(score[:, 2 * c, at:at + P], prob[:, 2 * c + g, n * P:(n + 1) * P],
                                                       k["ident"])
                    last.then_inc(s["pt_done"], 1)

            def weighted_values(t, j):
                b = TB * t + j
                pe.wait_ge(s["v_evac"], b + 1)
                if j == 0:
                    pe.wait_ge(s["ext_step"], floor0(2 * t))
                for c in range(C):
                    pe.wait_ge(s["ptb_evac" if c else "pta_evac"], b + 1)
                    for g in range(4):
                        for n in range(2):
                            last = mm(gather[32 * g:32 * g + 32, c, :, j * L:(j + 1) * L],
                                      vv[:, b_slot(j), n, c * P + 32 * g:c * P + 32 * g + 32],
                                      probT[:, c, n, 2 * L * g:2 * L * (g + 1)].rearrange("p (h q) -> p h q", h=2),
                                      start=n == 0, stop=n == 1)
                last.then_inc(s["pv_done"], 1)

            def last_probs(t):
                pe.wait_ge(s["plast_done"], TB * (t + 1))
                for c in range(C):
                    for g in range(2):
                        last = mm(sh_c[:, c], k["spread"][:, g * P:(g + 1) * P],
                                  plast[:, 2 * c + g, :, :].rearrange("p j q -> p (j q)"), start=g == 0, stop=g == 1)
                last.then_inc(s["ll_ps"], 1)

            def project_out(x, w, ready, t, done):
                pe.wait_ge(s[ready], t + 1)
                for c in range(C):
                    last = mm(shared[:, 0:D], x[:, c, :], w[:, c, :], start=c == 0, stop=c == C - 1)
                last.then_inc(s[done], 1)

            def transpose_rows(x, ready, t, done):
                pe.wait_ge(s[ready], t + 1)
                for c in range(C):
                    last = nc.tensor.transpose(sh_c[:, c], x[:, c * P:(c + 1) * P], k["ident"])
                last.then_inc(s[done], 1)

            def project_qk(t):
                pe.wait_ge(s["y1T_parts"], t + 1)
                for c in range(C):
                    for x, y in PASSES:
                        last = mm(shared[:, :], y1T_p[:, x, c, :], aqk_p[:, y, c, :],
                                  start=(c, x) == (0, LO), stop=(c, y) == (C - 1, LO))
                last.then_inc(s["qk_ps"], 1)

            def project_v2(t):
                pe.wait_ge(s["y1T_parts"], t + 1)
                for c in range(C):
                    for x, y in PASSES:
                        last = mm(shared[:, 0:D], y1T_p[:, x, c, :], av_p[:, y, c, :],
                                  start=(c, x) == (0, LO), stop=(c, y) == (C - 1, LO))
                last.then_inc(s["v2_ps"], 1)

            def transpose_qk(t):
                pe.wait_ge(s["rope_done"], t + 1)
                for c in range(2 * C):
                    last = nc.tensor.transpose(shared[:, c * P:(c + 1) * P], qk[:, c * P:(c + 1) * P], k["ident"])
                last.then_inc(s["qkt_ps"], 1)

            def scores2(t):
                pe.wait_ge(s["qbd2_in"], 16 * HH * (t + 1))
                for c in range(C):
                    for j in range(TB):
                        last = mm(shared[32 * j:32 * j + 32, c * D:(c + 1) * D], qkT[:, C + c, 32 * j:32 * j + 32],
                                  qbd2[:, c, :, 32 * j:32 * j + 32], start=True, stop=True)
                last.then_inc(s["s2_ps"], 1)

            def weight_sums(t):
                pe.wait_ge(s["sig_done"], TB * (t + 1))
                for c in range(C):
                    for g in range(4):
                        last = mm(shared[32 * g:32 * g + 32, c * D:(c + 1) * D], k["ones"][:, 0:32],
                                  wbd[:, 8 * c + 2 * g:8 * c + 2 * g + 2, :].rearrange("p h n -> p (h n)"),
                                  start=True, stop=True)
                last.then_inc(s["sm_ps"], 1)

            def weighted_values2(t):
                pe.wait_ge(s["v2_done"], t + 1)
                for c in range(C):
                    for g in range(4):
                        last = mm(shared[32 * g:32 * g + 32, c * D:(c + 1) * D], v2[:, c * P + 32 * g:c * P + 32 * g + 32],
                                  wbd[:, 8 * c + 2 * g:8 * c + 2 * g + 2, :].rearrange("p h n -> p (h n)"),
                                  start=True, stop=True)
                last.then_inc(s["pv2_ps"], 1)

            def gate(t):
                pe.wait_ge(s["y2T_done"], t + 1)
                for c in range(C):
                    last = mm(shared[:, 0:E], y2T[:, c, :], gw[:, c, :], start=c == 0, stop=c == C - 1)
                last.then_inc(s["g_ps"], 1)

            def positions(t):
                pe.wait_ge(s["oh_done"], t + 1)
                pe.wait_ge(s["seen_done"], t + 1)
                pe.wait_ge(s["bf_consts"], 2)
                mm(shared[:, 0:E], tri_bf[:, :], oh[:, :], start=True, stop=False)
                mm(shared[:, 0:E], ones_bf[:, :], seen[:, :], start=False, stop=True).then_inc(s["cum_ps"], 1)

            reader = ["vlast_done", 1]

            def turn(sem_name, count):
                pe.wait_ge(s[reader[0]], reader[1])
                reader[:] = sem_name, count

            turn("xnT_done", 1)
            transpose_queries(0)
            turn("qT_done", 1)
            project_queries(0)
            pe.wait_ge(s["wparts_done"], 5)
            keys(0, 0)
            values(0, 0)

            def body(i):
                q, xa, s1, s2 = stages(i)
                t1, t2 = i - 1, i - 2
                if not isinstance(i, int):
                    reader[:] = "cum_read", i - 2
                between = {
                    (0, 0): s1 and (lambda: (turn("att_tmp", t1 + 1), last_probs(t1))),
                    (0, 1): s2 and (lambda: (turn("relu_done", t2 + 1), scores2(t2))),
                    (0, 2): s1 and (lambda: (turn("x1_step", 3 * t1 + 1), project_out(att, wo, "att_done", t1, "o1_ps"))),
                    (0, 3): q and (lambda: (turn("xnT_done", i + 2), transpose_queries(i + 1))),
                    (1, 0): q and (lambda: (turn("qT_done", i + 2), project_queries(i + 1))),
                    (1, 1): s1 and (lambda: (turn("y1T_done", t1 + 1), transpose_rows(y1, "y1_done", t1, "y1t_ps"))),
                    (1, 2): s2 and (lambda: (turn("sm_step", 2 * (t2 + 1)), weight_sums(t2))),
                    (1, 3): s2 and (lambda: (turn("ext2_step", 2 * (t2 + 1)), weighted_values2(t2))),
                    (2, 0): s1 and (lambda: (turn("qk_done", t1 + 1), project_qk(t1))),
                    (2, 2): s2 and (lambda: (turn("x2_step", 3 * t2 + 1), project_out(att2, ao, "att2_done", t2, "o2_ps"))),
                    (2, 3): s1 and (lambda: (turn("qkT_done", t1 + 1), transpose_qk(t1))),
                    (3, 0): s2 and (lambda: (turn("y2T_done", t2 + 1), transpose_rows(row, "y2_done", t2, "y2t_ps"))),
                    (3, 1): s2 and (lambda: (turn("logit_done", t2 + 1), gate(t2))),
                    (3, 2): s1 and (lambda: (turn("v2_done", t1 + 1), project_v2(t1))),
                    (3, 3): s2 and (lambda: (turn("cum_read", t2 + 1), positions(t2))),
                }

                def short(j, place):
                    if between.get((j, place)):
                        between[j, place]()

                for j in range(TB):
                    ahead = xa and (j < TB - 1 or q)
                    ta, ja = (i, j + 1) if j < TB - 1 else (i + 1, 0)
                    if xa:
                        scores(i, j)
                    short(j, 0)
                    if ahead:
                        keys(ta, ja)
                    short(j, 1)
                    if ahead:
                        values(ta, ja)
                    short(j, 2)
                    if xa:
                        transpose_probs(i, j)
                    short(j, 3)
                    if xa:
                        weighted_values(i, j)

            tiles(loop=pe.Fori, body=body)

            hps = [score[:, m, 0:3 * CAP].rearrange("p (f n) -> p f n", f=3) for m in range(3)]
            dps = shared[:, 0:C * CAP].rearrange("p (c n) -> p c n", c=C)
            ops_ = score[:, 3, 0:C * CAP].rearrange("p (c n) -> p c n", c=C)
            turn("dt_evac", 0)

            def expert(i, r):
                e = 2 * i + r
                pe.wait_ge(s[f"ra_in{r}"], 32 * (i + 1))
                pe.wait_ge(s["dt_evac"], e)
                for c in range(C):
                    nc.tensor.transpose(dps[:, c, 0:P], ra[:, r, c * P:(c + 1) * P], k["ident"])
                    last = nc.tensor.transpose(dps[:, c, P:CAP], rb[:, r, c * P:(c + 1) * P],
                                               k["ident"][0:CR, 0:CR])
                last.then_inc(s["dt_ps"], 1)
                pe.wait_ge(s["dt_evac"], e + 1)
                pe.wait_ge(s[f"w1_in{r}"], 32 * (i + 1))
                for f in range(FT):
                    if f % 3 == 0:
                        pe.wait_ge(s["hid_done"], floor0(FT * (e - 1) + min(f + 3, FT)))
                    for c in range(C):
                        last = mm(hps[f // 3][:, f % 3, :], w1[:, r, c, f * P:(f + 1) * P], disp[:, c, :],
                                  start=c == 0, stop=c == C - 1)
                    if f % 3 == 2 or f == FT - 1:
                        last.then_inc(s["h_ps"], 1)
                pe.wait_ge(s["eo_done"], e)
                for c in range(C):
                    for f in range(FT):
                        if c == 0:
                            pe.wait_ge(s["hid_done"], FT * e + f + 1)
                        last = mm(ops_[:, c, :], w2[:, r, f, c * P:(c + 1) * P], hid[:, f, :],
                                  start=f == 0, stop=f == FT - 1)
                last.then_inc(s["eo_ps"], 1)
                last = None
                pe.wait_ge(s["eo_done"], e + 1)
                pe.wait_ge(s["fin_done"], e)
                for c in range(C):
                    nc.tensor.transpose(kps[:, 0, c * P:(c + 1) * P], eo[:, c, 0:P], k["ident"])
                    last = nc.tensor.transpose(vps[0:CR, 0, c * P:(c + 1) * P], eo[:, c, P:CAP], k["ident"])
                last.then_inc(s["et_ps"], 1)

            expert(0, 0)
            expert(0, 1)
            with pe.Fori(1, E // 2) as i:
                expert(i, 0)
                expert(i, 1)

        @block.scalar
        def _(act):
            af = nc.scalar.activation

            for r in range(2):
                act.dma_start(w1[:, r], a["w1"][r, :, :].rearrange("(c p) f -> p c f", c=C)).then_inc(s[f"w1_in{r}"], 16)
                act.dma_start(w2[:, r], a["w2"][r, :, :].rearrange("(t p) d -> p t d", t=FT)).then_inc(s[f"w1_in{r}"], 16)
            act.dma_start(b1[:], a["b1"].rearrange("e (t p) -> p e t", t=FT),
                          allow_slow_non_contiguous=True).then_inc(s["ffb_in"], 16)
            act.dma_start(b2[:], a["b2"].rearrange("e (c p) -> p e c", c=C),
                          allow_slow_non_contiguous=True).then_inc(s["ffb_in"], 16)
            act.wait_ge(s["weights_in"], 16 * 21)
            act.wait_ge(s["last_ps"], 1)
            for c in range(C):
                last = af(klast[:, c, :], shared[:, c * P:(c + 1) * P], ACT.Identity, bias=b_k[:, c:c + 1], scale=1.0)
            last.then_inc(s["klast_done"], 1)

            def copy_rows(dst, src, ready, t, done):
                act.wait_ge(s[ready], t + 1)
                af(dst, src, ACT.Copy).then_inc(s[done], 1)

            def exps(t, j):
                b = TB * t + j
                act.wait_ge(s["plast_done"], b)
                for c in range(C):
                    act.wait_ge(s["max_done"], 2 * b + c + 1)
                    for g in range(2):
                        m = 2 * c + g
                        last = af(prob[:, m, :], score[:, m, 0:S], ACT.Exp, bias=nmx[:, m:m + 1], scale=1.0,
                                  accum_out=esum[:, m:m + 1])
                    last.then_inc(s["exp_done"], 1)

            def keys(t, j):
                b = TB * t + j
                act.wait_ge(s["k_done"], b + 1)
                act.wait_ge(s["s_done"], floor0(2 * (b - 1)))
                for c in range(C):
                    last = af(kT[:, j % 2, HI, c, 0:SM], kps[:, c, :], ACT.Identity, bias=b_k[:, c:c + 1], scale=1.0)
                last.then_inc(s["k_evac"], 1)

            def context_hi(t, j):
                b, r, g = TB * t + j, j // 2, j % 2
                act.wait_ge(ctx_in[r], 16 * C * (t + 1))
                act.wait_ge(s["v_done"], floor0(b - 1))
                af(ctx_p[:, g, HI, :, :], ctxT[:, r, :, g, 0:SM], ACT.Copy).then_inc(s["ctx_hi"], 1)

            def queries_hi(t, j):
                b = TB * t + j
                if j == 0:
                    act.wait_ge(s["qbd_in"], 16 * HH * (t + 1))
                act.wait_ge(s["s_done"], floor0(2 * (b - 1)))
                af(qbd_p[:, j % 2, HI, :, :], qbd[:, :, j, :, :].rearrange("p c h q -> p c (h q)"), ACT.Copy
                   ).then_inc(s["qbd_hi"], 1)

            def values(t, j):
                b = TB * t + j
                act.wait_ge(s["v_done"], b + 1)
                act.wait_ge(s["pv_done"], floor0(b - 1))
                af(vv[:, j % 2], vps[:, :, :], ACT.Copy).then_inc(s["v_evac"], 1)

            def probsT(t, j):
                b = TB * t + j
                act.wait_ge(s["pt_done"], 2 * b + 2)
                af(probT[:, 1, :, :].rearrange("p n x -> p (n x)"), score[:, 2, :], ACT.Copy).then_inc(s["ptb_evac"], 1)

            def squares(t):
                act.wait_ge(s["y1_done"], t + 1)
                act.wait_ge(s["rms_step"], t)
                af(sq[:, :], y1[:, :], ACT.Square, scale=float(1 / np.sqrt(D)), accum_out=msq[:, 0:1]).then_inc(s["sq_done"], 1)

            def sigmoid_tanh(t):
                act.wait_ge(s["s2_ps"], t + 1)
                act.wait_ge(s["sig_done"], TB * t)
                af(th[:, :], shared[:, :], ACT.Tanh, scale=float(SCALE / 2)).then_inc(s["th_done"], 1)
                af(sneg[:, :], shared[:, :], ACT.Relu, scale=-1.0).then_inc(s["relu_done"], 1)

            def sigmoid_exp(t):
                act.wait_ge(s["th_done"], t + 1)
                act.wait_ge(s["relu_done"], t + 1)
                af(tabs[:, :], th[:, :], ACT.Abs)
                af(sneg[:, :], sneg[:, :], ACT.Exp, scale=float(-SCALE)).then_inc(s["sneg_exp"], 1)

            def gate_exp(t):
                act.wait_ge(s["logit_done"], t + 1)
                act.wait_ge(s["route_step"], floor0(5 * t))
                af(ex[:, :], logit[:, :], ACT.Exp, bias=nlm[:, 0:1], scale=1.0, accum_out=se[:, 0:1]).then_inc(s["ex_done"], 1)

            for part, full in ((wk_p, wk), (wv_p, wv)):
                af(part[:, HI], full[:, :, :], ACT.Copy).then_inc(s["wparts_hi"], 1)
            context_hi(0, 0)
            copy_rows(xnT[:, :, :], sh_c, "qt_ps", 0, "xnT_done")
            af(klast_p[:, HI], klast[:, :, :], ACT.Copy).then_inc(s["klast_hi"], 1)
            context_hi(0, 1)
            act.wait_ge(s["scaled"], 2 * C)
            for c in range(C):
                af(aqk_p[:, HI, c], aqk[:, c, :], ACT.Copy).then_inc(s["wparts_hi"], 1)
            af(av_p[:, HI], av[:, :, :], ACT.Copy).then_inc(s["wparts_hi"], 1)
            queries_hi(0, 0)
            keys(0, 0)
            values(0, 0)

            def body(i):
                q, xa, s1, s2 = stages(i)
                t1, t2 = i - 1, i - 2
                for j in range(TB):
                    ahead = xa and (j < TB - 1 or q)
                    ta, ja = (i, j + 1) if j < TB - 1 else (i + 1, 0)
                    if j == 3 and s2:
                        copy_rows(y2T[:, :, :], sh_c, "y2t_ps", t2, "y2T_done")
                    if xa:
                        exps(i, j)
                    if ahead:
                        keys(ta, ja)
                    if j == 0 and s2:
                        sigmoid_tanh(t2)
                    if j == 1 and s1:
                        squares(t1)
                        copy_rows(y1T[:, :, :], sh_c, "y1t_ps", t1, "y1T_done")
                    if ahead and j < 3:
                        queries_hi(ta, ja)
                    if j == 3 and s2:
                        gate_exp(t2)
                    if ahead:
                        values(ta, ja)
                    if ahead and j == 3:
                        queries_hi(ta, ja)
                    if xa and (j < 2 or q):
                        context_hi(*((i, j + 2) if j < 2 else (i + 1, j - 2)))
                    if j == 0 and s2:
                        sigmoid_exp(t2)
                    if xa:
                        probsT(i, j)
                    if j == 0 and q:
                        copy_rows(xnT[:, :, :], sh_c, "qt_ps", i + 1, "xnT_done")
                    if j == 2 and s1:
                        act.wait_ge(s["qbd2_in"], 16 * HH * t1)
                        copy_rows(qkT[:, :, :].rearrange("p c n -> p (c n)"), shared[:, :], "qkt_ps", t1, "qkT_done")

            tiles(loop=act.Fori, body=body)

            hps = [score[:, m, 0:3 * CAP].rearrange("p (f n) -> p f n", f=3) for m in range(3)]
            act.wait_ge(s["ffb_in"], 32)

            def hidden(e):
                act.wait_ge(s["eo_ps"], e)
                for f in range(FT):
                    if f % 3 == 0:
                        act.wait_ge(s["h_ps"], 3 * e + f // 3 + 1)
                    af(hid[:, f, :], hps[f // 3][:, f % 3, :], ACT.Gelu_apprx_tanh,
                       bias=b1[:, bass.ds(e, 1), f:f + 1].rearrange("p a b -> p (a b)"), scale=1.0).then_inc(s["hid_done"], 1)

            hidden(0)
            with act.Fori(1, E) as e:
                hidden(e)

        @block.vector
        def _(dve):
            v = nc.vector
            v.memset(qbd[:], 0.0).then_inc(s["zeroed"], 1)
            v.memset(kT[:, :, :, :, SM:SE].bitcast(F32), 0.0).then_inc(s["zeroed"], 1)
            v.memset(qbd2[:], 0.0).then_inc(s["zeroed"], 1)
            v.memset(wbd[:], 0.0).then_inc(s["zeroed"], 1)
            v.memset(seen[:, :], 0.0).then_inc(s["seen_done"], 1)
            v.memset(row[:, :], 0.0).then_inc(s["slots_init"], 1)
            dve.wait_ge(s["const_in"], 16)
            v.tensor_copy(tri_bf[:, :], k["tri"]).then_inc(s["bf_consts"], 1)
            v.tensor_copy(ones_bf[:, :], k["ones"]).then_inc(s["bf_consts"], 1)
            dve.wait_ge(s["slots_init"], 1)
            v.tensor_copy(row[:, 2 * D + 1:ROW], k["sentinel"]).then_inc(s["slots_init"], 1)
            dve.wait_ge(s["weights_in"], 16 * 21)
            for c in range(C):
                v.tensor_scalar(aqk[:, c, 0:D], aqk[:, c, 0:D], qn[:, c:c + 1], None, ALU.mult).then_inc(s["scaled"], 1)
                v.tensor_scalar(aqk[:, c, D:2 * D], aqk[:, c, D:2 * D], kn[:, c:c + 1], None, ALU.mult).then_inc(s["scaled"], 1)
            dve.wait_ge(s["klast_done"], 1)
            v.tensor_copy(vlast[:, :, :, :].rearrange("p t c j -> p c t j"),
                          shared[:, C * P:2 * C * P].rearrange("p (c t j) -> p c t j", c=C, j=TB)).then_inc(s["vlast_done"], 1)

            def norm_stats(x, n, step, base):
                v.bn_stats(stat[n][:, :], x).then_inc(s[step], 1)
                dve.wait_ge(s[step], base + 1)
                settle(dve)
                v.bn_aggr(mv[n][:, :], stat[n][:, :]).then_inc(s[step], 1)
                dve.wait_ge(s[step], base + 2)

            def norm_x(t):
                dve.wait_ge(s["xq_in"], 16 * (t + 1))
                norm_stats(xq[:, :], "q", "xn_stat", 3 * t)
                dve.wait_ge(s["xn_pow"], t)
                v.tensor_scalar(ve["q"][:, :], mv["q"][:, 1:2], 1e-5, None, ALU.add).then_inc(s["xn_stat"], 1)

            def norm_x_apply(t):
                dve.wait_ge(s["xn_pow"], t + 1)
                dve.wait_ge(s["qt_ps"], t)
                v.tensor_scalar(xn[:, :], xq[:, :], mv["q"][:, 0:1], rstd["q"][:, 0:1], ALU.subtract, ALU.mult
                                ).then_inc(s["xn_done"], 1)

            def weight_lo(part, full, count):
                dve.wait_ge(s["wparts_hi"], count)
                v.tensor_tensor(part[:, LO], full[:], part[:, HI].bitcast(F32), ALU.subtract).then_inc(s["wparts_done"], 1)

            def keys_lo(t, j):
                b = TB * t + j
                dve.wait_ge(s["k_evac"], b + 1)
                for c in range(C):
                    last = v.scalar_tensor_tensor(kT[:, j % 2, LO, c, 0:SM], kps[:, c, :], b_k[:, c:c + 1],
                                                  kT[:, j % 2, HI, c, 0:SM].bitcast(F32), ALU.add, ALU.subtract)
                last.then_inc(s["k_lo"], 1)

            def queries(t):
                dve.wait_ge(s["q_ps"], t + 1)
                dve.wait_ge(s["qbd_in"], 16 * HH * t)
                for c in range(C):
                    last = v.tensor_scalar(qT[:, c, :], sh_c[:, c], b_q[:, c:c + 1], None, ALU.add)
                last.then_inc(s["qT_done"], 1)

            def maxima(t, j):
                b = TB * t + j
                for c in range(C):
                    dve.wait_ge(s["s_done"], 2 * b + c + 1)
                    v.tensor_reduce(nmx[:, 2 * c:2 * c + 2], score[:, 2 * c:2 * c + 2, 0:S], AX.X, ALU.max, negate=True
                                    ).then_inc(s["max_done"], 1)

            def normalise(t, j):
                b = TB * t + j
                for c in range(C):
                    dve.wait_ge(s["exp_done"], 2 * b + c + 1)
                    v.reciprocal(rsum[:, 2 * c:2 * c + 2], esum[:, 2 * c:2 * c + 2]).then_inc(s["rsum_done"], 1)
                    dve.wait_ge(s["rsum_done"], 2 * b + c + 1)
                    for g in range(2):
                        m = 2 * c + g
                        last = v.tensor_scalar(prob[:, m, :], prob[:, m, :], rsum[:, m:m + 1], None, ALU.mult)
                    last.then_inc(s["norm_done"], 1)

            def probsT(t, j):
                b = TB * t + j
                dve.wait_ge(s["pt_done"], 2 * b + 1)
                v.tensor_copy(probT[:, 0, :, :].rearrange("p n x -> p (n x)"), score[:, 0, :]).then_inc(s["pta_evac"], 1)

            def extract(t):
                dve.wait_ge(s["pv_done"], TB * (t + 1))
                v.tensor_scalar(att[:, :, :], gather[:, :, 0, :], k["even"], None, ALU.mult).then_inc(s["ext_step"], 1)
                dve.wait_ge(s["ext_step"], 2 * t + 1)
                v.scalar_tensor_tensor(att[:, :, :], gather[:, :, 1, :], k["odd"], att[:, :, :], ALU.mult, ALU.add
                                       ).then_inc(s["ext_step"], 1)
            def attended(t):
                dve.wait_ge(s["att_tmp"], t + 1)
                dve.wait_ge(s["ext_step"], 2 * t + 2)
                for c in range(C):
                    last = v.scalar_tensor_tensor(att[:, c, :], alast[:, c, :], b_v[:, c:c + 1], att[:, c, :],
                                                  ALU.add, ALU.add)
                last.then_inc(s["att_done"], 1)

            def last_values(t):
                dve.wait_ge(s["ll_ps"], t + 1)
                v.tensor_tensor(alast[:, :, :].rearrange("p c (j q) -> p (c j) q", j=TB),
                                shared[:, 0:C * P].rearrange("p (x q) -> p x q", q=L),
                                vlast[:, bass.ds(t, 1), :, :].rearrange("p a c j -> p (a c j)").unsqueeze(2)
                                .to_broadcast([P, C * TB, L]), ALU.mult).then_inc(s["att_tmp"], 1)

            def residual1(t):
                dve.wait_ge(s["o1_ps"], t + 1)
                dve.wait_ge(s["xrb_done"], t + 1)
                dve.wait_ge(s["x1b_done"], t)
                v.tensor_tensor(x1[:, :], shared[:, 0:D], xr[:, :], ALU.add).then_inc(s["x1_step"], 1)

            def residual1_stats(t):
                dve.wait_ge(s["x1_step"], 3 * t + 1)
                v.bn_stats(stat["1"][:, :], x1[:, :]).then_inc(s["x1_step"], 1)
                dve.wait_ge(s["x1_step"], 3 * t + 2)
                settle(dve)
                v.bn_aggr(mv["1"][:, :], stat["1"][:, :]).then_inc(s["x1_step"], 1)
                dve.wait_ge(s["x1_step"], 3 * t + 3)
                v.tensor_scalar(ve["1"][:, :], mv["1"][:, 1:2], 1e-5, None, ALU.add).then_inc(s["x1_done"], 1)

            def norm1(t):
                dve.wait_ge(s["x1_pow"], t + 1)
                v.tensor_scalar(y1[:, :], x1[:, :], mv["1"][:, 0:1], rstd["1"][:, 0:1], ALU.subtract, ALU.mult
                                ).then_inc(s["y1_done"], 1)

            def evac_qk(t):
                dve.wait_ge(s["qk_ps"], t + 1)
                dve.wait_ge(s["rrms_done"], t + 1)
                v.scalar_tensor_tensor(qk[:, :], shared[:, :], rrms[:, 0:1], r_qk[:, :], ALU.mult, ALU.add
                                       ).then_inc(s["qk_done"], 1)
                dve.wait_ge(s["qk_done"], t + 1)
                v.tensor_tensor(qkc[:, :].rearrange("p (h d) -> p h d", d=HD), qk[:, :].rearrange("p (h d) -> p h d", d=HD),
                                k["cos"].unsqueeze(1).to_broadcast([P, 2 * H, HD]), ALU.mult).then_inc(s["qkc_done"], 1)

            def rope_add(t):
                dve.wait_ge(s["qkc_done"], t + 1)
                dve.wait_ge(s["qks_done"], t + 1)
                v.tensor_tensor(qk[:, :], qkc[:, :], qks[:, :], ALU.add).then_inc(s["rope_done"], 1)

            def evac_v2(t):
                dve.wait_ge(s["v2_ps"], t + 1)
                v.tensor_tensor(v2[:, :], shared[:, 0:D], r_v2[:, :], ALU.add).then_inc(s["v2_done"], 1)

            def sigmoid_blocks(t, batches):
                dve.wait_ge(s["sneg_exp"], t + 1)
                for j in batches:
                    b = slice(32 * j, 32 * j + 32)
                    v.scalar_tensor_tensor(wbd[b, :, b], tabs[b, :].rearrange("p (h q) -> p h q", h=H), 1.0,
                                           sneg[b, :].rearrange("p (h q) -> p h q", h=H), ALU.add, ALU.mult
                                           ).then_inc(s["sig_done"], 1)

            def sums2(t):
                dve.wait_ge(s["sm_ps"], t + 1)
                v.tensor_scalar(ssum[:, :, :], sh_pair[:, :, 0, :], k["even"], 2e-8, ALU.mult, ALU.add).then_inc(s["sm_step"], 1)
                dve.wait_ge(s["sm_step"], 2 * t + 1)
                v.scalar_tensor_tensor(ssum[:, :, :], sh_pair[:, :, 1, :], k["odd"], ssum[:, :, :], ALU.mult, ALU.add
                                       ).then_inc(s["sm_step"], 1)

            def inverse2(t):
                dve.wait_ge(s["sm_step"], 2 * t + 2)
                v.reciprocal(ssum[:, :, :], ssum[:, :, :]).then_inc(s["ssum_done"], 1)

            def extract2(t):
                dve.wait_ge(s["pv2_ps"], t + 1)
                v.tensor_scalar(att2[:, :, :], sh_pair[:, :, 0, :], k["even"], None, ALU.mult).then_inc(s["ext2_step"], 1)
                dve.wait_ge(s["ext2_step"], 2 * t + 1)
                v.scalar_tensor_tensor(att2[:, :, :], sh_pair[:, :, 1, :], k["odd"], att2[:, :, :], ALU.mult, ALU.add
                                       ).then_inc(s["ext2_step"], 1)
                dve.wait_ge(s["ext2_step"], 2 * t + 2)
                dve.wait_ge(s["ssum_done"], t + 1)
                v.tensor_tensor(att2[:, :, :], att2[:, :, :], ssum[:, :, :], ALU.mult).then_inc(s["att2_done"], 1)

            def residual2(t):
                dve.wait_ge(s["o2_ps"], t + 1)
                dve.wait_ge(s["sent"], 16 * t)
                dve.wait_ge(s["x2_out"], 16 * t)
                v.tensor_tensor(row[:, D:2 * D], shared[:, 0:D], x1b[:, :], ALU.add).then_inc(s["x2_step"], 1)

            def residual2_stats(t):
                dve.wait_ge(s["x2_step"], 3 * t + 1)
                v.bn_stats(stat["2"][:, :], row[:, D:2 * D]).then_inc(s["x2_step"], 1)
                dve.wait_ge(s["x2_step"], 3 * t + 2)
                settle(dve)
                v.bn_aggr(mv["2"][:, :], stat["2"][:, :]).then_inc(s["x2_step"], 1)
                dve.wait_ge(s["x2_step"], 3 * t + 3)
                v.tensor_scalar(ve["2"][:, :], mv["2"][:, 1:2], 1e-5, None, ALU.add).then_inc(s["x2_done"], 1)

            def norm2(t):
                dve.wait_ge(s["x2_pow"], t + 1)
                v.tensor_scalar(row[:, 0:D], row[:, D:2 * D], mv["2"][:, 0:1], rstd["2"][:, 0:1], ALU.subtract, ALU.mult
                                ).then_inc(s["y2_done"], 1)

            def logits(t):
                dve.wait_ge(s["g_ps"], t + 1)
                v.tensor_tensor(logit[:, :], shared[:, 0:E], r_g[:, :], ALU.add).then_inc(s["route_step"], 1)
                dve.wait_ge(s["route_step"], 5 * t + 1)
                v.tensor_reduce(nlm[:, :], logit[:, :], AX.X, ALU.max, negate=True).then_inc(s["logit_done"], 1)

            def choose(t):
                dve.wait_ge(s["ex_done"], t + 1)
                v.reciprocal(rse[:, :], se[:, :]).then_inc(s["route_step"], 1)
                dve.wait_ge(s["route_step"], 5 * t + 2)
                v.tensor_scalar(pr[:, :], ex[:, :], rse[:, 0:1], None, ALU.mult).then_inc(s["route_step"], 1)
                dve.wait_ge(s["route_step"], 5 * t + 3)
                v.tensor_reduce(row[:, 2 * D:2 * D + 1], pr[:, :], AX.X, ALU.max).then_inc(s["route_step"], 1)
                dve.wait_ge(s["route_step"], 5 * t + 4)
                v.scalar_tensor_tensor(eqr[:, :], pr[:, :], row[:, 2 * D:2 * D + 1], k["rank"], ALU.is_equal, ALU.mult
                                       ).then_inc(s["route_step"], 1)
                dve.wait_ge(s["route_step"], 5 * t + 5)
                dve.wait_ge(s["slot_done"], t)
                v.tensor_reduce(top[:, :], eqr[:, :], AX.X, ALU.max).then_inc(s["top_done"], 1)
                dve.wait_ge(s["top_done"], t + 1)
                v.tensor_scalar(oh[:, :], eqr[:, :], top[:, 0:1], None, ALU.is_equal).then_inc(s["oh_done"], 1)

            def position(t):
                dve.wait_ge(s["cum_ps"], t + 1)
                dve.wait_ge(s["oh_done"], t + 1)
                v.tensor_tensor(cumoh[:, :], shared[:, 0:E], oh[:, :], ALU.mult).then_inc(s["cum_read"], 1)
                v.tensor_tensor(seen[:, :], seen[:, :], oh[:, :], ALU.add).then_inc(s["seen_done"], 1)
                dve.wait_ge(s["cum_read"], t + 1)
                v.tensor_reduce(pos[:, :], cumoh[:, :], AX.X, ALU.add).then_inc(s["pos_done"], 1)

            norm_x(0)
            weight_lo(wk_p, wk, 1)
            weight_lo(wv_p, wv, 2)
            norm_x_apply(0)
            for c in range(C):
                dve.wait_ge(s["wparts_hi"], 3 + c)
                v.tensor_tensor(aqk_p[:, LO, c], aqk[:, c, :], aqk_p[:, HI, c].bitcast(F32), ALU.subtract
                                ).then_inc(s["wparts_done"], 1)
            queries(0)
            weight_lo(av_p, av, 5)
            keys_lo(0, 0)

            def body(i):
                q, xa, s1, s2 = stages(i)
                t1, t2 = i - 1, i - 2
                for j in range(TB):
                    if j == 0 and s1:
                        extract(t1)
                    if xa:
                        maxima(i, j)
                    if j == 0 and q:
                        norm_x(i + 1)
                    if j == 0 and s1:
                        last_values(t1)
                    if j == 1 and s1:
                        norm1(t1)
                    if j == 1 and q:
                        queries(i + 1)
                    if j == 2 and s1:
                        evac_qk(t1)
                    if xa:
                        normalise(i, j)
                    if j == 0:
                        if s1:
                            attended(t1)
                        if q:
                            norm_x_apply(i + 1)
                    if j == 1 and s2:
                        sigmoid_blocks(t2, (2, 3))
                    if j == 3 and s2:
                        logits(t2)
                        choose(t2)
                    if xa and (j < TB - 1 or q):
                        keys_lo(*((i, j + 1) if j < TB - 1 else (i + 1, 0)))
                    if j == 0 and s1:
                        residual1(t1)
                    if j == 1 and s2:
                        sums2(t2)
                    if j == 2 and s2:
                        residual2(t2)
                    if j == 2 and s1:
                        rope_add(t1)
                    if xa:
                        probsT(i, j)
                    if j == 0 and s1:
                        residual1_stats(t1)
                    if j == 0 and s2:
                        sigmoid_blocks(t2, (0, 1))
                    if j == 1 and s2:
                        inverse2(t2)
                        extract2(t2)
                    if j == 2 and s2:
                        residual2_stats(t2)
                        norm2(t2)
                    if j == 3 and s1:
                        evac_v2(t1)
                    if j == 3 and s2:
                        position(t2)

            tiles(loop=dve.Fori, body=body)

            dps = shared[:, 0:C * CAP]
            ops_ = score[:, 3, 0:C * CAP].rearrange("p (c n) -> p c n", c=C)

            def expert(i, r):
                e = 2 * i + r
                dve.wait_ge(s["dt_ps"], e + 1)
                v.tensor_copy(disp[:, :, :].rearrange("p c n -> p (c n)"), dps).then_inc(s["dt_evac"], 1)
                dve.wait_ge(s["eo_ps"], e + 1)
                for c in range(C):
                    last = v.tensor_scalar(eo[:, c, :], ops_[:, c, :], b2_of(e, c), None, ALU.add)
                last.then_inc(s["eo_done"], 1)
                dve.wait_ge(s["et_ps"], e + 1)
                dve.wait_ge(s[f"fin_out{r}"], 32 * i)
                v.scalar_tensor_tensor(fa[:, r, :], kps[:, 0, :], ra[:, r, 2 * D:2 * D + 1], ra[:, r, D:2 * D],
                                       ALU.mult, ALU.add)
                v.scalar_tensor_tensor(fb[:, r, :], vps[0:CR, 0, :], rb[:, r, 2 * D:2 * D + 1], rb[:, r, D:2 * D],
                                       ALU.mult, ALU.add).then_inc(s["fin_done"], 1)

            def b2_of(e, c):
                return b2[:, bass.ds(e, 1), c:c + 1].rearrange("p a b -> p (a b)")

            dve.wait_ge(s["ffb_in"], 32)
            for r in range(2):
                expert(0, r)
            with dve.Fori(1, E // 2) as i:
                for r in range(2):
                    expert(i, r)

        @block.gpsimd
        def _(pool):
            g = nc.gpsimd

            def power(n, ready, count, t, done):
                pool.wait_ge(s[ready], count)
                g.tensor_tensor(rstd[n][:, :], ve[n][:, :], k["mhalf"], ALU.pow).then_inc(s[done], 1)

            def last_key(t, j):
                b = TB * t + j
                pool.wait_ge(s["s_done"], floor0(2 * (b - 1)))
                g.tensor_copy(kT[:, j % 2, :, :, SM:S], klast_p[:, :, :, bass.ds(b, 1)]).then_inc(s["klast_cp"], 1)

            def context_lo(t, j):
                b, r, g_ = TB * t + j, j // 2, j % 2
                pool.wait_ge(s["ctx_hi"], b + 1)
                g.tensor_tensor(ctx_p[:, g_, LO, :, :], ctxT[:, r, :, g_, 0:SM], ctx_p[:, g_, HI, :, :].bitcast(F32),
                                ALU.subtract).then_inc(s["ctx_parts"], 1)

            def queries_lo(t, j):
                b = TB * t + j
                pool.wait_ge(s["qbd_hi"], b + 1)
                g.tensor_tensor(qbd_p[:, j % 2, LO, :, :], qbd[:, :, j, :, :].rearrange("p c h q -> p c (h q)"),
                                qbd_p[:, j % 2, HI, :, :].bitcast(F32), ALU.subtract).then_inc(s["qbd_parts"], 1)

            def rows_parts(t):
                pool.wait_ge(s["y1T_done"], t + 1)
                pool.wait_ge(s["v2_ps"], t)
                settle(pool)
                g.tensor_copy(y1T_p[:, HI], y1T[:, :, :]).then_inc(s["y1T_hi"], 1)
                pool.wait_ge(s["y1T_hi"], t + 1)
                g.tensor_tensor(y1T_p[:, LO], y1T[:, :, :], y1T_p[:, HI].bitcast(F32), ALU.subtract
                                ).then_inc(s["y1T_parts"], 1)

            def last_prob(t, j):
                b = TB * t + j
                pool.wait_ge(s["norm_done"], 2 * b + 2)
                if j == 0:
                    pool.wait_ge(s["ll_ps"], t)
                g.tensor_tensor(plast[:, :, j, :], k["diag"].unsqueeze(1).to_broadcast([P, MT, L]),
                                prob[:, :, SM:S].to_broadcast([P, MT, L]), ALU.mult).then_inc(s["plast_done"], 1)

            def residual_bias(t):
                pool.wait_ge(s["xr_in"], 16 * (t + 1))
                g.tensor_tensor(xr[:, :], xr[:, :], r_o[:, :], ALU.add).then_inc(s["xrb_done"], 1)

            def rms(t):
                pool.wait_ge(s["sq_done"], t + 1)
                settle(pool)
                g.tensor_scalar(mse[:, :], msq[:, :], 1e-8, None, ALU.add).then_inc(s["rms_step"], 1)
                pool.wait_ge(s["rms_step"], t + 1)
                g.tensor_tensor(rrms[:, :], mse[:, :], k["mhalf"], ALU.pow).then_inc(s["rrms_done"], 1)

            def rope_sin(t):
                pool.wait_ge(s["qk_done"], t + 1)
                for o in range(2):
                    last = g.tensor_tensor(
                        qks[:, :].rearrange("p (h d o) -> p h d o", d=HD // 2, o=2)[:, :, :, o],
                        qk[:, :].rearrange("p (h d o) -> p h d o", d=HD // 2, o=2)[:, :, :, 1 - o],
                        k["sin"].rearrange("p (d o) -> p d o", o=2)[:, :, o].unsqueeze(1).to_broadcast([P, 2 * H, HD // 2]),
                        ALU.mult)
                last.then_inc(s["qks_done"], 1)

            def residual_bias2(t):
                pool.wait_ge(s["y1_done"], t + 1)
                pool.wait_ge(s["x2_step"], floor0(3 * (t - 1) + 1))
                g.tensor_tensor(x1b[:, :], x1[:, :], r_o2[:, :], ALU.add).then_inc(s["x1b_done"], 1)

            def slot_numbers(t):
                pool.wait_ge(s["top_done"], t + 1)
                settle(pool)
                g.tensor_scalar(first[:, :], top[:, :], -float(CAP), float(E * CAP - 1), ALU.mult, ALU.add
                                ).then_inc(s["slot_step"], 1)
                g.tensor_scalar(token[:, :], away[:, :], -float(E * CAP), None, ALU.add).then_inc(s["slot_step"], 1)
                pool.wait_ge(s["slot_step"], 7 * t + 2)
                pool.wait_ge(s["pos_done"], t + 1)
                settle(pool)
                g.tensor_copy(row[:, 2 * D + 1:ROW].bitcast(I32), token[:, :]).then_inc(s["slot_step"], 1)
                g.tensor_tensor(slot[:, :], first[:, :], pos[:, :], ALU.add).then_inc(s["slot_step"], 1)
                pool.wait_ge(s["slot_step"], 7 * t + 4)
                g.tensor_tensor(off[:, :], slot[:, :], away[:, :], ALU.subtract).then_inc(s["slot_step"], 1)
                pool.wait_ge(s["slot_step"], 7 * t + 5)
                settle(pool)
                g.tensor_scalar(kept[:, :], pos[:, :], float(CAP), off[:, 0:1], ALU.is_le, ALU.mult).then_inc(s["slot_step"], 1)
                pool.wait_ge(s["slot_step"], 7 * t + 6)
                g.tensor_tensor(slotf[:, :], kept[:, :], away[:, :], ALU.add).then_inc(s["slot_step"], 1)
                pool.wait_ge(s["slot_step"], 7 * t + 7)
                pool.wait_ge(s["sent"], 16 * t)
                settle(pool)
                g.tensor_copy(sloti[:, :], slotf[:, :]).then_inc(s["slot_done"], 1)
                g.tensor_scalar(away[:, :], away[:, :], float(P), None, ALU.add).then_inc(s["away_done"], 1)
                pool.wait_ge(s["slot_done"], t + 1)
                pool.wait_ge(s["away_done"], t + 2)

            def send(t):
                pool.wait_ge(s["y2_done"], t + 1)
                settle(pool)
                g.indirect_dma_start(out=slots, out_offset=bass.IndirectOffsetOnAxis(sloti[:, 0:1], 0), in_=row[:, :],
                                     in_offset=None, bounds_check=E * CAP - 1, oob_is_err=False).then_inc(s["sent"], 16)

            pool.wait_ge(s["const_in"], 16)
            g.tensor_copy(away[:, :], k["token"]).then_inc(s["away_done"], 1)
            pool.wait_ge(s["slots_init"], 2)
            for n in range(E * CAP // P):
                pool.dma_start(slots[n * P:(n + 1) * P, :], row[:, :]).then_inc(s["slots_zero"], 16)
            power("q", "xn_stat", 3, 0, "xn_pow")
            context_lo(0, 0)
            pool.wait_ge(s["klast_hi"], 1)
            g.tensor_tensor(klast_p[:, LO], klast[:, :, :], klast_p[:, HI].bitcast(F32), ALU.subtract
                            ).then_inc(s["klast_parts"], 1)
            context_lo(0, 1)
            queries_lo(0, 0)
            pool.wait_ge(s["zeroed"], 4)
            pool.wait_ge(s["klast_parts"], 1)
            last_key(0, 0)
            pool.wait_ge(s["slots_zero"], 16 * (E * CAP // P))

            def body(i):
                q, xa, s1, s2 = stages(i)
                t1, t2 = i - 1, i - 2
                for j in range(TB):
                    if xa and (j < TB - 1 or q):
                        last_key(*((i, j + 1) if j < TB - 1 else (i + 1, 0)))
                    if j == 0 and q:
                        power("q", "xn_stat", 3 * (i + 2), i + 1, "xn_pow")
                    if j == 0 and s1:
                        residual_bias(t1)
                    if j == 2 and s1:
                        rope_sin(t1)
                    if xa and j < TB - 1:
                        queries_lo(i, j + 1)
                    if xa:
                        last_prob(i, j)
                    if xa and q and j == TB - 1:
                        queries_lo(i + 1, 0)
                    if xa and (j < 2 or q):
                        context_lo(*((i, j + 2) if j < 2 else (i + 1, j - 2)))
                    if j == 0 and s1:
                        power("1", "x1_done", t1 + 1, t1, "x1_pow")
                    if j == 1 and s1:
                        rms(t1)
                        rows_parts(t1)
                    if j == 2 and s2:
                        power("2", "x2_done", t2 + 1, t2, "x2_pow")
                    if j == 3 and s1:
                        residual_bias2(t1)
                    if j == 3 and s2:
                        slot_numbers(t2)
                        send(t2)

            tiles(loop=pool.Fori, body=body)

            with pool.Fori(0, E // 2) as i:
                for r in range(2):
                    pool.wait_ge(s["fin_done"], 2 * i + r + 1)
                    settle(pool)
                    for rows, res in ((ra, fa), (rb, fb)):
                        g.indirect_dma_start(out=out, out_offset=bass.IndirectOffsetOnAxis(
                                                 rows[:, r, 2 * D + 1:ROW].bitcast(I32), 0),
                                             in_=res[:, r, :], in_offset=None, bounds_check=B * L - 1, oob_is_err=False
                                             ).then_inc(s[f"fin_out{r}"], 16)


def kernel(x, ctx_1024, L0_xattn_Wq, L0_xattn_bq, L0_xattn_Wk, L0_xattn_bk, L0_xattn_Wv, L0_xattn_bv, L0_xattn_Wo,
           L0_xattn_bo, L0_attn_q_w, L0_attn_q_b, L0_attn_k_w, L0_attn_k_b, L0_attn_v_w, L0_attn_v_b, L0_attn_o_w,
           L0_attn_o_b, L0_attn_qn_scale, L0_attn_kn_scale, L0_ffn_gate_w, L0_ffn_gate_b, L0_ffn_w1, L0_ffn_b1,
           L0_ffn_w2, L0_ffn_b2):
    import concourse.bacc as bacc
    from concourse.bass_utils import run_bass_kernel_spmd

    ctxT = np.asarray(ctx_1024).transpose(2, 0, 1)
    arrays = {
        "x": np.asarray(x).reshape(B * L, D), "ctxT": ctxT, "lastT": ctxT[:, :, S - 1], "const": constants(),
        "Wq": np.asarray(L0_xattn_Wq).T, "Wk": np.asarray(L0_xattn_Wk).T, "Wv": np.asarray(L0_xattn_Wv).T,
        "Wo": np.asarray(L0_xattn_Wo).T, "q_w": np.asarray(L0_attn_q_w).T, "k_w": np.asarray(L0_attn_k_w).T,
        "v_w": np.asarray(L0_attn_v_w).T, "o_w": np.asarray(L0_attn_o_w).T,
        "bq": L0_xattn_bq, "bk": L0_xattn_bk, "bv": L0_xattn_bv, "bo": L0_xattn_bo,
        "q_b": L0_attn_q_b, "k_b": L0_attn_k_b, "v_b": L0_attn_v_b, "o_b": L0_attn_o_b,
        "qn": L0_attn_qn_scale, "kn": L0_attn_kn_scale, "gate_w": L0_ffn_gate_w, "gate_b": L0_ffn_gate_b,
        "w1": L0_ffn_w1, "b1": L0_ffn_b1, "w2": L0_ffn_w2, "b2": L0_ffn_b2,
    }
    arrays = {n: np.ascontiguousarray(v) for n, v in arrays.items()}
    nc = bacc.Bacc("TRN2", target_bir_lowering=False, num_devices=1)
    aps = {n: nc.dram_tensor("in_" + n, v.shape, mybir.dt.from_np(v.dtype), kind="ExternalInput").ap()
           for n, v in arrays.items()}
    out = nc.dram_tensor("out", (B * L, D), F32, kind="ExternalOutput").ap()
    build(nc, aps, out)
    r = run_bass_kernel_spmd(nc, [{"in_" + n: v for n, v in arrays.items()}], core_ids=[0])
    return r.results[0]["out"].reshape(B, L, D)
```

```python
from contextlib import ExitStack

import numpy as np
import concourse.bass as bass
from concourse import mybir

F32 = mybir.dt.float32
F32R = mybir.dt.float32r
BF16 = mybir.dt.bfloat16
I32 = mybir.dt.int32
ALU = mybir.AluOpType
ACT = mybir.ActivationFunctionType
AX = mybir.AxisListType

P = 128
B, L, D = 128, 32, 256
S = 257
SE = S + 1
SM = 256
H, HD = 16, 16
C = D // P
TB = P // L
T = B * L // P
HH = H // C
MT = H * L // P
E, CAP, F = 8, 160, 1024
FT = F // P
CR = CAP - P
ROW = 2 * D + 2
SCALE = 1.0 / np.sqrt(HD)

CONST = {}
_at = 0
for _name, _n in (("ident", P), ("tri", P), ("ones", P), ("spread", 2 * P), ("diag", L), ("cos", HD), ("sin", HD),
                  ("even", 1), ("odd", 1), ("rank", E), ("token", 1), ("mhalf", 1), ("sentinel", 1)):
    CONST[_name] = (_at, _at + _n)
    _at += _n
NCONST = _at


def constants():
    t = np.zeros((P, NCONST), np.float32)
    p = np.arange(P)

    def put(name, v):
        t[:, CONST[name][0]:CONST[name][1]] = v

    put("ident", np.eye(P))
    put("tri", p[:, None] <= p[None, :])
    put("ones", 1.0)
    put("spread", np.concatenate([(4 * m + p[:, None] // L) == p[None, :] // HD for m in range(2)], 1))
    put("diag", p[:, None] % L == np.arange(L)[None, :])
    inv_freq = 1.0 / np.float32(10000.0) ** (np.arange(0, HD, 2, dtype=np.float32) / HD)
    angle = (p % L).astype(np.float32)[:, None] * inv_freq[None, :].astype(np.float32)
    angle = np.concatenate([angle, angle], 1)
    put("cos", np.cos(angle))
    put("sin", np.sin(angle) * np.where(np.arange(HD) % 2, 1.0, -1.0))
    put("even", ((p // HD) % 2 == 0)[:, None])
    put("odd", ((p // HD) % 2 == 1)[:, None])
    put("rank", E - np.arange(E)[None, :])
    put("token", (E * CAP + p)[:, None])
    put("mhalf", -0.5)
    put("sentinel", 0.0)
    t[:, CONST["sentinel"][0]] = np.full(P, 1 << 20, np.int32).view(np.float32)
    return t


PASSES = ((1, 0), (0, 0), (0, 1))
HI, LO = 0, 1


def floor0(count):
    return max(count, 0) if isinstance(count, int) else count


def build(nc, a, out):
    ctx = ExitStack()
    with ctx:
        def sb(name, shape, dt=F32):
            return ctx.enter_context(nc.sbuf_tensor(name, shape, dt))

        def ps(name, shape, dt=F32):
            return ctx.enter_context(nc.psum_tensor(name, shape, dt))

        def sem(name):
            return ctx.enter_context(nc.semaphore(name))

        slots = nc.dram_tensor("slots", (E * CAP, ROW), F32, kind="Internal").ap()

        wq, wk, wv, wo, av, ao = (sb(n, [P, C, D]) for n in ("wq", "wk", "wv", "wo", "av", "ao"))
        aqk = sb("aqk", [P, C, 2 * D])
        gw = sb("gw", [P, C, E])
        const = sb("const", [P, NCONST])
        wk_p, wv_p, av_p = (sb(n, [P, 2, C, D], F32R) for n in ("wk_p", "wv_p", "av_p"))
        aqk_p = sb("aqk_p", [P, 2, C, 2 * D], F32R)
        k = {n: const[:, lo:hi] for n, (lo, hi) in CONST.items()}
        tri_bf, ones_bf = sb("tri_bf", [P, P], BF16), sb("ones_bf", [P, P], BF16)
        b_q, b_k, b_v = (sb(n, [P, C]) for n in ("b_q", "b_k", "b_v"))
        qn, kn = sb("qn", [P, C]), sb("kn", [P, C])
        r_o, r_v2, r_o2 = (sb(n, [P, D]) for n in ("r_o", "r_v2", "r_o2"))
        r_qk = sb("r_qk", [P, 2 * D])
        r_g = sb("r_g", [P, E])
        ctxT = sb("ctxT", [P, 2, C, 2, S])
        lastT = sb("lastT", [P, C, B])
        ctx_p = sb("ctx_p", [P, 2, 2, C, SM], F32R)
        klast = sb("klast", [P, C, B])
        klast_p = sb("klast_p", [P, 2, C, B], F32R)
        vlast = sb("vlast", [P, T, C, TB])
        kT = sb("kT", [P, 2, 2, C, SE], F32R)
        vv = sb("vv", [P, 2, C, D])
        xq, xn, xnT, qT = sb("xq", [P, D]), sb("xn", [P, D]), sb("xnT", [P, C, P]), sb("qT", [P, C, P])
        qbd = sb("qbd", [P, C, TB, HH, L])
        qbd_p = sb("qbd_p", [P, 2, 2, C, HH * L], F32R)
        nmx, esum, rsum = sb("nmx", [P, MT]), sb("esum", [P, MT]), sb("rsum", [P, MT])
        prob = sb("prob", [P, MT, S])
        probT = sb("probT", [P, C, 2, HH * L])
        plast = sb("plast", [P, MT, TB, L])
        att, alast = sb("att", [P, C, P]), sb("alast", [P, C, P])
        xr, x1, x1b, y1, sq = (sb(n, [P, D]) for n in ("xr", "x1", "x1b", "y1", "sq"))
        y1T = sb("y1T", [P, C, P])
        y1T_p = sb("y1T_p", [P, 2, C, P], F32R)
        qk, qkc, qks = sb("qk", [P, 2 * D]), sb("qkc", [P, 2 * D]), sb("qks", [P, 2 * D])
        qkT = sb("qkT", [P, 2 * C, P])
        qbd2 = sb("qbd2", [P, C, HH, P])
        v2 = sb("v2", [P, D])
        th, tabs, sneg = (sb(n, [P, 2 * D]) for n in ("th", "tabs", "sneg"))
        wbd = sb("wbd", [P, H, P])
        ssum, att2 = sb("ssum", [P, C, P]), sb("att2", [P, C, P])
        row = sb("row", [P, ROW])
        y2T = sb("y2T", [P, C, P])
        stat = {n: sb("stat_" + n, [P, 6]) for n in "q12"}
        mv = {n: sb("mv_" + n, [P, 2]) for n in "q12"}
        ve = {n: sb("ve_" + n, [P, 1]) for n in "q12"}
        rstd = {n: sb("rstd_" + n, [P, 1]) for n in "q12"}
        msq, mse, rrms = sb("msq", [P, 1]), sb("mse", [P, 1]), sb("rrms", [P, 1])
        logit, nlm, ex, se, rse, pr = (sb(n, [P, w]) for n, w in (("logit", E), ("nlm", 1), ("ex", E), ("se", 1), ("rse", 1), ("pr", E)))
        eqr, top, oh = sb("eqr", [P, E]), sb("top", [P, 1]), sb("oh", [P, E], BF16)
        seen = sb("seen", [P, E], BF16)
        cumoh, pos = sb("cumoh", [P, E]), sb("pos", [P, 1])
        first, slot, off, kept, slotf = (sb(n, [P, 1]) for n in ("first", "slot", "off", "kept", "slotf"))
        away, token = sb("away", [P, 1]), sb("token", [P, 1])
        sloti = sb("sloti", [P, 1], I32)
        w1 = sb("w1", [P, 2, C, F])
        w2 = sb("w2", [P, 2, FT, D])
        b1, b2 = sb("b1", [P, E, FT]), sb("b2", [P, E, C])
        y_a, y_b = sb("y_a", [P, 2, D]), sb("y_b", [CR, 2, D])
        x_a, x_b = sb("x_a", [P, 2, ROW - D]), sb("x_b", [CR, 2, ROW - D])
        gelu_table = sb("gelu_table", [P, 1])
        disp = sb("disp", [P, C, CAP])
        hid = sb("hid", [P, FT, CAP])
        eo = sb("eo", [P, C, CAP])
        fa, fb = sb("fa", [P, 2, D]), sb("fb", [CR, 2, D])

        score = ps("score", [P, MT, 512])
        kps, vps = ps("kps", [P, C, SM]), ps("vps", [P, C, D])
        shared = ps("shared", [P, 512])
        gather = ps("gather", [P, C, 2, P])
        sh_c = shared[:, 0:C * P].rearrange("p (c n) -> p c n", c=C)
        spare = score[:, 1, 0:C * P]
        spare_c = spare.rearrange("p (c n) -> p c n", c=C)
        counts = gather[:, 0, 0, 0:E]
        sh_pair = shared[:, :].rearrange("p (c g n) -> p c g n", c=C, g=2)

        names = """const_in wq_in wkv_in weights_in bf_consts scaled zeroed klast_done vlast_done last_ps xq_in
            xr_in xn_stat xn_pow xn_done qt_ps xnT_done q_ps qT_done qbd_in k_done k_evac klast_cp v_done
            v_evac s_done max_done exp_done rsum_done norm_done plast_done pt_done pta_evac ptb_evac pv_done
            ll_ps ext_step att_done xrb_done o1_ps x1_step x1_done x1_pow y1_done sq_done rms_step rrms_done
            x1b_done y1t_ps y1T_done qk_ps qk_done qkc_done qks_done qks_odd rope_done v2_ps v2_done qkt_ps
            qkT_done qbd2_in s2_ps sig_flat sig_done sm_ps sm_step ssum_done pv2_ps ext2_step att2_done
            o2_ps x2_step x2_done x2_pow y2_done x2_out y2t_ps y2T_done g_ps route_step logit_done ex_done
            oh_done cum_ps cum_read seen_done pos_done slot_step slot_done sent slots_init slots_zero
            away_done top_done att_tmp th_done relu_done tabs_done sneg_exp y_in0 y_in1 x_in0 x_in1 w1_in0
            w1_in1 w2_in0 w2_in1 ffb_in dt_ps dt_evac h_ps hid_done eo_ps eo_done et_ps fin_done fin_out0
            fin_out1 wparts_hi wparts_done klast_hi klast_parts ctx_hi ctx_parts qbd_hi qbd_parts k_lo
            y1T_hi y1T_parts settled""".split()
        s = {n: sem(n) for n in names}
        ctx_in = [sem("ctx_in0"), sem("ctx_in1")]
        block = ctx.enter_context(nc.Block())

        def settle(eng):
            eng.sem_inc(s["settled"], 1)

        def tiles(*, loop, body):
            for i in range(4):
                body(i)
            with loop(2, T // 2 - 1) as pair:
                body(2 * pair)
                body(2 * pair + 1)
            for i in range(T - 2, T + 2):
                body(i)

        def stages(i):
            if not isinstance(i, int):
                return True, True, True, True
            return i <= T - 2, i <= T - 1, 1 <= i <= T, 2 <= i

        def pairs(x):
            return x[:, :].rearrange("p (h d o) -> p h d o", d=HD // 2, o=2)

        def sines(o):
            return k["sin"].rearrange("p (d o) -> p d o", o=2)[:, :, o].unsqueeze(1).to_broadcast([P, 2 * H, HD // 2])

        def once(t, n=0):
            return isinstance(t, int) and t == n

        def norms_ahead(i):
            return not isinstance(i, int) or i <= T - 3

        @block.sync
        def _(sp):
            def load_ctx(t, r):
                sp.wait_ge(s["ctx_parts"], floor0(TB * t + 2 * r - 2))
                b = TB * t + 2 * r
                for c in range(C):
                    sp.dma_start(ctxT[:, r, c], a["ctxT"][c * P:(c + 1) * P, bass.ds(b, 2), :]).then_inc(ctx_in[r], 16)

            def load_x(dst, t, done):
                sp.dma_start(dst[:, :], a["x"][bass.ds(P * t, P), :]).then_inc(s[done], 16)

            def send_diag(src, dst, done):
                for h in range(HH):
                    sp.dma_start(dst(h), src(h)).then_inc(s[done], 16)

            def send_queries(t):
                sp.wait_ge(s["qT_done"], t + 1)
                settle(sp)
                sp.wait_ge(s["qbd_parts"], floor0(TB * t))
                settle(sp)
                send_diag(lambda h: qT[HD * h:HD * (h + 1), :, :].rearrange("p c (j q) -> p c j q", j=TB),
                          lambda h: qbd[HD * h:HD * (h + 1), :, :, h, :], "qbd_in")

            load_x(xq, 0, "xq_in")
            sp.dma_start(const[:, :], a["const"]).then_inc(s["const_in"], 16)
            sp.dma_start(wq[:], a["Wq"].rearrange("(c p) n -> p c n", c=C)).then_inc(s["wq_in"], 16)
            load_ctx(0, 0)
            sp.dma_start(b_q[:, :], a["bq"].rearrange("(c p) -> p c", c=C),
                         allow_slow_non_contiguous=True).then_inc(s["wq_in"], 16)
            load_ctx(0, 1)
            sp.wait_ge(s["zeroed"], 1)
            send_queries(0)

            def load_weights():
                for dst, src in ((qn, "qn"), (kn, "kn")):
                    sp.dma_start(dst[:, :], a[src].rearrange("(c p) -> p c", c=C),
                                 allow_slow_non_contiguous=True).then_inc(s["weights_in"], 16)
                for dst, src in ((aqk[:, :, 0:D], "q_w"), (aqk[:, :, D:2 * D], "k_w"), (av[:], "v_w"), (wo[:], "Wo"),
                                 (ao[:], "o_w"), (gw[:], "gate_w")):
                    sp.dma_start(dst, a[src].rearrange("(c p) n -> p c n", c=C)).then_inc(s["weights_in"], 16)
                for dst, src in ((r_o[:, :], "bo"), (r_v2[:, :], "v_b"), (r_o2[:, :], "o_b"),
                                 (r_qk[:, 0:D], "q_b"), (r_qk[:, D:2 * D], "k_b"), (r_g[:, :], "gate_b")):
                    sp.dma_start(dst, a[src].partition_broadcast(P)).then_inc(s["weights_in"], 16)

            def body(i):
                q, xa, s1, s2 = stages(i)
                if once(i):
                    sp.wait_ge(s["xn_done"], 1)
                    load_x(xq, 1, "xq_in")
                if q:
                    load_ctx(i + 1, 0)
                if once(i):
                    load_weights()
                    load_x(xr, 0, "xr_in")
                if once(i, 1):
                    sp.wait_ge(s["slots_init"], 2)
                    for n in range(E * CAP // P):
                        sp.dma_start(slots[n * P:(n + 1) * P, :], row[:, :]).then_inc(s["slots_zero"], 16)
                if s1 and xa:
                    sp.wait_ge(s["x1_done"], i)
                    load_x(xr, i, "xr_in")
                if q:
                    load_ctx(i + 1, 1)
                if norms_ahead(i):
                    sp.wait_ge(s["xn_done"], i + 2)
                    load_x(xq, i + 2, "xq_in")
                if q:
                    send_queries(i + 1)
                if s1:
                    if once(i, 1):
                        sp.wait_ge(s["zeroed"], 3)
                    sp.wait_ge(s["qkT_done"], i)
                    send_diag(lambda h: qkT[HD * h:HD * (h + 1), 0:C, :],
                              lambda h: qbd2[HD * h:HD * (h + 1), :, h, :], "qbd2_in")
                if s2:
                    sp.wait_ge(s["x2_done"], i - 1)
                    sp.dma_start(out[bass.ds(P * (i - 2), P), :], row[:, D:2 * D]).then_inc(s["x2_out"], 16)

            tiles(loop=sp.Fori, body=body)

            sp.wait_ge(s["sent"], 16 * T)

            def load_rows(e, r, a_, b_, columns, done):
                sp.dma_start(a_[:, r, :], slots[bass.ds(CAP * e, P), columns]).then_inc(s[f"{done}{r}"], 16)
                sp.dma_start(b_[:, r, :], slots[bass.ds(CAP * e + P, CR), columns]).then_inc(s[f"{done}{r}"], 16)

            for r in range(2):
                load_rows(r, r, y_a, y_b, slice(0, D), "y_in")
            for r in range(2):
                load_rows(r, r, x_a, x_b, slice(D, ROW), "x_in")
            with sp.Fori(0, E // 2 - 1) as i:
                for r in range(2):
                    e = 2 * i + r
                    sp.wait_ge(s["dt_ps"], e + 1)
                    load_rows(e + 2, r, y_a, y_b, slice(0, D), "y_in")
                    sp.wait_ge(s["h_ps"], 3 * e + 3)
                    sp.dma_start(w1[:, r], a["w1"][bass.ds(e + 2, 1), :, :].rearrange("a (c p) f -> p (a c) f", c=C)
                                 ).then_inc(s[f"w1_in{r}"], 16)
                    sp.wait_ge(s["eo_ps"], e + 1)
                    settle(sp)
                    sp.dma_start(w2[:, r], a["w2"][bass.ds(e + 2, 1), :, :].rearrange("a (t p) d -> p (a t) d", t=FT)
                                 ).then_inc(s[f"w2_in{r}"], 16)
                    sp.wait_ge(s[f"fin_out{r}"], 32 * i + 32)
                    load_rows(e + 2, r, x_a, x_b, slice(D, ROW), "x_in")
            for r in range(2):
                sp.wait_ge(s[f"fin_out{r}"], 32 * (E // 2))
            sp.wait_ge(s["x2_out"], 16 * T)

        @block.tensor
        def _(pe):
            mm = nc.tensor.matmul

            def last_rows():
                pe.wait_ge(s["wkv_in"], 16 * 5)
                for w, o in ((wk, 0), (wv, C * P)):
                    for c in range(C):
                        for n in range(C):
                            last = mm(shared[:, o + c * P:o + (c + 1) * P], w[:, n, c * P:(c + 1) * P], lastT[:, n, :],
                                      start=n == 0, stop=n == C - 1)
                last.then_inc(s["last_ps"], 1)

            def transpose_queries(t):
                pe.wait_ge(s["xn_done"], t + 1)
                for c in range(C):
                    last = nc.tensor.transpose(sh_c[:, c], xn[:, c * P:(c + 1) * P], k["ident"])
                last.then_inc(s["qt_ps"], 1)

            def project_queries(t):
                pe.wait_ge(s["xnT_done"], t + 1)
                for c in range(C):
                    for n in range(C):
                        last = mm(sh_c[:, c], wq[:, n, c * P:(c + 1) * P], xnT[:, n, :], start=n == 0, stop=n == C - 1)
                last.then_inc(s["q_ps"], 1)

            def keys(t, j):
                b, g = TB * t + j, j % 2
                pe.wait_ge(s["ctx_parts"], b + 1)
                pe.wait_ge(s["k_lo"], b)
                for c in range(C):
                    for n in range(C):
                        for x, y in PASSES:
                            last = mm(kps[:, c, :], wk_p[:, x, n, c * P:(c + 1) * P], ctx_p[:, g, y, n, :],
                                      start=(n, x) == (0, LO), stop=(n, y) == (C - 1, LO))
                last.then_inc(s["k_done"], 1)

            def values(t, j):
                b, g = TB * t + j, j % 2
                pe.wait_ge(s["v_evac"], b)
                for c in range(C):
                    for n in range(C):
                        for x, y in PASSES:
                            last = mm(vps[:, c, :], ctx_p[:, g, x, n, c * P:(c + 1) * P], wv_p[:, y, n, :],
                                      start=(n, x) == (0, LO), stop=(n, y) == (C - 1, LO))
                last.then_inc(s["v_done"], 1)

            def scores(t, j):
                b = TB * t + j
                pe.wait_ge(s["qbd_parts"], b + 1)
                pe.wait_ge(s["klast_cp"], b + 1)
                pe.wait_ge(s["k_lo"], b + 1)
                if j == 0 and (not isinstance(t, int) or t >= 2):
                    pe.wait_ge(s["v2_done"], t - 1)
                if j == 2 and (not isinstance(t, int) or t >= 1):
                    pe.wait_ge(s["y1T_done"], t)
                for m in range(MT):
                    c, g = m // 2, m % 2
                    for x, y in PASSES:
                        last = mm(score[:, m, 0:SE], qbd_p[:, b_slot(j), x, c, g * P:(g + 1) * P],
                                  kT[:, b_slot(j), y, c, :], start=x == LO, stop=y == LO)
                    if g:
                        last.then_inc(s["s_done"], 1)

            def b_slot(j):
                return j % 2

            def transpose_probs(t, j):
                b = TB * t + j
                for c in range(C):
                    pe.wait_ge(s["norm_done"], 2 * b + c + 1)
                    for g in range(2):
                        for n in range(2):
                            at = n * HH * L + g * P
                            last = nc.tensor.transpose(score[:, 2 * c, at:at + P], prob[:, 2 * c + g, n * P:(n + 1) * P],
                                                       k["ident"])
                    last.then_inc(s["pt_done"], 1)

            def weighted_values(t, j):
                b = TB * t + j
                pe.wait_ge(s["v_evac"], b + 1)
                if j == 0:
                    pe.wait_ge(s["ext_step"], floor0(2 * t))
                if j == 0 and (not isinstance(t, int) or t >= 3):
                    pe.wait_ge(s["cum_read"], t - 2)
                for c in range(C):
                    pe.wait_ge(s["ptb_evac" if c else "pta_evac"], b + 1)
                    for g in range(4):
                        for n in range(2):
                            last = mm(gather[32 * g:32 * g + 32, c, :, j * L:(j + 1) * L],
                                      vv[:, b_slot(j), n, c * P + 32 * g:c * P + 32 * g + 32],
                                      probT[:, c, n, 2 * L * g:2 * L * (g + 1)].rearrange("p (h q) -> p h q", h=2),
                                      start=n == 0, stop=n == 1)
                last.then_inc(s["pv_done"], 1)

            def last_probs(t):
                pe.wait_ge(s["plast_done"], TB * (t + 1))
                for c in range(C):
                    for g in range(2):
                        last = mm(sh_c[:, c], k["spread"][:, g * P:(g + 1) * P],
                                  plast[:, 2 * c + g, :, :].rearrange("p j q -> p (j q)"), start=g == 0, stop=g == 1)
                last.then_inc(s["ll_ps"], 1)

            def project_out(x, w, ready, t, done):
                pe.wait_ge(s[ready], t + 1)
                for c in range(C):
                    last = mm(shared[:, 0:D], x[:, c, :], w[:, c, :], start=c == 0, stop=c == C - 1)
                last.then_inc(s[done], 1)

            def transpose_rows(x, ready, t, done, to):
                pe.wait_ge(s[ready], t + 1)
                for c in range(C):
                    last = nc.tensor.transpose(to[:, c], x[:, c * P:(c + 1) * P], k["ident"])
                last.then_inc(s[done], 1)

            def project_qk(t):
                if once(t):
                    pe.wait_ge(s["wparts_done"], 5)
                pe.wait_ge(s["y1T_parts"], t + 1)
                for c in range(C):
                    for x, y in PASSES:
                        last = mm(shared[:, :], y1T_p[:, x, c, :], aqk_p[:, y, c, :],
                                  start=(c, x) == (0, LO), stop=(c, y) == (C - 1, LO))
                last.then_inc(s["qk_ps"], 1)

            def project_v2(t):
                pe.wait_ge(s["y1T_parts"], t + 1)
                for c in range(C):
                    for x, y in PASSES:
                        last = mm(spare, y1T_p[:, x, c, :], av_p[:, y, c, :],
                                  start=(c, x) == (0, LO), stop=(c, y) == (C - 1, LO))
                last.then_inc(s["v2_ps"], 1)

            def transpose_qk(t):
                pe.wait_ge(s["rope_done"], t + 1)
                for c in range(2 * C):
                    last = nc.tensor.transpose(shared[:, c * P:(c + 1) * P], qk[:, c * P:(c + 1) * P], k["ident"])
                last.then_inc(s["qkt_ps"], 1)

            def scores2(t):
                pe.wait_ge(s["qbd2_in"], 16 * HH * (t + 1))
                for c in range(C):
                    for j in range(TB):
                        last = mm(shared[32 * j:32 * j + 32, c * D:(c + 1) * D], qkT[:, C + c, 32 * j:32 * j + 32],
                                  qbd2[:, c, :, 32 * j:32 * j + 32], start=True, stop=True)
                last.then_inc(s["s2_ps"], 1)

            def weight_sums(t):
                pe.wait_ge(s["sig_done"], TB * (t + 1))
                for c in range(C):
                    for g in range(4):
                        last = mm(shared[32 * g:32 * g + 32, c * D:(c + 1) * D], k["ones"][:, 0:32],
                                  wbd[:, 8 * c + 2 * g:8 * c + 2 * g + 2, :].rearrange("p h n -> p (h n)"),
                                  start=True, stop=True)
                last.then_inc(s["sm_ps"], 1)

            def weighted_values2(t):
                pe.wait_ge(s["v2_done"], t + 1)
                for c in range(C):
                    for g in range(4):
                        last = mm(shared[32 * g:32 * g + 32, c * D:(c + 1) * D], v2[:, c * P + 32 * g:c * P + 32 * g + 32],
                                  wbd[:, 8 * c + 2 * g:8 * c + 2 * g + 2, :].rearrange("p h n -> p (h n)"),
                                  start=True, stop=True)
                last.then_inc(s["pv2_ps"], 1)

            def gate(t):
                pe.wait_ge(s["y2T_done"], t + 1)
                for c in range(C):
                    last = mm(shared[:, 0:E], y2T[:, c, :], gw[:, c, :], start=c == 0, stop=c == C - 1)
                last.then_inc(s["g_ps"], 1)

            def positions(t):
                pe.wait_ge(s["oh_done"], t + 1)
                pe.wait_ge(s["seen_done"], t + 1)
                pe.wait_ge(s["ext_step"], min(2 * t + 6, 2 * T) if isinstance(t, int) else 2 * t + 6)
                pe.wait_ge(s["bf_consts"], 2)
                mm(counts, tri_bf[:, :], oh[:, :], start=True, stop=False)
                mm(counts, ones_bf[:, :], seen[:, :], start=False, stop=True).then_inc(s["cum_ps"], 1)

            reader = ["const_in", 16]

            def turn(sem_name, count):
                pe.wait_ge(s[reader[0]], reader[1])
                reader[:] = sem_name, count

            def spare_free(xa, t, j):
                if xa:
                    pe.wait_ge(s["exp_done"], 2 * (TB * t + j) + 1)

            turn("xnT_done", 1)
            transpose_queries(0)
            turn("qT_done", 1)
            pe.wait_ge(s["wq_in"], 32)
            project_queries(0)
            turn("vlast_done", 1)
            last_rows()
            pe.wait_ge(s["wparts_done"], 2)
            keys(0, 0)
            values(0, 0)

            def body(i):
                q, xa, s1, s2 = stages(i)
                t1, t2 = i - 1, i - 2
                if not isinstance(i, int):
                    reader[:] = "logit_done", i - 2
                t3 = (t2 - 1) if not isinstance(i, int) or i >= 3 else None
                between = {
                    (0, 0): s1 and (lambda: (turn("att_tmp", t1 + 1), last_probs(t1))),
                    (0, 1): lambda: (t3 is not None and positions(t3),
                                     s2 and (turn("relu_done", t2 + 1), scores2(t2))),
                    (0, 2): s1 and (lambda: (turn("x1_step", 3 * t1 + 1), project_out(att, wo, "att_done", t1, "o1_ps"))),
                    (0, 3): q and (lambda: (turn("xnT_done", i + 2), transpose_queries(i + 1))),
                    (1, 0): q and (lambda: (turn("qT_done", i + 2), project_queries(i + 1))),
                    (1, 1): s1 and (lambda: (spare_free(xa, i, 1), transpose_rows(y1, "y1_done", t1, "y1t_ps", spare_c))),
                    (1, 2): s2 and (lambda: (turn("sm_step", 2 * (t2 + 1)), weight_sums(t2))),
                    (1, 3): s2 and (lambda: (turn("ext2_step", 2 * (t2 + 1)), weighted_values2(t2))),
                    (2, 0): s1 and (lambda: (turn("qk_done", t1 + 1), project_qk(t1))),
                    (2, 2): s2 and (lambda: (turn("x2_step", 3 * t2 + 1), project_out(att2, ao, "att2_done", t2, "o2_ps"))),
                    (2, 3): s1 and (lambda: (turn("qkT_done", t1 + 1), transpose_qk(t1))),
                    (3, 0): s2 and (lambda: (turn("y2T_done", t2 + 1), transpose_rows(row, "y2_done", t2, "y2t_ps", sh_c))),
                    (3, 1): s2 and (lambda: (turn("logit_done", t2 + 1), gate(t2))),
                    (3, 3): s1 and (lambda: (spare_free(xa, i, 3), project_v2(t1))),
                }

                def short(j, place):
                    if between.get((j, place)):
                        between[j, place]()

                for j in range(TB):
                    ahead = xa and (j < TB - 1 or q)
                    ta, ja = (i, j + 1) if j < TB - 1 else (i + 1, 0)
                    if xa:
                        scores(i, j)
                    short(j, 0)
                    if ahead:
                        keys(ta, ja)
                    short(j, 1)
                    if ahead:
                        values(ta, ja)
                    short(j, 2)
                    if xa:
                        transpose_probs(i, j)
                    short(j, 3)
                    if xa:
                        weighted_values(i, j)

            tiles(loop=pe.Fori, body=body)
            positions(T - 1)

            hps = [score[:, m, 0:3 * CAP].rearrange("p (f n) -> p f n", f=3) for m in range(3)]
            dps = shared[:, 0:C * CAP].rearrange("p (c n) -> p c n", c=C)
            ops_ = score[:, 3, 0:C * CAP].rearrange("p (c n) -> p c n", c=C)
            turn("dt_evac", 0)

            def transpose_dispatched(i, r):
                e = 2 * i + r
                pe.wait_ge(s[f"y_in{r}"], 32 * (i + 1))
                pe.wait_ge(s["dt_evac"], e)
                for c in range(C):
                    nc.tensor.transpose(dps[:, c, 0:P], y_a[:, r, c * P:(c + 1) * P], k["ident"])
                    last = nc.tensor.transpose(dps[:, c, P:CAP], y_b[:, r, c * P:(c + 1) * P],
                                               k["ident"][0:CR, 0:CR])
                last.then_inc(s["dt_ps"], 1)

            def transpose_results(e):
                pe.wait_ge(s["eo_done"], e + 1)
                pe.wait_ge(s["fin_done"], e)
                for c in range(C):
                    nc.tensor.transpose(kps[:, 0, c * P:(c + 1) * P], eo[:, c, 0:P], k["ident"])
                    last = nc.tensor.transpose(vps[0:CR, 0, c * P:(c + 1) * P], eo[:, c, P:CAP], k["ident"])
                last.then_inc(s["et_ps"], 1)

            def expert(i, r, before=True, after=True):
                e = 2 * i + r
                pe.wait_ge(s["dt_evac"], e + 1)
                pe.wait_ge(s[f"w1_in{r}"], 16 * (i + 1))
                for f in range(FT):
                    if f % 3 == 0:
                        pe.wait_ge(s["hid_done"], floor0(FT * (e - 1) + min(f + 3, FT)))
                    for c in range(C):
                        last = mm(hps[f // 3][:, f % 3, :], w1[:, r, c, f * P:(f + 1) * P], disp[:, c, :],
                                  start=c == 0, stop=c == C - 1)
                    if f % 3 == 2 or f == FT - 1:
                        last.then_inc(s["h_ps"], 1)
                    if f == 2 and before:
                        transpose_results(e - 1)
                if after:
                    transpose_dispatched(i + (r + 1) // 2, (r + 1) % 2)
                pe.wait_ge(s[f"w2_in{r}"], 16 * (i + 1))
                pe.wait_ge(s["eo_done"], e)
                for c in range(C):
                    for f in range(FT):
                        if c == 0:
                            pe.wait_ge(s["hid_done"], FT * e + f + 1)
                        last = mm(ops_[:, c, :], w2[:, r, f, c * P:(c + 1) * P], hid[:, f, :],
                                  start=f == 0, stop=f == FT - 1)
                last.then_inc(s["eo_ps"], 1)

            transpose_dispatched(0, 0)
            expert(0, 0, before=False)
            expert(0, 1)
            with pe.Fori(1, E // 2 - 1) as i:
                expert(i, 0)
                expert(i, 1)
            expert(E // 2 - 1, 0)
            expert(E // 2 - 1, 1, after=False)
            transpose_results(E - 1)

        @block.scalar
        def _(act):
            af = nc.scalar.activation

            for dst, src in ((wk[:], a["Wk"]), (wv[:], a["Wv"]), (lastT[:], a["lastT"])):
                act.dma_start(dst, src.rearrange("(c p) n -> p c n", c=C)).then_inc(s["wkv_in"], 16)
            for dst, src in ((b_k, "bk"), (b_v, "bv")):
                act.dma_start(dst[:, :], a[src].rearrange("(c p) -> p c", c=C),
                              allow_slow_non_contiguous=True).then_inc(s["wkv_in"], 16)

            def load_experts():
                for r in range(2):
                    act.dma_start(w1[:, r], a["w1"][r, :, :].rearrange("(c p) f -> p c f", c=C)).then_inc(s[f"w1_in{r}"], 16)
                    act.dma_start(w2[:, r], a["w2"][r, :, :].rearrange("(t p) d -> p t d", t=FT)).then_inc(s[f"w2_in{r}"], 16)
                act.dma_start(b1[:], a["b1"].rearrange("e (t p) -> p e t", t=FT),
                              allow_slow_non_contiguous=True).then_inc(s["ffb_in"], 16)
                act.dma_start(b2[:], a["b2"].rearrange("e (c p) -> p e c", c=C),
                              allow_slow_non_contiguous=True).then_inc(s["ffb_in"], 16)

            def copy_rows(dst, src, ready, t, done):
                act.wait_ge(s[ready], t + 1)
                af(dst, src, ACT.Copy).then_inc(s[done], 1)

            def even_heads(dst, src, ready, count, done):
                act.wait_ge(s[ready], count)
                af(dst[:, :, :], src, ACT.Copy, scale=k["even"]).then_inc(s[done], 1)

            def queries(t):
                act.wait_ge(s["q_ps"], t + 1)
                act.wait_ge(s["qbd_in"], 16 * HH * t)
                for c in range(C):
                    last = af(qT[:, c, :], sh_c[:, c], ACT.Identity, bias=b_q[:, c:c + 1], scale=1.0)
                last.then_inc(s["qT_done"], 1)

            def exps(t, j):
                b = TB * t + j
                act.wait_ge(s["plast_done"], b)
                for c in range(C):
                    act.wait_ge(s["max_done"], 2 * b + c + 1)
                    for g in range(2):
                        m = 2 * c + g
                        last = af(prob[:, m, :], score[:, m, 0:S], ACT.Exp, bias=nmx[:, m:m + 1], scale=1.0,
                                  accum_out=esum[:, m:m + 1])
                    last.then_inc(s["exp_done"], 1)

            def keys(t, j):
                b = TB * t + j
                act.wait_ge(s["k_done"], b + 1)
                act.wait_ge(s["s_done"], floor0(2 * (b - 1)))
                for c in range(C):
                    last = af(kT[:, j % 2, HI, c, 0:SM], kps[:, c, :], ACT.Identity, bias=b_k[:, c:c + 1], scale=1.0)
                last.then_inc(s["k_evac"], 1)

            def context_hi(t, j):
                b, r, g = TB * t + j, j // 2, j % 2
                act.wait_ge(ctx_in[r], 16 * C * (t + 1))
                act.wait_ge(s["v_done"], floor0(b - 1))
                af(ctx_p[:, g, HI, :, :], ctxT[:, r, :, g, 0:SM], ACT.Copy).then_inc(s["ctx_hi"], 1)

            def queries_hi(t, j):
                b = TB * t + j
                if j == 0:
                    act.wait_ge(s["qbd_in"], 16 * HH * (t + 1))
                act.wait_ge(s["s_done"], floor0(2 * (b - 1)))
                af(qbd_p[:, j % 2, HI, :, :], qbd[:, :, j, :, :].rearrange("p c h q -> p c (h q)"), ACT.Copy
                   ).then_inc(s["qbd_hi"], 1)

            def values(t, j):
                b = TB * t + j
                act.wait_ge(s["v_done"], b + 1)
                act.wait_ge(s["pv_done"], floor0(b - 1))
                af(vv[:, j % 2], vps[:, :, :], ACT.Copy).then_inc(s["v_evac"], 1)

            def probsT(t, j):
                b = TB * t + j
                if j == 2:
                    act.wait_ge(s["pt_done"], 2 * b + 1)
                    af(probT[:, 0, :, :].rearrange("p n x -> p (n x)"), score[:, 0, :], ACT.Copy).then_inc(s["pta_evac"], 1)
                act.wait_ge(s["pt_done"], 2 * b + 2)
                af(probT[:, 1, :, :].rearrange("p n x -> p (n x)"), score[:, 2, :], ACT.Copy).then_inc(s["ptb_evac"], 1)

            def squares(t):
                act.wait_ge(s["y1_done"], t + 1)
                act.wait_ge(s["rms_step"], t)
                af(sq[:, :], y1[:, :], ACT.Square, scale=float(1 / np.sqrt(D)), accum_out=msq[:, 0:1]).then_inc(s["sq_done"], 1)

            def sigmoid_tanh(t):
                act.wait_ge(s["s2_ps"], t + 1)
                act.wait_ge(s["sig_done"], TB * t)
                af(th[:, :], shared[:, :], ACT.Tanh, scale=float(SCALE / 2)).then_inc(s["th_done"], 1)
                af(sneg[:, :], shared[:, :], ACT.Relu, scale=-1.0).then_inc(s["relu_done"], 1)

            def sigmoid_abs(t):
                act.wait_ge(s["th_done"], t + 1)
                af(tabs[:, :], th[:, :], ACT.Abs).then_inc(s["tabs_done"], 1)

            def sigmoid_exp(t):
                act.wait_ge(s["relu_done"], t + 1)
                af(sneg[:, :], sneg[:, :], ACT.Exp, scale=float(-SCALE)).then_inc(s["sneg_exp"], 1)

            def sigmoid_blocks(t, batches):
                if once(t):
                    act.wait_ge(s["zeroed"], 4)
                act.wait_ge(s["sig_flat"], t + 1)
                for j in batches:
                    b = slice(32 * j, 32 * j + 32)
                    af(wbd[b, :, b], th[b, :].rearrange("p (h q) -> p h q", h=H), ACT.Copy).then_inc(s["sig_done"], 1)

            def gate_exp(t):
                act.wait_ge(s["logit_done"], t + 1)
                act.wait_ge(s["route_step"], floor0(5 * t))
                af(ex[:, :], logit[:, :], ACT.Exp, bias=nlm[:, 0:1], scale=1.0, accum_out=se[:, 0:1]).then_inc(s["ex_done"], 1)

            def weight_hi(part, full):
                af(part, full, ACT.Copy).then_inc(s["wparts_hi"], 1)

            act.wait_ge(s["wkv_in"], 16 * 5)
            weight_hi(wk_p[:, HI], wk[:, :, :])
            copy_rows(xnT[:, :, :], sh_c, "qt_ps", 0, "xnT_done")
            act.wait_ge(s["wq_in"], 32)
            queries(0)
            weight_hi(wv_p[:, HI], wv[:, :, :])
            context_hi(0, 0)
            act.wait_ge(s["last_ps"], 1)
            for c in range(C):
                last = af(klast[:, c, :], shared[:, c * P:(c + 1) * P], ACT.Identity, bias=b_k[:, c:c + 1], scale=1.0)
            last.then_inc(s["klast_done"], 1)
            act.wait_ge(s["klast_done"], 1)
            af(klast_p[:, HI], klast[:, :, :], ACT.Copy).then_inc(s["klast_hi"], 1)
            context_hi(0, 1)
            keys(0, 0)
            queries_hi(0, 0)
            values(0, 0)

            def body(i):
                q, xa, s1, s2 = stages(i)
                t1, t2 = i - 1, i - 2
                for j in range(TB):
                    ahead = xa and (j < TB - 1 or q)
                    ta, ja = (i, j + 1) if j < TB - 1 else (i + 1, 0)
                    if j == 0 and once(i):
                        load_experts()
                    if j == 0 and s1:
                        act.wait_ge(s["o1_ps"], t1)
                        even_heads(att, gather[:, :, 0, :], "pv_done", TB * (t1 + 1), "ext_step")
                    if j == 2 and s2:
                        act.wait_ge(s["o2_ps"], t2)
                        even_heads(att2, sh_pair[:, :, 0, :], "pv2_ps", t2 + 1, "ext2_step")
                    if j == 3 and once(i):
                        act.wait_ge(s["scaled"], 2 * C)
                        weight_hi(aqk_p[:, HI, 0], aqk[:, 0, :])
                        weight_hi(aqk_p[:, HI, 1], aqk[:, 1, :])
                        weight_hi(av_p[:, HI], av[:, :, :])
                    if j == 3 and s2:
                        copy_rows(y2T[:, :, :], sh_c, "y2t_ps", t2, "y2T_done")
                    if xa:
                        exps(i, j)
                    if j == 1 and q:
                        queries(i + 1)
                    if j == 1 and s2:
                        sigmoid_blocks(t2, (2,))
                    if j == 1 and s1:
                        copy_rows(y1T[:, :, :], spare_c, "y1t_ps", t1, "y1T_done")
                    if ahead:
                        keys(ta, ja)
                    if j == 0 and s2:
                        sigmoid_tanh(t2)
                    if j == 1 and s1:
                        squares(t1)
                    if ahead:
                        queries_hi(ta, ja)
                    if j == 3 and s2:
                        gate_exp(t2)
                    if ahead:
                        values(ta, ja)
                    if xa and j < 3 and (j < 2 or q):
                        context_hi(*((i, j + 2) if j < 2 else (i + 1, j - 2)))
                    if j == 0 and s2:
                        sigmoid_abs(t2)
                    if xa:
                        probsT(i, j)
                    if j == 0 and s2:
                        sigmoid_exp(t2)
                    if xa and j == 3 and q:
                        context_hi(i + 1, 1)
                    if j == 0 and q:
                        copy_rows(xnT[:, :, :], sh_c, "qt_ps", i + 1, "xnT_done")
                    if j == 0 and s2:
                        sigmoid_blocks(t2, (0, 1))
                    if j == 2 and s1:
                        act.wait_ge(s["qbd2_in"], 16 * HH * t1)
                        copy_rows(qkT[:, :, :].rearrange("p c n -> p (c n)"), shared[:, :], "qkt_ps", t1, "qkT_done")

            tiles(loop=act.Fori, body=body)

            hps = [score[:, m, 0:3 * CAP].rearrange("p (f n) -> p f n", f=3) for m in range(3)]
            af(gelu_table[:, :], k["ones"][:, 0:1], ACT.Gelu_apprx_tanh)
            act.wait_ge(s["ffb_in"], 32)

            def hidden(e):
                act.wait_ge(s["eo_ps"], e)
                for f in range(FT):
                    if f % 3 == 0:
                        act.wait_ge(s["h_ps"], 3 * e + f // 3 + 1)
                    af(hid[:, f, :], hps[f // 3][:, f % 3, :], ACT.Gelu_apprx_tanh,
                       bias=b1[:, bass.ds(e, 1), f:f + 1].rearrange("p a b -> p (a b)"), scale=1.0).then_inc(s["hid_done"], 1)

            hidden(0)
            with act.Fori(1, E) as e:
                hidden(e)

        @block.vector
        def _(dve):
            v = nc.vector
            v.memset(qbd[:], 0.0).then_inc(s["zeroed"], 1)
            v.memset(kT[:, :, :, :, SM:SE].bitcast(F32), 0.0).then_inc(s["zeroed"], 1)

            def setup(j):
                if j == 0:
                    v.memset(qbd2[:], 0.0).then_inc(s["zeroed"], 1)
                    v.memset(wbd[:], 0.0).then_inc(s["zeroed"], 1)
                if j == 1:
                    v.memset(seen[:, :], 0.0).then_inc(s["seen_done"], 1)
                    v.memset(row[:, :], 0.0).then_inc(s["slots_init"], 1)
                    v.tensor_copy(tri_bf[:, :], k["tri"]).then_inc(s["bf_consts"], 1)
                    v.tensor_copy(ones_bf[:, :], k["ones"]).then_inc(s["bf_consts"], 1)
                    dve.wait_ge(s["slots_init"], 1)
                    v.tensor_copy(row[:, 2 * D + 1:ROW], k["sentinel"]).then_inc(s["slots_init"], 1)
                if j == 2:
                    dve.wait_ge(s["weights_in"], 16 * 14)
                    for c in range(C):
                        v.tensor_scalar(aqk[:, c, 0:D], aqk[:, c, 0:D], qn[:, c:c + 1], None, ALU.mult
                                        ).then_inc(s["scaled"], 1)
                        v.tensor_scalar(aqk[:, c, D:2 * D], aqk[:, c, D:2 * D], kn[:, c:c + 1], None, ALU.mult
                                        ).then_inc(s["scaled"], 1)
                if j == 3:
                    for c in range(C):
                        weight_lo(aqk_p[:, LO, c], aqk[:, c, :], aqk_p[:, HI, c], 3 + c)
                    weight_lo(av_p[:, LO], av[:, :, :], av_p[:, HI], 5)

            def norm_stats(x, n, step, base):
                v.bn_stats(stat[n][:, :], x).then_inc(s[step], 1)
                dve.wait_ge(s[step], base + 1)
                settle(dve)
                v.bn_aggr(mv[n][:, :], stat[n][:, :]).then_inc(s[step], 1)
                dve.wait_ge(s[step], base + 2)

            def norm_x(t):
                dve.wait_ge(s["xq_in"], 16 * (t + 1))
                norm_stats(xq[:, :], "q", "xn_stat", 3 * t)
                dve.wait_ge(s["xn_pow"], t)
                v.tensor_scalar(ve["q"][:, :], mv["q"][:, 1:2], 1e-5, None, ALU.add).then_inc(s["xn_stat"], 1)

            def norm_x_apply(t):
                dve.wait_ge(s["xn_pow"], t + 1)
                dve.wait_ge(s["qt_ps"], t)
                v.tensor_scalar(xn[:, :], xq[:, :], mv["q"][:, 0:1], rstd["q"][:, 0:1], ALU.subtract, ALU.mult
                                ).then_inc(s["xn_done"], 1)

            def weight_lo(lo, full, hi, count):
                dve.wait_ge(s["wparts_hi"], count)
                v.tensor_tensor(lo, full, hi.bitcast(F32), ALU.subtract).then_inc(s["wparts_done"], 1)

            def keys_lo(t, j):
                b = TB * t + j
                dve.wait_ge(s["k_evac"], b + 1)
                for c in range(C):
                    last = v.scalar_tensor_tensor(kT[:, j % 2, LO, c, 0:SM], kps[:, c, :], b_k[:, c:c + 1],
                                                  kT[:, j % 2, HI, c, 0:SM].bitcast(F32), ALU.add, ALU.subtract)
                last.then_inc(s["k_lo"], 1)

            def maxima(t, j):
                b = TB * t + j
                for c in range(C):
                    dve.wait_ge(s["s_done"], 2 * b + c + 1)
                    v.tensor_reduce(nmx[:, 2 * c:2 * c + 2], score[:, 2 * c:2 * c + 2, 0:S], AX.X, ALU.max, negate=True
                                    ).then_inc(s["max_done"], 1)

            def normalise(t, j):
                b = TB * t + j
                for c in range(C):
                    dve.wait_ge(s["exp_done"], 2 * b + c + 1)
                    v.reciprocal(rsum[:, 2 * c:2 * c + 2], esum[:, 2 * c:2 * c + 2]).then_inc(s["rsum_done"], 1)
                    dve.wait_ge(s["rsum_done"], 2 * b + c + 1)
                    for g in range(2):
                        m = 2 * c + g
                        last = v.tensor_scalar(prob[:, m, :], prob[:, m, :], rsum[:, m:m + 1], None, ALU.mult)
                    last.then_inc(s["norm_done"], 1)

            def probsT(t, j):
                b = TB * t + j
                dve.wait_ge(s["pt_done"], 2 * b + 1)
                v.tensor_copy(probT[:, 0, :, :].rearrange("p n x -> p (n x)"), score[:, 0, :]).then_inc(s["pta_evac"], 1)

            def extract(t):
                dve.wait_ge(s["ext_step"], 2 * t + 1)
                v.scalar_tensor_tensor(att[:, :, :], gather[:, :, 1, :], k["odd"], att[:, :, :], ALU.mult, ALU.add
                                       ).then_inc(s["ext_step"], 1)
            def attended(t):
                dve.wait_ge(s["att_tmp"], t + 1)
                dve.wait_ge(s["ext_step"], 2 * t + 2)
                for c in range(C):
                    last = v.scalar_tensor_tensor(att[:, c, :], alast[:, c, :], b_v[:, c:c + 1], att[:, c, :],
                                                  ALU.add, ALU.add)
                last.then_inc(s["att_done"], 1)

            def last_values(t):
                dve.wait_ge(s["ll_ps"], t + 1)
                v.tensor_tensor(alast[:, :, :].rearrange("p c (j q) -> p (c j) q", j=TB),
                                shared[:, 0:C * P].rearrange("p (x q) -> p x q", q=L),
                                vlast[:, bass.ds(t, 1), :, :].rearrange("p a c j -> p (a c j)").unsqueeze(2)
                                .to_broadcast([P, C * TB, L]), ALU.mult).then_inc(s["att_tmp"], 1)

            def residual1(t):
                dve.wait_ge(s["o1_ps"], t + 1)
                dve.wait_ge(s["xrb_done"], t + 1)
                dve.wait_ge(s["x1b_done"], t)
                v.tensor_tensor(x1[:, :], shared[:, 0:D], xr[:, :], ALU.add).then_inc(s["x1_step"], 1)

            def residual1_stats(t):
                dve.wait_ge(s["x1_step"], 3 * t + 1)
                v.bn_stats(stat["1"][:, :], x1[:, :]).then_inc(s["x1_step"], 1)

            def residual1_mean(t):
                dve.wait_ge(s["x1_step"], 3 * t + 2)
                settle(dve)
                v.bn_aggr(mv["1"][:, :], stat["1"][:, :]).then_inc(s["x1_step"], 1)
                dve.wait_ge(s["x1_step"], 3 * t + 3)
                v.tensor_scalar(ve["1"][:, :], mv["1"][:, 1:2], 1e-5, None, ALU.add).then_inc(s["x1_done"], 1)

            def norm1(t):
                dve.wait_ge(s["x1_pow"], t + 1)
                v.tensor_scalar(y1[:, :], x1[:, :], mv["1"][:, 0:1], rstd["1"][:, 0:1], ALU.subtract, ALU.mult
                                ).then_inc(s["y1_done"], 1)

            def evac_qk(t):
                dve.wait_ge(s["qk_ps"], t + 1)
                dve.wait_ge(s["rrms_done"], t + 1)
                v.scalar_tensor_tensor(qk[:, :], shared[:, :], rrms[:, 0:1], r_qk[:, :], ALU.mult, ALU.add
                                       ).then_inc(s["qk_done"], 1)
                dve.wait_ge(s["qk_done"], t + 1)
                v.tensor_tensor(qkc[:, :].rearrange("p (h d) -> p h d", d=HD), qk[:, :].rearrange("p (h d) -> p h d", d=HD),
                                k["cos"].unsqueeze(1).to_broadcast([P, 2 * H, HD]), ALU.mult).then_inc(s["qkc_done"], 1)
                v.tensor_tensor(pairs(qks)[:, :, :, 1], pairs(qk)[:, :, :, 0], sines(1), ALU.mult).then_inc(s["qks_odd"], 1)

            def rope_add(t):
                dve.wait_ge(s["qkc_done"], t + 1)
                dve.wait_ge(s["qks_done"], t + 1)
                dve.wait_ge(s["qks_odd"], t + 1)
                v.tensor_tensor(qk[:, :], qkc[:, :], qks[:, :], ALU.add).then_inc(s["rope_done"], 1)

            def evac_v2(t):
                dve.wait_ge(s["v2_ps"], t + 1)
                v.tensor_tensor(v2[:, :], spare, r_v2[:, :], ALU.add).then_inc(s["v2_done"], 1)

            def sigmoid_product(t):
                dve.wait_ge(s["sneg_exp"], t + 1)
                dve.wait_ge(s["tabs_done"], t + 1)
                v.scalar_tensor_tensor(th[:, :], tabs[:, :], 1.0, sneg[:, :], ALU.add, ALU.mult).then_inc(s["sig_flat"], 1)

            def sigmoid_block(t, j):
                dve.wait_ge(s["sig_flat"], t + 1)
                b = slice(32 * j, 32 * j + 32)
                v.tensor_copy(wbd[b, :, b], th[b, :].rearrange("p (h q) -> p h q", h=H)).then_inc(s["sig_done"], 1)

            def sums2(t):
                dve.wait_ge(s["sm_ps"], t + 1)
                v.tensor_scalar(ssum[:, :, :], sh_pair[:, :, 0, :], k["even"], 2e-8, ALU.mult, ALU.add).then_inc(s["sm_step"], 1)
                dve.wait_ge(s["sm_step"], 2 * t + 1)
                v.scalar_tensor_tensor(ssum[:, :, :], sh_pair[:, :, 1, :], k["odd"], ssum[:, :, :], ALU.mult, ALU.add
                                       ).then_inc(s["sm_step"], 1)

            def inverse2(t, c):
                dve.wait_ge(s["sm_step"], 2 * t + 2)
                v.reciprocal(ssum[:, c, :], ssum[:, c, :]).then_inc(s["ssum_done"], 1)

            def extract2(t):
                dve.wait_ge(s["ext2_step"], 2 * t + 1)
                v.scalar_tensor_tensor(att2[:, :, :], sh_pair[:, :, 1, :], k["odd"], att2[:, :, :], ALU.mult, ALU.add
                                       ).then_inc(s["ext2_step"], 1)

            def weigh2(t):
                dve.wait_ge(s["ext2_step"], 2 * t + 2)
                dve.wait_ge(s["ssum_done"], C * (t + 1))
                v.tensor_tensor(att2[:, :, :], att2[:, :, :], ssum[:, :, :], ALU.mult).then_inc(s["att2_done"], 1)

            def residual2(t):
                dve.wait_ge(s["o2_ps"], t + 1)
                if once(t):
                    dve.wait_ge(s["slots_zero"], 16 * (E * CAP // P))
                dve.wait_ge(s["sent"], 16 * t)
                dve.wait_ge(s["x2_out"], 16 * t)
                v.tensor_tensor(row[:, D:2 * D], shared[:, 0:D], x1b[:, :], ALU.add).then_inc(s["x2_step"], 1)

            def residual2_stats(t):
                dve.wait_ge(s["x2_step"], 3 * t + 1)
                v.bn_stats(stat["2"][:, :], row[:, D:2 * D]).then_inc(s["x2_step"], 1)

            def residual2_mean(t):
                dve.wait_ge(s["x2_step"], 3 * t + 2)
                settle(dve)
                v.bn_aggr(mv["2"][:, :], stat["2"][:, :]).then_inc(s["x2_step"], 1)
                dve.wait_ge(s["x2_step"], 3 * t + 3)
                v.tensor_scalar(ve["2"][:, :], mv["2"][:, 1:2], 1e-5, None, ALU.add).then_inc(s["x2_done"], 1)

            def norm2(t):
                dve.wait_ge(s["x2_pow"], t + 1)
                v.tensor_scalar(row[:, 0:D], row[:, D:2 * D], mv["2"][:, 0:1], rstd["2"][:, 0:1], ALU.subtract, ALU.mult
                                ).then_inc(s["y2_done"], 1)

            def logits(t):
                dve.wait_ge(s["g_ps"], t + 1)
                v.tensor_tensor(logit[:, :], shared[:, 0:E], r_g[:, :], ALU.add).then_inc(s["route_step"], 1)
                dve.wait_ge(s["route_step"], 5 * t + 1)
                v.tensor_reduce(nlm[:, :], logit[:, :], AX.X, ALU.max, negate=True).then_inc(s["logit_done"], 1)

            def choose(t):
                dve.wait_ge(s["ex_done"], t + 1)
                v.reciprocal(rse[:, :], se[:, :]).then_inc(s["route_step"], 1)
                dve.wait_ge(s["route_step"], 5 * t + 2)
                v.tensor_scalar(pr[:, :], ex[:, :], rse[:, 0:1], None, ALU.mult).then_inc(s["route_step"], 1)
                dve.wait_ge(s["route_step"], 5 * t + 3)
                v.tensor_reduce(row[:, 2 * D:2 * D + 1], pr[:, :], AX.X, ALU.max).then_inc(s["route_step"], 1)
                dve.wait_ge(s["route_step"], 5 * t + 4)
                v.scalar_tensor_tensor(eqr[:, :], pr[:, :], row[:, 2 * D:2 * D + 1], k["rank"], ALU.is_equal, ALU.mult
                                       ).then_inc(s["route_step"], 1)
                dve.wait_ge(s["route_step"], 5 * t + 5)
                dve.wait_ge(s["slot_done"], t)
                v.tensor_reduce(top[:, :], eqr[:, :], AX.X, ALU.max).then_inc(s["top_done"], 1)
                dve.wait_ge(s["top_done"], t + 1)
                v.tensor_scalar(oh[:, :], eqr[:, :], top[:, 0:1], None, ALU.is_equal).then_inc(s["oh_done"], 1)

            def position(t):
                dve.wait_ge(s["cum_ps"], t + 1)
                dve.wait_ge(s["oh_done"], t + 1)
                v.tensor_tensor(cumoh[:, :], counts, oh[:, :], ALU.mult).then_inc(s["cum_read"], 1)
                v.tensor_tensor(seen[:, :], seen[:, :], oh[:, :], ALU.add).then_inc(s["seen_done"], 1)
                dve.wait_ge(s["cum_read"], t + 1)
                v.tensor_reduce(pos[:, :], cumoh[:, :], AX.X, ALU.add).then_inc(s["pos_done"], 1)

            norm_x(0)
            norm_x_apply(0)
            weight_lo(wk_p[:, LO], wk[:, :, :], wk_p[:, HI], 1)
            weight_lo(wv_p[:, LO], wv[:, :, :], wv_p[:, HI], 2)
            dve.wait_ge(s["klast_done"], 1)
            v.tensor_copy(vlast[:, :, :, :].rearrange("p t c j -> p c t j"),
                          shared[:, C * P:2 * C * P].rearrange("p (c t j) -> p c t j", c=C, j=TB)).then_inc(s["vlast_done"], 1)
            dve.wait_ge(s["wkv_in"], 16 * 5)
            keys_lo(0, 0)

            def body(i):
                q, xa, s1, s2 = stages(i)
                t1, t2 = i - 1, i - 2
                for j in range(TB):
                    if j == 0 and s1:
                        extract(t1)
                    if xa:
                        maxima(i, j)
                    if j == 0 and once(i):
                        norm_x(1)
                    if j == 0 and s1:
                        last_values(t1)
                    if j == 1 and s1:
                        norm1(t1)
                    if j == 2 and s2:
                        weigh2(t2)
                    if j == 2 and s1:
                        evac_qk(t1)
                    if xa:
                        normalise(i, j)
                    if j == 0 and (not isinstance(i, int) or i >= 3):
                        position(t2 - 1)
                    if j == 0:
                        if s1:
                            attended(t1)
                        if q:
                            norm_x_apply(i + 1)
                    if j == 3 and s2:
                        logits(t2)
                    if xa and (j < TB - 1 or q) and j not in (1, 2):
                        keys_lo(*((i, j + 1) if j < TB - 1 else (i + 1, 0)))
                    if j == 0 and s1:
                        residual1(t1)
                    if j == 1 and s2:
                        sigmoid_block(t2, 3)
                        sums2(t2)
                    if j == 2 and s1:
                        rope_add(t1)
                    if j == 2 and s2:
                        residual2(t2)
                    if xa and j != 2:
                        probsT(i, j)
                    if xa and j == 1:
                        keys_lo(i, 2)
                    if j == 3 and s1:
                        evac_v2(t1)
                    if j == 3 and s2:
                        choose(t2)
                    if j == 3 and norms_ahead(i):
                        norm_x(i + 2)
                    if j == 0 and s1:
                        residual1_stats(t1)
                        residual1_mean(t1)
                    if j == 0 and s2:
                        sigmoid_product(t2)
                    if j == 1 and s2:
                        inverse2(t2, 0)
                        extract2(t2)
                        inverse2(t2, 1)
                    if j == 2 and s2:
                        residual2_stats(t2)
                    if xa and j == 2:
                        keys_lo(i, 3)
                    if j == 2 and s2:
                        residual2_mean(t2)
                        norm2(t2)
                    if once(i):
                        setup(j)

            tiles(loop=dve.Fori, body=body)
            position(T - 1)

            dps = shared[:, 0:C * CAP]
            ops_ = score[:, 3, 0:C * CAP].rearrange("p (c n) -> p c n", c=C)

            def dispatched(e):
                dve.wait_ge(s["dt_ps"], e + 1)
                dve.wait_ge(s["h_ps"], floor0(3 * e))
                v.tensor_copy(disp[:, :, :].rearrange("p c n -> p (c n)"), dps).then_inc(s["dt_evac"], 1)

            def expert(i, r, after=True):
                e = 2 * i + r
                if after:
                    dispatched(e + 1)
                dve.wait_ge(s["eo_ps"], e + 1)
                dve.wait_ge(s["et_ps"], e)
                for c in range(C):
                    last = v.tensor_scalar(eo[:, c, :], ops_[:, c, :], b2_of(e, c), None, ALU.add)
                last.then_inc(s["eo_done"], 1)
                dve.wait_ge(s["et_ps"], e + 1)
                dve.wait_ge(s[f"x_in{r}"], 32 * (i + 1))
                dve.wait_ge(s[f"fin_out{r}"], 32 * i)
                v.scalar_tensor_tensor(fa[:, r, :], kps[:, 0, :], x_a[:, r, D:D + 1], x_a[:, r, 0:D],
                                       ALU.mult, ALU.add)
                v.scalar_tensor_tensor(fb[:, r, :], vps[0:CR, 0, :], x_b[:, r, D:D + 1], x_b[:, r, 0:D],
                                       ALU.mult, ALU.add).then_inc(s["fin_done"], 1)

            def b2_of(e, c):
                return b2[:, bass.ds(e, 1), c:c + 1].rearrange("p a b -> p (a b)")

            dve.wait_ge(s["ffb_in"], 32)
            dispatched(0)
            for r in range(2):
                expert(0, r)
            with dve.Fori(1, E // 2 - 1) as i:
                for r in range(2):
                    expert(i, r)
            expert(E // 2 - 1, 0)
            expert(E // 2 - 1, 1, after=False)

        @block.gpsimd
        def _(pool):
            g = nc.gpsimd

            def power(n, ready, count, t, done):
                pool.wait_ge(s[ready], count)
                g.tensor_tensor(rstd[n][:, :], ve[n][:, :], k["mhalf"], ALU.pow).then_inc(s[done], 1)

            def last_key(t, j):
                b = TB * t + j
                pool.wait_ge(s["s_done"], floor0(2 * (b - 1)))
                g.tensor_copy(kT[:, j % 2, :, :, SM:S], klast_p[:, :, :, bass.ds(b, 1)]).then_inc(s["klast_cp"], 1)

            def context_lo(t, j):
                b, r, g_ = TB * t + j, j // 2, j % 2
                pool.wait_ge(s["ctx_hi"], b + 1)
                g.tensor_tensor(ctx_p[:, g_, LO, :, :], ctxT[:, r, :, g_, 0:SM], ctx_p[:, g_, HI, :, :].bitcast(F32),
                                ALU.subtract).then_inc(s["ctx_parts"], 1)

            def queries_lo(t, j):
                b = TB * t + j
                pool.wait_ge(s["qbd_hi"], b + 1)
                g.tensor_tensor(qbd_p[:, j % 2, LO, :, :], qbd[:, :, j, :, :].rearrange("p c h q -> p c (h q)"),
                                qbd_p[:, j % 2, HI, :, :].bitcast(F32), ALU.subtract).then_inc(s["qbd_parts"], 1)

            def rows_parts(t):
                pool.wait_ge(s["y1T_done"], t + 1)
                pool.wait_ge(s["v2_ps"], t)
                settle(pool)
                g.tensor_copy(y1T_p[:, HI], y1T[:, :, :]).then_inc(s["y1T_hi"], 1)
                pool.wait_ge(s["y1T_hi"], t + 1)
                g.tensor_tensor(y1T_p[:, LO], y1T[:, :, :], y1T_p[:, HI].bitcast(F32), ALU.subtract
                                ).then_inc(s["y1T_parts"], 1)

            def last_prob(t, j):
                b = TB * t + j
                pool.wait_ge(s["norm_done"], 2 * b + 2)
                if j == 0:
                    pool.wait_ge(s["ll_ps"], t)
                g.tensor_tensor(plast[:, :, j, :], k["diag"].unsqueeze(1).to_broadcast([P, MT, L]),
                                prob[:, :, SM:S].to_broadcast([P, MT, L]), ALU.mult).then_inc(s["plast_done"], 1)

            def residual_bias(t):
                pool.wait_ge(s["xr_in"], 16 * (t + 1))
                g.tensor_tensor(xr[:, :], xr[:, :], r_o[:, :], ALU.add).then_inc(s["xrb_done"], 1)

            def rms(t):
                pool.wait_ge(s["sq_done"], t + 1)
                settle(pool)
                g.tensor_scalar(mse[:, :], msq[:, :], 1e-8, None, ALU.add).then_inc(s["rms_step"], 1)
                pool.wait_ge(s["rms_step"], t + 1)
                g.tensor_tensor(rrms[:, :], mse[:, :], k["mhalf"], ALU.pow).then_inc(s["rrms_done"], 1)

            def rope_sin(t):
                pool.wait_ge(s["qk_done"], t + 1)
                g.tensor_tensor(pairs(qks)[:, :, :, 0], pairs(qk)[:, :, :, 1], sines(0), ALU.mult).then_inc(s["qks_done"], 1)

            def residual_bias2(t):
                pool.wait_ge(s["y1_done"], t + 1)
                pool.wait_ge(s["x2_step"], floor0(3 * (t - 1) + 1))
                g.tensor_tensor(x1b[:, :], x1[:, :], r_o2[:, :], ALU.add).then_inc(s["x1b_done"], 1)

            def slot_numbers(t):
                pool.wait_ge(s["top_done"], t + 1)
                settle(pool)
                g.tensor_scalar(first[:, :], top[:, :], -float(CAP), float(E * CAP - 1), ALU.mult, ALU.add
                                ).then_inc(s["slot_step"], 1)
                g.tensor_scalar(token[:, :], away[:, :], -float(E * CAP), None, ALU.add).then_inc(s["slot_step"], 1)
                pool.wait_ge(s["slot_step"], 7 * t + 2)
                pool.wait_ge(s["pos_done"], t + 1)
                settle(pool)
                g.tensor_copy(row[:, 2 * D + 1:ROW].bitcast(I32), token[:, :]).then_inc(s["slot_step"], 1)
                g.tensor_tensor(slot[:, :], first[:, :], pos[:, :], ALU.add).then_inc(s["slot_step"], 1)
                pool.wait_ge(s["slot_step"], 7 * t + 4)
                g.tensor_tensor(off[:, :], slot[:, :], away[:, :], ALU.subtract).then_inc(s["slot_step"], 1)
                pool.wait_ge(s["slot_step"], 7 * t + 5)
                settle(pool)
                g.tensor_scalar(kept[:, :], pos[:, :], float(CAP), off[:, 0:1], ALU.is_le, ALU.mult).then_inc(s["slot_step"], 1)
                pool.wait_ge(s["slot_step"], 7 * t + 6)
                g.tensor_tensor(slotf[:, :], kept[:, :], away[:, :], ALU.add).then_inc(s["slot_step"], 1)
                pool.wait_ge(s["slot_step"], 7 * t + 7)
                pool.wait_ge(s["sent"], 16 * t)
                settle(pool)
                g.tensor_copy(sloti[:, :], slotf[:, :]).then_inc(s["slot_done"], 1)
                g.tensor_scalar(away[:, :], away[:, :], float(P), None, ALU.add).then_inc(s["away_done"], 1)
                pool.wait_ge(s["slot_done"], t + 1)
                pool.wait_ge(s["away_done"], t + 2)

            def send(t):
                if once(t):
                    pool.wait_ge(s["slots_zero"], 16 * (E * CAP // P))
                pool.wait_ge(s["y2_done"], t + 1)
                settle(pool)
                g.indirect_dma_start(out=slots, out_offset=bass.IndirectOffsetOnAxis(sloti[:, 0:1], 0), in_=row[:, :],
                                     in_offset=None, bounds_check=E * CAP - 1, oob_is_err=False).then_inc(s["sent"], 16)

            pool.wait_ge(s["const_in"], 16)
            g.tensor_copy(away[:, :], k["token"]).then_inc(s["away_done"], 1)
            power("q", "xn_stat", 3, 0, "xn_pow")
            context_lo(0, 0)
            pool.wait_ge(s["klast_hi"], 1)
            g.tensor_tensor(klast_p[:, LO], klast[:, :, :], klast_p[:, HI].bitcast(F32), ALU.subtract
                            ).then_inc(s["klast_parts"], 1)
            context_lo(0, 1)
            pool.wait_ge(s["zeroed"], 2)
            pool.wait_ge(s["klast_parts"], 1)
            last_key(0, 0)
            queries_lo(0, 0)

            def body(i):
                q, xa, s1, s2 = stages(i)
                t1, t2 = i - 1, i - 2
                for j in range(TB):
                    if xa and (j < TB - 1 or q):
                        last_key(*((i, j + 1) if j < TB - 1 else (i + 1, 0)))
                    if j == 0 and once(i):
                        power("q", "xn_stat", 6, 1, "xn_pow")
                    if j == 0 and s1:
                        residual_bias(t1)
                    if j == 2 and s1:
                        rope_sin(t1)
                    if j == 1 and s1:
                        rows_parts(t1)
                    if xa and j < TB - 1:
                        queries_lo(i, j + 1)
                    if xa:
                        last_prob(i, j)
                    if j == 1 and s1:
                        rms(t1)
                    if xa and q and j == TB - 1:
                        queries_lo(i + 1, 0)
                    if xa and (j < 2 or q):
                        context_lo(*((i, j + 2) if j < 2 else (i + 1, j - 2)))
                    if j == 0 and s1:
                        power("1", "x1_done", t1 + 1, t1, "x1_pow")
                    if j == 0 and (not isinstance(i, int) or i >= 3):
                        slot_numbers(t2 - 1)
                        send(t2 - 1)
                    if j == 2 and s2:
                        power("2", "x2_done", t2 + 1, t2, "x2_pow")
                    if j == 3 and norms_ahead(i):
                        power("q", "xn_stat", 3 * (i + 3), i + 2, "xn_pow")
                    if j == 3 and s1:
                        residual_bias2(t1)

            tiles(loop=pool.Fori, body=body)
            slot_numbers(T - 1)
            send(T - 1)

            with pool.Fori(0, E // 2) as i:
                for r in range(2):
                    pool.wait_ge(s["fin_done"], 2 * i + r + 1)
                    settle(pool)
                    for rows, res in ((x_a, fa), (x_b, fb)):
                        g.indirect_dma_start(out=out, out_offset=bass.IndirectOffsetOnAxis(
                                                 rows[:, r, D + 1:D + 2].bitcast(I32), 0),
                                             in_=res[:, r, :], in_offset=None, bounds_check=B * L - 1, oob_is_err=False
                                             ).then_inc(s[f"fin_out{r}"], 16)


def kernel(x, ctx_1024, L0_xattn_Wq, L0_xattn_bq, L0_xattn_Wk, L0_xattn_bk, L0_xattn_Wv, L0_xattn_bv, L0_xattn_Wo,
           L0_xattn_bo, L0_attn_q_w, L0_attn_q_b, L0_attn_k_w, L0_attn_k_b, L0_attn_v_w, L0_attn_v_b, L0_attn_o_w,
           L0_attn_o_b, L0_attn_qn_scale, L0_attn_kn_scale, L0_ffn_gate_w, L0_ffn_gate_b, L0_ffn_w1, L0_ffn_b1,
           L0_ffn_w2, L0_ffn_b2):
    import concourse.bacc as bacc
    from concourse.bass_utils import run_bass_kernel_spmd

    ctxT = np.asarray(ctx_1024).transpose(2, 0, 1)
    arrays = {
        "x": np.asarray(x).reshape(B * L, D), "ctxT": ctxT, "lastT": ctxT[:, :, S - 1], "const": constants(),
        "Wq": np.asarray(L0_xattn_Wq).T, "Wk": np.asarray(L0_xattn_Wk).T, "Wv": np.asarray(L0_xattn_Wv).T,
        "Wo": np.asarray(L0_xattn_Wo).T, "q_w": np.asarray(L0_attn_q_w).T, "k_w": np.asarray(L0_attn_k_w).T,
        "v_w": np.asarray(L0_attn_v_w).T, "o_w": np.asarray(L0_attn_o_w).T,
        "bq": L0_xattn_bq, "bk": L0_xattn_bk, "bv": L0_xattn_bv, "bo": L0_xattn_bo,
        "q_b": L0_attn_q_b, "k_b": L0_attn_k_b, "v_b": L0_attn_v_b, "o_b": L0_attn_o_b,
        "qn": L0_attn_qn_scale, "kn": L0_attn_kn_scale, "gate_w": L0_ffn_gate_w, "gate_b": L0_ffn_gate_b,
        "w1": L0_ffn_w1, "b1": L0_ffn_b1, "w2": L0_ffn_w2, "b2": L0_ffn_b2,
    }
    arrays = {n: np.ascontiguousarray(v) for n, v in arrays.items()}
    nc = bacc.Bacc("TRN2", target_bir_lowering=False, num_devices=1)
    aps = {n: nc.dram_tensor("in_" + n, v.shape, mybir.dt.from_np(v.dtype), kind="ExternalInput").ap()
           for n, v in arrays.items()}
    out = nc.dram_tensor("out", (B * L, D), F32, kind="ExternalOutput").ap()
    build(nc, aps, out)
    r = run_bass_kernel_spmd(nc, [{"in_" + n: v for n, v in arrays.items()}], core_ids=[0])
    return r.results[0]["out"].reshape(B, L, D)
```
